# Optimizing a Trainium2 kernel written in Bass

```python
import numpy as np
import jax
import jax.numpy as jnp

def _softmax(x, axis=-1):
    return jax.nn.softmax(x, axis=axis)

def _gelu(x):
    return jax.nn.gelu(x, approximate=True)

def _silu(x):
    return jax.nn.silu(x)

def _sigmoid(x):
    return jax.nn.sigmoid(x)

def _layernorm(x, axis=-1, eps=1e-05):
    m = jnp.mean(x, axis=axis, keepdims=True)
    v = jnp.var(x, axis=axis, keepdims=True)
    return (x - m) / jnp.sqrt(v + eps)

def _scatter_add(tgt, idx, src, axis=0):
    return tgt.at[idx].add(src)

def _segment_sum(src, seg, n):
    return jax.ops.segment_sum(src, seg, n)
kernel_name = 'mk_flamingo_gated_d1_seqx_r4_2a0895'

def setup_inputs(seed: int=0):
    np.random.seed(seed)
    _w = jnp.asarray

    def _rec_inputs():
        import jax
        import jax.numpy as jnp
        _rk = jax.random.key(seed)
        x = -0.0002928 + 1 * jax.random.normal(jax.random.fold_in(_rk, 1), (4, 512, 256), jnp.float32)
        _lenS = 512 - jax.random.randint(jax.random.fold_in(_rk, 7), (4,), 0, max(1, 512 // 4) + 1, jnp.int32)
        _lenS2 = 64 - jax.random.randint(jax.random.fold_in(_rk, 8), (4,), 0, max(1, 64 // 4) + 1, jnp.int32)
        _ctx_1024P = jax.random.normal(jax.random.fold_in(_rk, 11), (4, 16, 256), jnp.float32)
        _ctx_1024c = jax.random.dirichlet(jax.random.fold_in(_rk, 511), 0.3 * jnp.ones((16,), jnp.float32), (4, 64))
        _ctx_1024t = jnp.einsum('bsk,bkd->bsd', _ctx_1024c, _ctx_1024P)
        _ctx_1024t = _ctx_1024t * jax.lax.rsqrt(jnp.mean(jnp.square(_ctx_1024t)) + 1e-12) * 0.953939
        ctx_1024 = -1.39393e-06 + 0.999914 * (_ctx_1024t + 0.3 * jax.random.normal(jax.random.fold_in(_rk, 611), (4, 64, 256), jnp.float32))
        _g = jax.random.normal(jax.random.fold_in(_rk, 9001), (2, 1), jnp.float32)
        _g = jnp.sign(_g) * jnp.maximum(jnp.abs(_g), 1.0) + (_g == 0) * 1.0
        g_xattn = _g[0]
        g_ffn = _g[1]
        return (x, ctx_1024, g_xattn, g_ffn)
    x, ctx_1024, g_xattn, g_ffn = _rec_inputs()

    def _L0_xattn_setup():
        import jax, jax.numpy as jnp
        import numpy as np
        HEADS = 16
        DIM_HEAD = 64
        SCALE = DIM_HEAD ** (-0.5)
        key = jax.random.key(seed)
        ks = jax.random.split(key, 7)
        b, n, m, d = (2, 512, 512, 256)
        inner = HEADS * DIM_HEAD
        patch_embed = jax.random.normal(ks[0], (b, n, d), dtype=jnp.float32)
        pixel_embed = jax.random.normal(ks[1], (b, m, d), dtype=jnp.float32)
        s = 1.0 / np.sqrt(d)
        Wq = jax.random.normal(ks[2], (d, inner), dtype=jnp.float32) * s
        Wk = jax.random.normal(ks[3], (d, inner), dtype=jnp.float32) * s
        Wv = jax.random.normal(ks[4], (d, inner), dtype=jnp.float32) * s
        Wo = jax.random.normal(ks[5], (inner, d), dtype=jnp.float32) * (1.0 / np.sqrt(inner))
        bo = jax.random.normal(ks[6], (d,), dtype=jnp.float32) * 0.01
        return {'patch_embed': patch_embed, 'pixel_embed': pixel_embed, 'Wq': Wq, 'Wk': Wk, 'Wv': Wv, 'Wo': Wo, 'bo': bo}
    _L0_xattn_all = _L0_xattn_setup()
    _L0_xattn_in = {k: v for k, v in _L0_xattn_all.items() if k in ('Wq', 'Wk', 'Wv', 'Wo', 'bo')}
    del _L0_xattn_all

    def _L0_ffn_setup():
        import jax, jax.numpy as jnp
        import numpy as np
        B, S, D, E, H, DO = (4, 512, 256, 8, 1024, 256)
        TOP_K = 2
        LN_EPS = 1e-05
        key = jax.random.key(seed)
        ks = jax.random.split(key, 9)
        s = 0.02
        return {'x': jax.random.normal(ks[0], (B, S, D), dtype=jnp.float32), 'W1': jax.random.normal(ks[1], (E, D, H), dtype=jnp.float32) * s, 'b1': jnp.zeros((E, H), dtype=jnp.float32), 'W2': jax.random.normal(ks[2], (E, H, DO), dtype=jnp.float32) * s, 'b2': jnp.zeros((E, DO), dtype=jnp.float32), 'gate_W': jax.random.normal(ks[3], (D, E), dtype=jnp.float32) * s, 'shared_W': jax.random.normal(ks[4], (D, DO), dtype=jnp.float32) * s, 'shared_b': jnp.zeros((DO,), dtype=jnp.float32), 'gamma': jnp.ones((DO,), dtype=jnp.float32), 'beta': jnp.zeros((DO,), dtype=jnp.float32)}
    _L0_ffn_all = _L0_ffn_setup()
    _L0_ffn_in = {k: v for k, v in _L0_ffn_all.items() if k in ('W1', 'b1', 'W2', 'b2', 'gate_W', 'shared_W', 'shared_b', 'gamma', 'beta')}
    del _L0_ffn_all
    return {'x': x, 'ctx_1024': ctx_1024, 'g_xattn': g_xattn, 'g_ffn': g_ffn, 'L0_xattn_Wq': _L0_xattn_in['Wq'], 'L0_xattn_Wk': _L0_xattn_in['Wk'], 'L0_xattn_Wv': _L0_xattn_in['Wv'], 'L0_xattn_Wo': _L0_xattn_in['Wo'], 'L0_xattn_bo': _L0_xattn_in['bo'], 'L0_ffn_W1': _L0_ffn_in['W1'], 'L0_ffn_b1': _L0_ffn_in['b1'], 'L0_ffn_W2': _L0_ffn_in['W2'], 'L0_ffn_b2': _L0_ffn_in['b2'], 'L0_ffn_gate_W': _L0_ffn_in['gate_W'], 'L0_ffn_shared_W': _L0_ffn_in['shared_W'], 'L0_ffn_shared_b': _L0_ffn_in['shared_b'], 'L0_ffn_gamma': _L0_ffn_in['gamma'], 'L0_ffn_beta': _L0_ffn_in['beta']}

def reference(x, ctx_1024, g_xattn, g_ffn, L0_xattn_Wq, L0_xattn_Wk, L0_xattn_Wv, L0_xattn_Wo, L0_xattn_bo, L0_ffn_W1, L0_ffn_b1, L0_ffn_W2, L0_ffn_b2, L0_ffn_gate_W, L0_ffn_shared_W, L0_ffn_shared_b, L0_ffn_gamma, L0_ffn_beta):
    import jax
    import jax.numpy as jnp

    def _L0_xattn_ref(patch_embed, pixel_embed, Wq, Wk, Wv, Wo, bo):
        import jax, jax.numpy as jnp
        import numpy as np
        HEADS = 16
        DIM_HEAD = 64
        SCALE = DIM_HEAD ** (-0.5)
        b, n, _ = patch_embed.shape
        h, dh = (HEADS, DIM_HEAD)
        q = patch_embed @ Wq
        k = pixel_embed @ Wk
        v = pixel_embed @ Wv
        q = q.reshape(b, n, h, dh)
        k = k.reshape(b, -1, h, dh)
        v = v.reshape(b, -1, h, dh)
        sim = jnp.einsum('bihd,bjhd->bhij', q, k) * SCALE
        attn = jax.nn.softmax(sim, axis=-1)
        out = jnp.einsum('bhij,bjhd->bihd', attn, v)
        out = out.reshape(b, n, h * dh)
        return out @ Wo + bo

    def _L0_ffn_ref(x, W1, b1, W2, b2, gate_W, shared_W, shared_b, gamma, beta):
        import jax, jax.numpy as jnp
        import numpy as np
        B, S, D, E, H, DO = (4, 512, 256, 8, 1024, 256)
        TOP_K = 2
        LN_EPS = 1e-05
        d = x.shape[-1]
        flat = x.reshape(-1, d)
        n_exp = gate_W.shape[-1]
        probs = jax.nn.softmax(flat @ gate_W, axis=-1)
        topk_w, topk_idx = jax.lax.top_k(probs, TOP_K)
        topk_w = topk_w / topk_w.sum(axis=-1, keepdims=True)
        combine = (jax.nn.one_hot(topk_idx, n_exp, dtype=flat.dtype) * topk_w[..., None]).sum(axis=1)
        out = 0.5 * jax.nn.gelu(flat @ shared_W + shared_b, approximate=False)
        for e in range(n_exp):
            h = jax.nn.gelu(flat @ W1[e] + b1[e], approximate=False)
            out = out + combine[:, e:e + 1] * (h @ W2[e] + b2[e])
        mean = out.mean(axis=-1, keepdims=True)
        var = ((out - mean) ** 2).mean(axis=-1, keepdims=True)
        out = (out - mean) * jax.lax.rsqrt(var + LN_EPS) * gamma + beta
        return out.reshape(*x.shape[:-1], out.shape[-1])
    x = x + jnp.tanh(g_xattn[0]) * _L0_xattn_ref(_layernorm(x, axis=-1), ctx_1024, L0_xattn_Wq, L0_xattn_Wk, L0_xattn_Wv, L0_xattn_Wo, L0_xattn_bo)
    x = x + jnp.tanh(g_ffn[0]) * _L0_ffn_ref(_layernorm(x, axis=-1), L0_ffn_W1, L0_ffn_b1, L0_ffn_W2, L0_ffn_b2, L0_ffn_gate_W, L0_ffn_shared_W, L0_ffn_shared_b, L0_ffn_gamma, L0_ffn_beta)
    return x

_drawn_inputs = setup_inputs


def setup_inputs(seed=0):
    import zlib

    import numpy as np

    out = dict(_drawn_inputs(seed))
    spreads = {'L0_ffn_b1': (0.0, 0.1),
     'L0_ffn_b2': (0.0, 0.1),
     'L0_ffn_shared_b': (0.0, 0.1),
     'L0_ffn_gamma': (1.0, 0.2),
     'L0_ffn_beta': (0.0, 0.1)}
    factors = {}
    for name, (base, spread) in spreads.items():
        noise = np.random.default_rng([zlib.crc32(name.encode()), seed]).standard_normal(out[name].shape)
        drawn = base * np.exp(spread * noise) if base else spread * noise
        out[name] = jnp.asarray(drawn.astype(out[name].dtype))
    for name, factor in factors.items():
        out[name] = (out[name] * factor).astype(out[name].dtype)
    return out
```

```python
from contextlib import ExitStack

import numpy as np
import concourse.bass as bass
from concourse import mybir

P = 128
B, S, D = 4, 512, 256
NCTX = 64
HEADS, DH = 16, 64
INNER = HEADS * DH
EXPERTS, HID = 8, 1024
CHOICES = 2
TOKENS = B * S
TILES = TOKENS // P
TPB = S // P
DC = D // P
HC = HID // P
JC = INNER // P
MTILES = (CHOICES * TOKENS + EXPERTS * (P - 1)) // P
PAIRS = CHOICES * TILES
BANK = 512
LN_EPS = 1e-5
SCALE = DH ** -0.5

f32 = mybir.dt.float32
bf16 = mybir.dt.bfloat16
i32 = mybir.dt.int32
ALU = mybir.AluOpType
ACT = mybir.ActivationFunctionType
AX = mybir.AxisListType.X


def build(nc, x, ctx_in, g_xattn, g_ffn, Wq, Wk, Wv, Wo, bo, W1, b1, W2, b2, gate_W, shared_W, shared_b,
          gamma, beta, out, xn2_dram, acc_dram):
    stack = ExitStack()
    with stack:
        def sb(name, shape, dt=f32):
            return stack.enter_context(nc.sbuf_tensor(name, shape, dt))

        def sem(name):
            return stack.enter_context(nc.semaphore(name))

        WE = sb("WE", [P, EXPERTS, 2 * DC * HID])
        half = DC * HID
        W1_sb = WE[:, :, 0:half].rearrange("p e (c n) -> p e c n", c=DC)
        W2_sb = WE[:, :, half:2 * half].rearrange("p e (j n) -> p e j n", j=HC)
        Wk_sb = WE[:, 2, 0:half].rearrange("p (c n) -> p c n", c=DC)
        Wv_sb = WE[:, 2, half:].rearrange("p (c n) -> p c n", c=DC)
        Wq_sb = WE[:, 3, 0:half].rearrange("p (c n) -> p c n", c=DC)
        Wo_sb = WE[:, 3, half:].rearrange("p (j n) -> p j n", j=JC)
        WqT = WE[:, 4, 0:half].rearrange("p (j n) -> p j n", j=JC)
        KT = WE[:, 4, half:].rearrange("p (j n) -> p j n", j=JC)
        VBD = WE[:, 5, :].rearrange("p (j b h k) -> p j b h k", j=JC, b=B, h=2)
        XN2T = WE[:, 5, :].rearrange("p (t n) -> p t n", t=TILES)
        A = WE[:, 6:8, :].rearrange("p e n -> p (e n)").rearrange("p (c b n) -> p c b n", c=DC, b=B)

        VOR = sb("VOR", [P, B * JC * D])
        VO = VOR[:, :].rearrange("p (b j n) -> p b j n", b=B, j=JC)
        b2_bc = VOR[:, 0:EXPERTS * D].rearrange("p (e n) -> p e n", e=EXPERTS)
        res = VOR[:, 7168:8192].rearrange("p (s n) -> p s n", s=2)
        xs = VOR[:, 2048:2816].rearrange("p (s n) -> p s n", s=3)
        xsT = VOR[:, 2816:3072].rearrange("p (c n) -> p c n", c=DC)
        hid = VOR[:, 3072:4096]
        hidT = VOR[:, 4096:5120].rearrange("p (j n) -> p j n", j=HC)
        ys = VOR[:, 5120:5888].rearrange("p (s n) -> p s n", s=3)
        RT = [VOR[:, 2048 + 128 * n:2176 + 128 * n].rearrange("p (t e) -> p t e", e=EXPERTS) for n in range(8)]
        eq_hi = VOR[:, 0:PAIRS * MTILES].rearrange("p (n m) -> p n m", m=MTILES)
        cmp = VOR[0:1, 1280:1280 + MTILES * EXPERTS].rearrange("p (m e) -> p m e", e=EXPERTS)
        sm = VOR[:, 2688:2848].rearrange("p (a t) -> p a t", t=TILES)
        posi = VOR[:, 2848:2944].rearrange("p (a n) -> p a n", a=3).bitcast(i32)
        lohi = VOR[:, 2944:3008].rearrange("p (a n) -> p a n", a=2)
        cum = VOR[:, 3008:3072].rearrange("p (a n) -> p a n", a=4)
        iota_lo = VOR[:, 4096:4096 + P]
        cnti = VOR[:, 4224:4240].rearrange("p (a e) -> p a e", a=2).bitcast(i32)
        base8 = VOR[:, 4240:4248]
        tab = VOR[:, 6848:6965].rearrange("p (a m) -> p a m", a=3)
        gidx = VOR[:, 6965:7004].bitcast(i32)
        sidx = VOR[:, 7004:7043].bitcast(i32)
        assert 3 * MTILES == 117 and 4352 + PAIRS * 2 * MTILES <= 6848
        sW = VOR[:, 3072:3584].rearrange("p (c n) -> p c n", c=DC)
        sb_row = VOR[0:1, 3584:4096].rearrange("p (a n) -> p a n", a=2)
        b1_rows = VOR[0:EXPERTS * HC, 0:P]
        RH = VOR[:, 4352:4352 + PAIRS * 2 * MTILES].rearrange("p (n a m) -> p n a m", a=2, m=MTILES)
        assert PAIRS * MTILES <= 1280

        X = sb("X", [P, TILES, D])
        AT = sb("AT", [P, 4 * HID])
        E = AT[:, 0:2 * HID].rearrange("p (s n) -> p s n", s=2)
        PT = AT[:, 2 * HID:].rearrange("p (s j n) -> p s j n", s=2, j=JC)
        OH_lo = AT[:, :].rearrange("p (n m) -> p n m", m=P)
        F = AT[:, :].rearrange("p (t n) -> p t n", t=TILES)

        ctx_sb = sb("ctx_sb", [P, DC, D])
        cT = sb("cT", [P, DC, B * NCTX])
        xn_b = [sb(f"xn{s}", [P, D]) for s in range(2)]
        xnT_b = [sb(f"xnT{s}", [P, DC, P]) for s in range(2)]
        xn2_b = [ctx_sb[:, s, :] for s in range(2)]
        xn2T_b = [cT[:, s, :].rearrange("p (c n) -> p c n", c=DC) for s in range(2)]
        ident = sb("ident", [P, P])
        upper = sb("upper", [P, P], bf16)
        ones_b = sb("ones_b", [P, P], bf16)
        ones_row = sb("ones_row", [1, P])
        gW = sb("gW", [P, DC, EXPERTS])
        bo_bc = sb("bo_bc", [P, D])
        tgam = sb("tgam", [P, D])
        tbet = sb("tbet", [P, D])
        tg = sb("tg", [P, 2])
        b1T = sb("b1T", [P, EXPERTS * HC])
        st = sb("st", [P, TILES, 6])
        mv = sb("mv", [P, TILES, 2])
        rstd = sb("rstd", [P, TILES])
        nmr = sb("nmr", [P, TILES])
        st2 = sb("st2", [P, 2, 6])
        mv2 = sb("mv2", [P, 2, 2])
        ve2 = sb("ve2", [P, 2])
        rs2 = sb("rs2", [P, 2, 2])
        mhalf = sb("mhalf", [P, TILES])
        mx = sb("mx", [P, 2, HEADS])
        rsum = sb("rsum", [P, 2, HEADS])
        rinv = sb("rinv", [P, 2, HEADS])
        M_bf = sb("M_bf", [P, TILES, EXPERTS], bf16)
        wtok = sb("wtok", [P, CHOICES, TILES])
        pos = sb("pos", [P, CHOICES, TILES])
        tokid = sb("tokid", [P, TILES])
        iota_m = sb("iota_m", [P, MTILES])
        rank8 = sb("rank8", [P, EXPERTS])
        pad_row = sb("pad_row", [P, 1])
        etf = sb("etf", [1, MTILES])
        etile = sb("etile", [1, MTILES], i32)
        gslot = sb("gslot", [P, 3], i32)
        sslot = sb("sslot", [P, 3], i32)
        gcol = [gslot[:, s:s + 1] for s in range(3)]
        scol = [sslot[:, s:s + 1] for s in range(3)]

        PS = stack.enter_context(nc.psum_tensor("PS", [P, 8, BANK], f32))
        S_ps = [PS[:, 0, :], PS[:, 1, :]]
        PT_ps = [PS[:, 2, :], PS[:, 3, :]]
        O_ps = PS[:, 4, 0:D]
        xT_ps, x2T_ps = PS[:, 5, 0:D], PS[:, 6, D:2 * D]
        G_ps = PS[:, 6, 0:TILES * EXPERTS]
        rank_ps = PS[:, 7, 0:TILES * EXPERTS]
        cnt_ps = PS[:, 6, 256:256 + EXPERTS]
        tab_ps = PS[:, 7, 256:256 + 2 * MTILES]

        ld_ctx, ld_wk, ld_wq, ld_wv, ld_wo, ld_x, ld_small, ld_b2, ld_exp, ld_shared = [
            sem(n) for n in "ld_ctx ld_wk ld_wq ld_wv ld_wo ld_x ld_small ld_b2 ld_exp ld_shared".split()]
        c_pool, c_ident, c_vbd, c_half = sem("c_pool"), sem("c_ident"), sem("c_vbd"), sem("c_half")
        pre_mm, pre_dve, pre_act = sem("pre_mm"), sem("pre_dve"), sem("pre_act")
        b1_mm, b1_ready = sem("b1_mm"), sem("b1_ready")
        tanh_ready, bo_ready, gb_ready = sem("tanh_ready"), sem("bo_ready"), sem("gb_ready")
        ln1_mv, ln1_ready = sem("ln1_mv"), sem("ln1_ready")
        s_mm, xT_mm, x2T_mm, pT_mm, o_mm, g_mm = [sem(n) for n in "s_mm xT_mm x2T_mm pT_mm o_mm g_mm".split()]
        xn_ready, xT_ready, exp_ready, pT_ready, xn2_ready, x2T_ready = [
            sem(n) for n in "xn_ready xT_ready exp_ready pT_ready xn2_ready x2T_ready".split()]
        mx_ready, shifted, sum_ready, rinv_ready, x2_ready, st2_ready, mv2_ready = [
            sem(n) for n in "mx_ready shifted sum_ready rinv_ready x2_ready st2_ready mv2_ready".split()]
        p_ready, bo_added, ve2_ready, pow2_ready, rstd2_ready = [
            sem(n) for n in "p_ready bo_added ve2_ready pow2_ready rstd2_ready".split()]
        st_xn2 = [sem(f"st_xn2_{s}") for s in range(2)]
        st_x2T = [sem(f"st_x2T_{s}") for s in range(2)]
        dchain, pchain = sem("dchain"), sem("pchain")
        z_mm, z_gelu, z_ready, x_beta = sem("z_mm"), sem("z_gelu"), sem("z_ready"), sem("x_beta")
        st_acc = [sem(f"st_acc{s}") for s in range(2)]
        pad_acc = sem("pad_acc")
        lg_ready, pexp_ready, M_ready, cnt_mm, rank_mm, oh_ready, tab_mm, route_ready = [
            sem(n) for n in "lg_ready pexp_ready M_ready cnt_mm rank_mm oh_ready tab_mm route_ready".split()]
        ga = [sem(f"ga{s}") for s in range(3)]
        sc = [sem(f"sc{s}") for s in range(3)]
        xsT_mm, h_mm, hT_mm, y_mm = [sem(n) for n in "xsT_mm h_mm hT_mm y_mm".split()]
        xsT_ready, gel_ready = sem("xsT_ready"), sem("gel_ready")
        h_ready, yb_ready, y_ready, gi_ready = [sem(n) for n in "h_ready yb_ready y_ready gi_ready".split()]
        ld_f = [sem(f"ld_f{k}") for k in range(B)]
        f_st, f_mv, f_norm, f_gam, f_rstd, f_ve, f_pow, f_out, st_out = [
            sem(n) for n in "f_st f_mv f_norm f_gam f_rstd f_ve f_pow f_out st_out".split()]

        dve_waits, pool_waits = sem("dve_waits"), sem("pool_waits")

        block = stack.enter_context(nc.Block())

        def wait(eng, s, value):
            if not isinstance(value, int) or value > 0:
                eng.wait_ge(s, value)

        def alone(eng, g, own):
            if not isinstance(g, int):
                eng.sem_inc(own, 1)

        def at(ap, i):
            if isinstance(i, int):
                return ap[:, i]
            one = ap[:, bass.ds(i, 1)]
            return one.rearrange("p o n -> p (o n)") if len(one.shape) == 3 else one

        def batch_of(g, u):
            pair = g + u // 2
            b = pair // (TPB // 2)
            return b if isinstance(b, int) else b.with_bounds(min_val=0, max_val=B - 1)

        def col(ap, i):
            return ap[:, i:i + 1] if isinstance(i, int) else ap[:, bass.ds(i, 1)]

        x_t = x.rearrange("b (t p) d -> p (b t) d", p=P)
        out_t = out.rearrange("b (t p) d -> p (b t) d", p=P)
        xn2_rows = xn2_dram.rearrange("(t p) d -> p t d", p=P)
        acc_rows = acc_dram[0:TOKENS, :].rearrange("(t p) d -> p t d", p=P)

        def W1_of(e):
            return W1[e].rearrange("(c p) n -> p c n", p=P)

        def W2_of(e):
            return W2[e].rearrange("(j p) n -> p j n", p=P)

        KT0, QT0, A0 = 1, 1 + JC // 2, 1 + JC
        VT0 = A0 + HEADS
        VO0 = VT0 + JC // 2
        GROUPS = VO0 + B * JC // 2

        def evacuated(eng, n):
            wait(eng, pre_dve, n // 2 + 1)
            wait(eng, pre_act, (n + 1) // 2)

        A_PEEL_END = 14

        def attention_steps(eng, step):
            for i in range(4):
                step(i // 2, i % 2)
            with eng.Fori(2, A_PEEL_END // 2) as g:
                step(g, 0)
                step(g, 1)
            for i in range(A_PEEL_END, TILES + 2):
                step(i // 2, i % 2)

        M_PEEL_END = 36

        def mixture_steps(eng, step):
            for i in range(6):
                step(i // 3, i % 3)
            with eng.Fori(2, M_PEEL_END // 3) as g:
                for u in range(3):
                    step(g, u)
            for i in range(M_PEEL_END, MTILES + 1):
                step(i // 3, i % 3)

        @block.sync
        def _(sp):
            sp.dma_start(ctx_sb[:, :, :], ctx_in.rearrange("b k d -> (b k) d").rearrange("(t p) d -> p t d", p=P)
                         ).then_inc(ld_ctx, 16)
            sp.dma_start(Wk_sb, Wk.rearrange("(c p) n -> p c n", p=P)).then_inc(ld_wk, 16)
            sp.dma_start(Wq_sb, Wq.rearrange("(c p) n -> p c n", p=P)).then_inc(ld_wq, 16)
            for b in range(B):
                sp.dma_start(X[:, TPB * b:TPB * (b + 1), :], x_t[:, TPB * b:TPB * (b + 1), :]).then_inc(ld_x, 16)
            sp.dma_start(Wv_sb, Wv.rearrange("(c p) n -> p c n", p=P)).then_inc(ld_wv, 16)
            sp.dma_start(Wo_sb, Wo.rearrange("(j p) n -> p j n", p=P)).then_inc(ld_wo, 16)
            for e in (0, 1):
                sp.dma_start(W1_sb[:, e], W1_of(e)).then_inc(ld_exp, 16)
                sp.dma_start(W2_sb[:, e], W2_of(e)).then_inc(ld_exp, 16)
            sp.wait_ge(pre_mm, GROUPS)
            for e in (2, 3, 4):
                sp.dma_start(W1_sb[:, e], W1_of(e)).then_inc(ld_exp, 16)
                sp.dma_start(W2_sb[:, e], W2_of(e)).then_inc(ld_exp, 16)

            def store(i, s):
                wait(sp, xn2_ready, i + 1)
                sp.dma_start(at(xn2_rows, i), xn2_b[s]).then_inc(st_xn2[s], 16)
                wait(sp, x2T_ready, i + 1)
                sp.dma_start(at(XN2T, i), xn2T_b[s][:, :, :].rearrange("p c n -> p (c n)")
                             ).then_inc(st_x2T[s], 16)

            with sp.Fori(0, TILES // 2 - 1) as g:
                store(2 * g, 0)
                store(2 * g + 1, 1)
            sp.wait_ge(s_mm, 2 * TILES)
            for e in (6, 7):
                sp.dma_start(W1_sb[:, e], W1_of(e)).then_inc(ld_exp, 16)
                sp.dma_start(W2_sb[:, e], W2_of(e)).then_inc(ld_exp, 16)
            store(TILES - 2, 0)
            store(TILES - 1, 1)
            sp.wait_ge(o_mm, TILES)
            sp.dma_start(sW, shared_W.rearrange("(c p) n -> p c n", p=P)).then_inc(ld_shared, 16)
            for r in range(2):
                sp.dma_start(sb_row[:, r, :], shared_b.rearrange("(a n) -> a n", a=1)).then_inc(ld_shared, 16)
            for q in range(TILES // 2):
                sp.wait_ge(z_ready, q + 1)
                sp.dma_start(acc_rows[:, 2 * q:2 * q + 2, :], res[:, q % 2].rearrange("p (t n) -> p t n", t=2)
                             ).then_inc(st_acc[q % 2], 16)
            sp.wait_ge(z_mm, TILES // 2)
            sp.dma_start(W1_sb[:, 5], W1_of(5)).then_inc(ld_exp, 16)
            sp.dma_start(W2_sb[:, 5], W2_of(5)).then_inc(ld_exp, 16)
            sp.wait_ge(route_ready, 1)
            sp.dma_start(b2_bc, b2.rearrange("e n -> (e n)").partition_broadcast(P)
                         .rearrange("p (e n) -> p e n", e=EXPERTS)).then_inc(ld_b2, 16)
            for s in range(3):
                sp.wait_ge(sc[s], 16 * ((MTILES - s + 2) // 3))
            for k in range(B):
                sp.dma_start(F[:, TPB * k:TPB * (k + 1), :], acc_rows[:, TPB * k:TPB * (k + 1), :]
                             ).then_inc(ld_f[k], 16)
            for k in range(B):
                sp.wait_ge(f_out, k + 1)
                sp.dma_start(out_t[:, TPB * k:TPB * (k + 1), :], X[:, TPB * k:TPB * (k + 1), :]
                             ).then_inc(st_out, 16)
            sp.wait_ge(st_out, 16 * B)
            sp.wait_ge(pad_acc, 16)

        @block.gpsimd
        def _(pool):
            pool.memset(ident[:, :], 0.0).then_inc(c_pool, 1)
            pool.memset(upper[:, :], 1.0).then_inc(c_pool, 1)
            pool.memset(ones_b[:, :], 1.0).then_inc(c_pool, 1)
            pool.memset(ones_row[:, :], 1.0).then_inc(c_pool, 1)
            pool.memset(mhalf[:, :], -0.5).then_inc(c_half, 1)
            pool.wait_ge(c_pool, 4)
            pool.affine_select(out=ident[:, :], in_=ident[:, :], compare_op=ALU.not_equal, fill=1.0, base=0,
                               pattern=[[-1, P]], channel_multiplier=1).then_inc(c_ident, 1)
            pool.affine_select(out=upper[:, :], in_=upper[:, :], compare_op=ALU.is_gt, fill=0.0, base=0,
                               pattern=[[1, P]], channel_multiplier=-1).then_inc(c_pool, 1)
            pool.memset(WE[:, 5, :], 0.0).then_inc(c_vbd, 1)
            pool.iota(tokid[:, :], pattern=[[P, TILES]], base=1, channel_multiplier=1,
                      allow_small_or_imprecise_dtypes=True).then_inc(c_pool, 1)
            pool.iota(iota_m[:, :], pattern=[[1, MTILES]], base=0, channel_multiplier=0,
                      allow_small_or_imprecise_dtypes=True).then_inc(c_pool, 1)
            pool.iota(rank8[:, :], pattern=[[-1, EXPERTS]], base=EXPERTS, channel_multiplier=0,
                      allow_small_or_imprecise_dtypes=True).then_inc(c_pool, 1)
            pool.iota(pad_row[:, :], pattern=[[0, 1]], base=TOKENS + 1, channel_multiplier=1,
                      allow_small_or_imprecise_dtypes=True).then_inc(c_pool, 1)
            pool.wait_ge(tanh_ready, 1)
            pool.wait_ge(ld_small, 16 * 7)
            pool.tensor_scalar(bo_bc[:, :], bo_bc[:, :], tg[:, 0:1], None, ALU.mult).then_inc(bo_ready, 1)
            pool.tensor_scalar(tgam[:, :], tgam[:, :], tg[:, 1:2], None, ALU.mult).then_inc(gb_ready, 1)
            pool.tensor_scalar(tbet[:, :], tbet[:, :], tg[:, 1:2], None, ALU.mult).then_inc(gb_ready, 1)
            pool.wait_ge(ln1_mv, 1)
            pool.wait_ge(c_half, 1)
            pool.tensor_tensor(rstd[:, :], nmr[:, :], mhalf[:, :], ALU.pow).then_inc(pchain, 1)
            pool.wait_ge(pchain, 1)
            pool.tensor_tensor(nmr[:, :], mv[:, :, 0], rstd[:, :], ALU.mult).then_inc(pchain, 1)
            pool.wait_ge(pchain, 2)
            pool.tensor_scalar(nmr[:, :], nmr[:, :], -1.0, None, ALU.mult).then_inc(ln1_ready, 1)
            pool.wait_ge(bo_ready, 1)

            def step(g, u):
                i = 2 * g + u
                static = isinstance(i, int)
                if not static or i < TILES:
                    wait(pool, xn_ready, i + 1)
                    pool.tensor_tensor(at(X, i), at(X, i), bo_bc[:, :], ALU.add).then_inc(bo_added, 1)
                    for h in range(2):
                        wait(pool, rinv_ready, 2 * i + h + 1)
                        w = E[:, u, BANK * h:BANK * (h + 1)].rearrange("p (a k) -> p a k", k=NCTX)
                        r = rinv[:, u, 8 * h:8 * h + 8].unsqueeze(2).to_broadcast([P, 8, NCTX])
                        pool.tensor_tensor(w, w, r, ALU.mult).then_inc(p_ready, 1)
                if not static or 1 <= i <= TILES:
                    v = 1 - u
                    wait(pool, mv2_ready, i)
                    alone(pool, g, pool_waits)
                    pool.tensor_scalar(ve2[:, v:v + 1], mv2[:, v, 1:2], LN_EPS, None, ALU.add
                                       ).then_inc(ve2_ready, 1)
                    wait(pool, ve2_ready, i)
                    wait(pool, xn2_ready, i - 2)
                    pool.tensor_tensor(rs2[:, v, 0:1], ve2[:, v:v + 1], mhalf[:, 0:1], ALU.pow
                                       ).then_inc(pow2_ready, 1)
                    wait(pool, pow2_ready, i)
                    alone(pool, g, pool_waits)
                    pool.tensor_scalar(rs2[:, v, 1:2], mv2[:, v, 0:1], rs2[:, v, 0:1], -1.0, ALU.mult, ALU.mult
                                       ).then_inc(rstd2_ready, 1)

            attention_steps(pool, step)

            pool.wait_ge(o_mm, TILES)
            pool.iota(iota_lo[:, :], pattern=[[1, P]], base=0, channel_multiplier=0,
                      allow_small_or_imprecise_dtypes=True).then_inc(c_pool, 1)
            pool.memset(cum[:, :, :], 0.0).then_inc(c_pool, 1)
            pool.wait_ge(gb_ready, 2)
            pool.wait_ge(x2_ready, TILES)
            pool.wait_ge(mv2_ready, TILES)

            def half_shared(q):
                pool.wait_ge(z_gelu, q + 1)
                pool.tensor_scalar(res[:, q % 2], res[:, q % 2], 0.5, None, ALU.mult).then_inc(z_ready, 1)

            for q in range(TILES // 2):
                half_shared(q)
                if q % 2:
                    k = q // 2
                    part = X[:, TPB * k:TPB * (k + 1), :]
                    pool.wait_ge(xn2_ready, TILES)
                    pool.tensor_tensor(part, part, tbet[:, :].unsqueeze(1).to_broadcast([P, TPB, D]), ALU.add
                                       ).then_inc(x_beta, 1)
            pool.wait_ge(st_acc[0], 16 * (TILES // 4))
            pool.wait_ge(st_acc[1], 16 * (TILES // 4))
            pool.memset(res[:, 0, 0:D], 0.0).then_inc(pchain, 1)
            pool.wait_ge(pchain, 3)
            pool.dma_start(acc_dram[TOKENS:TOKENS + P, :], res[:, 0, 0:D]).then_inc(pad_acc, 16)
            for s in range(2):
                pool.wait_ge(st_xn2[s], 16 * TILES // 2)

            def gather(g, u):
                i = 3 * g + u
                wait(pool, gi_ready, i + 1)
                wait(pool, xsT_mm, i - 2)
                alone(pool, g, pool_waits)
                pool.indirect_dma_start(xs[:, u, :], None, xn2_dram,
                                        bass.IndirectOffsetOnAxis(ap=gcol[u], axis=0)).then_inc(ga[u], 16)

            gather(0, 0)
            gather(0, 1)
            pool.wait_ge(pad_acc, 16)

            def mix(g, u):
                i = 3 * g + u
                static = isinstance(i, int)
                if not static or i + 2 < MTILES:
                    gather(g + (u + 2) // 3, (u + 2) % 3)
                if not static or i >= 1:
                    s = (u - 1) % 3
                    wait(pool, y_ready, i)
                    wait(pool, sc[(u - 2) % 3], 16 * (g + (u - 2) // 3 + 1))
                    alone(pool, g, pool_waits)
                    pool.indirect_dma_start(acc_dram, bass.IndirectOffsetOnAxis(ap=scol[s], axis=0), ys[:, s, :],
                                            None, compute_op=ALU.add).then_inc(sc[s], 16)

            mixture_steps(pool, mix)

            for k in range(B):
                tiles = slice(TPB * k, TPB * (k + 1))
                pool.wait_ge(f_mv, k + 1)
                pool.tensor_scalar(nmr[:, tiles], mv[:, tiles, 1], LN_EPS, None, ALU.add).then_inc(f_ve, 1)
                pool.wait_ge(f_ve, k + 1)
                pool.tensor_tensor(rstd[:, tiles], nmr[:, tiles], mhalf[:, 0:TPB], ALU.pow).then_inc(f_pow, 1)
                pool.wait_ge(f_pow, 2 * k + 1)
                pool.tensor_tensor(nmr[:, tiles], mv[:, tiles, 0], rstd[:, tiles], ALU.mult).then_inc(f_pow, 1)
                pool.wait_ge(f_pow, 2 * k + 2)
                pool.tensor_scalar(nmr[:, tiles], nmr[:, tiles], -1.0, None, ALU.mult).then_inc(f_rstd, 1)
                if k >= 1:
                    last = slice(TPB * (k - 1), TPB * k)
                    pool.wait_ge(f_gam, k)
                    pool.tensor_tensor(X[:, last, :], X[:, last, :], F[:, last, :], ALU.add).then_inc(f_out, 1)
            last = slice(TPB * (B - 1), TPB * B)
            pool.wait_ge(f_gam, B)
            pool.tensor_tensor(X[:, last, :], X[:, last, :], F[:, last, :], ALU.add).then_inc(f_out, 1)

        @block.scalar
        def _(act):
            act.dma_start(tg[:, 0:1], g_xattn.partition_broadcast(P)).then_inc(ld_small, 16)
            act.dma_start(tg[:, 1:2], g_ffn.partition_broadcast(P)).then_inc(ld_small, 16)
            act.dma_start(b1_rows[:, :], b1.rearrange("e (j p) -> (e j) p", p=P)).then_inc(ld_small, 16)
            act.dma_start(gW[:, :, :], gate_W.rearrange("(c p) n -> p c n", p=P)).then_inc(ld_small, 16)
            act.dma_start(bo_bc[:, :], bo.partition_broadcast(P)).then_inc(ld_small, 16)
            act.dma_start(tgam[:, :], gamma.partition_broadcast(P)).then_inc(ld_small, 16)
            act.dma_start(tbet[:, :], beta.partition_broadcast(P)).then_inc(ld_small, 16)
            act.wait_ge(ld_small, 16 * 7)
            act.activation(tg[:, :], tg[:, :], ACT.Tanh).then_inc(tanh_ready, 1)
            act.wait_ge(b1_mm, 1)
            act.activation(b1T[:, :], PS[:, 7, 0:EXPERTS * HC], ACT.Copy).then_inc(b1_ready, 1)

            for n in range(1, GROUPS, 2):
                act.wait_ge(pre_mm, n + 1)
                bank = PS[:, n % 8, :]
                if n < QT0:
                    j = 2 * (n - KT0)
                    m = act.activation(KT[:, j:j + 2, :].rearrange("p j n -> p (j n)"), bank, ACT.Copy, scale=SCALE)
                elif n < A0:
                    j = 2 * (n - QT0)
                    m = act.activation(WqT[:, j:j + 2, :].rearrange("p j n -> p (j n)"), bank, ACT.Copy)
                elif n < VT0:
                    h = n - A0
                    for c in range(DC):
                        m = act.activation(A[:, c, :, NCTX * h:NCTX * (h + 1)],
                                           bank[:, D * c:D * (c + 1)].rearrange("p (b k) -> p b k", b=B), ACT.Copy)
                elif n < VO0:
                    j = 2 * (n - VT0)
                    act.wait_ge(c_vbd, 1)
                    for s in range(2):
                        for jj in range(2):
                            m = act.activation(VBD[DH * s:DH * (s + 1), j + jj, :, s, :],
                                               bank[DH * s:DH * (s + 1), D * jj:D * (jj + 1)].rearrange(
                                                   "p (b k) -> p b k", b=B), ACT.Copy)
                else:
                    b, j = divmod(2 * (n - VO0), JC)
                    m = act.activation(VO[:, b, j:j + 2, :].rearrange("p j n -> p (j n)"), bank, ACT.Copy)
                m.then_inc(pre_act, 1)

            act.wait_ge(ln1_ready, 1)

            def ln1(i, s):
                wait(act, xT_mm, i - 1)
                act.activation(xn_b[s][:, :], at(X, i), ACT.Identity, bias=col(nmr, i), scale=col(rstd, i)
                               ).then_inc(xn_ready, 1)

            def xT_evac(i, s):
                wait(act, xT_mm, i + 1)
                wait(act, s_mm, 2 * (i - 1))
                act.activation(xnT_b[s][:, :, :].rearrange("p c n -> p (c n)"), xT_ps, ACT.Copy
                               ).then_inc(xT_ready, 1)

            ln1(0, 0)
            xT_evac(0, 0)
            ln1(1, 1)

            def step(g, u):
                i = 2 * g + u
                v = 1 - u
                static = isinstance(i, int)
                scores = not static or i < TILES
                if not static or i >= 2:
                    wait(act, rstd2_ready, i - 1)
                    wait(act, st_xn2[u], 16 * (g - 1))
                    act.activation(xn2_b[u], at(X, i - 2), ACT.Identity, bias=rs2[:, u, 1:2],
                                   scale=rs2[:, u, 0:1]).then_inc(xn2_ready, 1)
                if not static or 1 <= i <= TILES:
                    for h in range(2):
                        wait(act, pT_mm, 2 * i - 2 + h + 1)
                        wait(act, o_mm, i - 2)
                        act.activation(PT[:, v, 4 * h:4 * h + 4, :].rearrange("p j n -> p (j n)"), PT_ps[h],
                                       ACT.Copy).then_inc(pT_ready, 1)
                if scores:
                    wait(act, shifted, 2 * i + 1)
                    act.activation(E[:, u, 0:BANK], E[:, u, 0:BANK], ACT.Exp).then_inc(exp_ready, 1)
                if not static or i + 1 < TILES:
                    xT_evac(i + 1, v)
                if not static or i >= 2:
                    wait(act, x2T_mm, i - 1)
                    wait(act, st_x2T[u], 16 * (g - 1))
                    wait(act, g_mm, i - 3 if static else 0)
                    act.activation(xn2T_b[u][:, :, :].rearrange("p c n -> p (c n)"), x2T_ps, ACT.Copy
                                   ).then_inc(x2T_ready, 1)
                if scores:
                    wait(act, shifted, 2 * i + 2)
                    act.activation(E[:, u, BANK:], E[:, u, BANK:], ACT.Exp).then_inc(exp_ready, 1)
                if not static or i + 2 < TILES:
                    ln1(i + 2, u)

            attention_steps(act, step)

            act.wait_ge(lg_ready, 1)
            act.activation(RT[0], RT[0], ACT.Exp).then_inc(pexp_ready, 1)
            for q in range(TILES // 2):
                act.wait_ge(z_mm, q + 1)
                if q >= 2:
                    act.wait_ge(st_acc[q % 2], 16 * (q // 2))
                act.activation(res[:, q % 2], PS[:, q % 4, :], ACT.Gelu).then_inc(z_gelu, 1)
            act.wait_ge(route_ready, 1)
            act.wait_ge(b1_ready, 1)

            def xsT_evac(i):
                wait(act, xsT_mm, i + 1)
                wait(act, h_mm, 2 * i)
                act.activation(xsT[:, :, :].rearrange("p c n -> p (c n)"), PS[:, 5, 0:D], ACT.Copy
                               ).then_inc(xsT_ready, 1)

            xsT_evac(0)

            def mix(g, u):
                i = 3 * g + u
                static = isinstance(i, int)
                if not static or i + 1 < MTILES:
                    xsT_evac(i + 1)
                if not static or i < MTILES:
                    e = act.value_load(col(etile, i), min_val=0, max_val=EXPERTS - 1)
                    for h in range(2):
                        wait(act, hT_mm, 2 * i + h + 1)
                        if h == 0:
                            wait(act, y_mm, i)
                        for j in range(4 * h, 4 * h + 4):
                            m = act.activation(hidT[:, j, :], PS[:, 2 + h, P * (j % 4):P * (j % 4 + 1)], ACT.Gelu,
                                               bias=b1T[:, bass.ds(e * HC + j, 1)])
                        m.then_inc(gel_ready, 1)

            mixture_steps(act, mix)

            for k in range(B):
                act.wait_ge(f_rstd, k + 1)
                for t in range(TPB * k, TPB * (k + 1)):
                    m = act.activation(F[:, t, :], F[:, t, :], ACT.Identity, bias=nmr[:, t:t + 1],
                                       scale=rstd[:, t:t + 1])
                m.then_inc(f_norm, 1)

        @block.vector
        def _(dve):
            chain = [0]

            def link(ins):
                chain[0] += 1
                ins.then_inc(dchain, 1)
                dve.wait_ge(dchain, chain[0])

            def evac(n):
                dve.wait_ge(pre_mm, n + 1)
                bank = PS[:, n % 8, :]
                if n == 0:
                    m = dve.tensor_copy(cT[:, :, :].rearrange("p c n -> p (c n)"), bank)
                elif n < QT0:
                    j = 2 * (n - KT0)
                    m = dve.tensor_scalar(KT[:, j:j + 2, :].rearrange("p j n -> p (j n)"), bank, SCALE, None,
                                          ALU.mult)
                elif n < A0:
                    j = 2 * (n - QT0)
                    m = dve.tensor_copy(WqT[:, j:j + 2, :].rearrange("p j n -> p (j n)"), bank)
                elif n < VT0:
                    h = n - A0
                    for c in range(DC):
                        m = dve.tensor_copy(A[:, c, :, NCTX * h:NCTX * (h + 1)],
                                            bank[:, D * c:D * (c + 1)].rearrange("p (b k) -> p b k", b=B))
                elif n < VO0:
                    j = 2 * (n - VT0)
                    dve.wait_ge(c_vbd, 1)
                    for s in range(2):
                        for jj in range(2):
                            m = dve.tensor_copy(VBD[DH * s:DH * (s + 1), j + jj, :, s, :],
                                                bank[DH * s:DH * (s + 1), D * jj:D * (jj + 1)].rearrange(
                                                    "p (b k) -> p b k", b=B))
                else:
                    b, j = divmod(2 * (n - VO0), JC)
                    m = dve.tensor_copy(VO[:, b, j:j + 2, :].rearrange("p j n -> p (j n)"), bank)
                m.then_inc(pre_dve, 1)

            for n in range(0, A0, 2):
                evac(n)
            dve.wait_ge(ld_x, 16 * B)
            for t in range(TILES):
                m = dve.bn_stats(st[:, t, :], X[:, t, :])
            link(m)
            for t in range(TILES):
                m = dve.bn_aggr(mv[:, t, :], st[:, t, :])
            link(m)
            dve.tensor_scalar(nmr[:, :], mv[:, :, 1], LN_EPS, None, ALU.add).then_inc(ln1_mv, 1)
            for n in range(A0 + A0 % 2, GROUPS, 2):
                evac(n)
            dve.wait_ge(tanh_ready, 1)

            def step(g, u):
                i = 2 * g + u
                v = 1 - u
                static = isinstance(i, int)
                if not static or i < TILES:
                    for h in range(2):
                        s = S_ps[h].rearrange("p (a k) -> p a k", k=NCTX)
                        m8 = mx[:, u, 8 * h:8 * h + 8]
                        wait(dve, s_mm, 2 * i + h + 1)
                        dve.tensor_reduce(m8, s, AX, ALU.max).then_inc(mx_ready, 1)
                        wait(dve, mx_ready, 2 * i + h + 1)
                        wait(dve, pT_mm, 2 * i - 4 + h + 1)
                        dve.tensor_tensor(E[:, u, BANK * h:BANK * (h + 1)].rearrange("p (a k) -> p a k", k=NCTX), s,
                                          m8.unsqueeze(2).to_broadcast([P, 8, NCTX]), ALU.subtract
                                          ).then_inc(shifted, 1)
                    for h in range(2):
                        wait(dve, exp_ready, 2 * i + h + 1)
                        r8 = rsum[:, u, 8 * h:8 * h + 8]
                        dve.tensor_reduce(r8, E[:, u, BANK * h:BANK * (h + 1)].rearrange("p (a k) -> p a k", k=NCTX),
                                          AX, ALU.add).then_inc(sum_ready, 1)
                        wait(dve, sum_ready, 2 * i + h + 1)
                        wait(dve, p_ready, 2 * i - 4 + h + 1)
                        dve.reciprocal(rinv[:, u, 8 * h:8 * h + 8], r8).then_inc(rinv_ready, 1)
                if not static or 1 <= i <= TILES:
                    wait(dve, o_mm, i)
                    wait(dve, bo_added, i)
                    dve.scalar_tensor_tensor(at(X, i - 1), O_ps, tg[:, 0:1], at(X, i - 1), ALU.mult, ALU.add
                                             ).then_inc(x2_ready, 1)
                    wait(dve, x2_ready, i)
                    alone(dve, g, dve_waits)
                    dve.bn_stats(st2[:, v, :], at(X, i - 1)).then_inc(st2_ready, 1)
                    wait(dve, st2_ready, i)
                    wait(dve, rstd2_ready, i - 2)
                    alone(dve, g, dve_waits)
                    dve.bn_aggr(mv2[:, v, :], st2[:, v, :]).then_inc(mv2_ready, 1)

            attention_steps(dve, step)

            TE = [P, TILES, EXPERTS]
            L = G_ps.rearrange("p (t e) -> p t e", e=EXPERTS)
            prob, oh1, oh2, tmp, tmp2 = RT[0], RT[1], RT[2], RT[3], RT[4]
            lmax, ssum, sinv, m1, m2, c1, c2, den = [sm[:, n, :] for n in range(8)]
            r8 = rank8[:, :].unsqueeze(1).to_broadcast(TE)

            def per_token(a):
                return a.unsqueeze(2).to_broadcast(TE)

            dve.wait_ge(g_mm, TILES)
            dve.wait_ge(c_pool, 11)
            link(dve.tensor_reduce(lmax, L, AX, ALU.max))
            dve.tensor_tensor(prob, L, per_token(lmax), ALU.subtract).then_inc(lg_ready, 1)
            dve.wait_ge(pexp_ready, 1)
            link(dve.tensor_reduce(ssum, prob, AX, ALU.add))
            link(dve.reciprocal(sinv, ssum))
            link(dve.tensor_tensor(prob, prob, per_token(sinv), ALU.mult))

            def largest(p, m, c, oh):
                link(dve.tensor_reduce(m, p, AX, ALU.max))
                link(dve.tensor_tensor(tmp, p, per_token(m), ALU.is_equal))
                link(dve.tensor_tensor(tmp, tmp, r8, ALU.mult))
                link(dve.tensor_reduce(c, tmp, AX, ALU.max))
                link(dve.tensor_tensor(oh, r8, per_token(c), ALU.is_equal))

            largest(prob, m1, c1, oh1)
            link(dve.scalar_tensor_tensor(tmp2, oh1, -2.0, prob, ALU.mult, ALU.add))
            largest(tmp2, m2, c2, oh2)
            dve.tensor_tensor(M_bf[:, :, :], oh1, oh2, ALU.add).then_inc(M_ready, 1)
            link(dve.tensor_tensor(den, m1, m2, ALU.add))
            link(dve.reciprocal(sinv, den))
            dve.tensor_tensor(wtok[:, 0, :], m1, sinv, ALU.mult)
            link(dve.tensor_tensor(wtok[:, 1, :], m2, sinv, ALU.mult))
            dve.wait_ge(cnt_mm, 1)
            link(dve.tensor_scalar(cnti[:, 0, :], cnt_ps, float(P - 1), None, ALU.add))
            link(dve.tensor_scalar(cnti[:, 1, :], cnti[:, 0, :], 7, None, ALU.logical_shift_right))
            link(dve.tensor_copy(cum[:, 0, EXPERTS:], cnti[:, 1, :]))
            for n in range(3):
                link(dve.tensor_tensor(cum[:, n + 1, EXPERTS:], cum[:, n, EXPERTS:],
                                       cum[:, n, EXPERTS - 2 ** n:2 * EXPERTS - 2 ** n], ALU.add))
            first = cum[:, 3, EXPERTS - 1:2 * EXPERTS - 1]
            link(dve.tensor_scalar(base8[:, :], first, float(P), None, ALU.mult))
            dve.wait_ge(rank_mm, 1)
            link(dve.tensor_tensor(tmp, rank_ps.rearrange("p (t e) -> p t e", e=EXPERTS),
                                   base8[:, :].unsqueeze(1).to_broadcast(TE), ALU.add))
            for k, oh in ((0, oh1), (1, oh2)):
                link(dve.tensor_tensor(tmp2, tmp, oh, ALU.mult))
                link(dve.tensor_reduce(pos[:, k, :], tmp2, AX, ALU.add))
            link(dve.tensor_copy(posi[:, 0, :], pos[:, :, :].rearrange("p k t -> p (k t)")))
            dve.tensor_scalar(posi[:, 1, :], posi[:, 0, :], P - 1, None, ALU.bitwise_and)
            link(dve.tensor_scalar(posi[:, 2, :], posi[:, 0, :], 7, None, ALU.logical_shift_right))
            link(dve.tensor_copy(lohi[:, :, :], posi[:, 1:3, :]))
            PM = [P, PAIRS, MTILES]
            link(dve.tensor_tensor(eq_hi, iota_m[:, :].unsqueeze(1).to_broadcast(PM),
                                   lohi[:, 1, :].unsqueeze(2).to_broadcast(PM), ALU.is_equal))
            for k in range(CHOICES):
                n = slice(TILES * k, TILES * (k + 1))
                TM = [P, TILES, MTILES]
                dve.tensor_tensor(RH[:, n, 0, :], eq_hi[:, n, :], tokid[:, :].unsqueeze(2).to_broadcast(TM),
                                  ALU.mult)
                dve.tensor_tensor(RH[:, n, 1, :], eq_hi[:, n, :], wtok[:, k, :].unsqueeze(2).to_broadcast(TM),
                                  ALU.mult)
            for n in range(0, PAIRS, 8):
                NM = [P, 8, P]
                dve.tensor_tensor(OH_lo[:, n:n + 8, :], iota_lo[:, :].unsqueeze(1).to_broadcast(NM),
                                  lohi[:, 0, n:n + 8].unsqueeze(2).to_broadcast(NM), ALU.is_equal
                                  ).then_inc(oh_ready, 1)
            ME = [1, MTILES, EXPERTS]
            link(dve.tensor_tensor(cmp[:, :, :], iota_m[0:1, :].unsqueeze(2).to_broadcast(ME),
                                   first[0:1, :].unsqueeze(1).to_broadcast(ME), ALU.is_ge))
            link(dve.tensor_reduce(etf[:, :], cmp[:, :, :], AX, ALU.add))
            link(dve.tensor_scalar(etile[:, :], etf[:, :], -1.0, None, ALU.add))
            dve.wait_ge(tab_mm, 1)
            link(dve.tensor_copy(tab[:, 0:2, :].rearrange("p a m -> p (a m)"), tab_ps))
            dve.tensor_scalar(gidx[:, :], tab[:, 0, :], -1.0, 0.0, ALU.add, ALU.max)
            link(dve.tensor_scalar(tab[:, 2, :], tab[:, 0, :], 0.0, None, ALU.is_equal))
            link(dve.scalar_tensor_tensor(tab[:, 2, :], tab[:, 2, :], pad_row[:, :], tab[:, 0, :], ALU.mult,
                                          ALU.add))
            dve.tensor_scalar(sidx[:, :], tab[:, 2, :], -1.0, None, ALU.add).then_inc(route_ready, 1)
            dve.wait_ge(route_ready, 1)

            def token_numbers(i, s, r):
                wait(dve, ga[s], 16 * r)
                dve.tensor_copy(gcol[s], col(gidx, i)).then_inc(gi_ready, 1)

            token_numbers(0, 0, 0)
            token_numbers(1, 1, 0)
            dve.wait_ge(ld_b2, 16)

            def mix(g, u):
                i = 3 * g + u
                static = isinstance(i, int)
                if not static or i + 2 < MTILES:
                    token_numbers(i + 2, (u + 2) % 3, g + (u + 2) // 3)
                if not static or i < MTILES:
                    for h in range(2):
                        wait(dve, h_mm, 2 * i + h + 1)
                        wait(dve, hT_mm, 2 * i)
                        dve.tensor_copy(hid[:, BANK * h:BANK * (h + 1)], PS[:, h, :]).then_inc(h_ready, 1)
                if not static or i >= 1:
                    s = (u - 1) % 3
                    e = dve.value_load(col(etile, i - 1), min_val=0, max_val=EXPERTS - 1)
                    wait(dve, y_mm, i)
                    wait(dve, sc[s], 16 * (g + (u - 1) // 3))
                    dve.tensor_tensor(ys[:, s, :], PS[:, 4, 0:D], at(b2_bc, e), ALU.add).then_inc(yb_ready, 1)
                    dve.tensor_copy(scol[s], col(sidx, i - 1))
                    wait(dve, yb_ready, i)
                    dve.tensor_scalar(ys[:, s, :], ys[:, s, :], col(tab[:, 1, :], i - 1), None, ALU.mult
                                      ).then_inc(y_ready, 1)

            mixture_steps(dve, mix)

            def gain(k):
                part = F[:, TPB * k:TPB * (k + 1), :]
                dve.wait_ge(f_norm, k + 1)
                dve.tensor_tensor(part, part, tgam[:, :].unsqueeze(1).to_broadcast([P, TPB, D]), ALU.mult
                                  ).then_inc(f_gam, 1)

            for k in range(B):
                dve.wait_ge(ld_f[k], 16)
                for t in range(TPB * k, TPB * (k + 1)):
                    m = dve.bn_stats(st[:, t, :], F[:, t, :])
                link(m)
                for t in range(TPB * k, TPB * (k + 1)):
                    m = dve.bn_aggr(mv[:, t, :], st[:, t, :])
                m.then_inc(f_mv, 1)
                if k >= 1:
                    gain(k - 1)
            gain(B - 1)

        @block.tensor
        def _(pe):
            pe.wait_ge(c_ident, 1)
            pe.wait_ge(ld_small, 16 * 7)
            pe.transpose(PS[:, 7, 0:EXPERTS * HC], b1_rows[:, :], ident[0:EXPERTS * HC, 0:EXPERTS * HC]
                         ).then_inc(b1_mm, 1)

            def claim(n):
                if n == 7:
                    pe.wait_ge(b1_ready, 1)
                if n >= 8:
                    s, c = (pre_act, (n - 8) // 2 + 1) if n % 2 else (pre_dve, (n - 8) // 2 + 1)
                    pe.wait_ge(s, c)
                return PS[:, n % 8, :]

            pe.wait_ge(ld_ctx, 16)
            bank = claim(0)
            for c in range(DC):
                for t in range(DC):
                    m = pe.transpose(bank[:, D * c + P * t:D * c + P * (t + 1)], ctx_sb[:, t, P * c:P * (c + 1)],
                                     ident[:, :])
            m.then_inc(pre_mm, 1)

            def project(n, w, j):
                bank = claim(n)
                for jj in range(2):
                    for c in range(DC):
                        m = pe.matmul(bank[:, D * jj:D * (jj + 1)], w[:, c, P * (j + jj):P * (j + jj + 1)],
                                      cT[:, c, :], start=(c == 0), stop=(c == DC - 1))
                m.then_inc(pre_mm, 1)

            evacuated(pe, 0)
            pe.wait_ge(ld_wk, 16)
            for n in range(KT0, QT0):
                project(n, Wk_sb, 2 * (n - KT0))
            pe.wait_ge(ld_wq, 16)
            for n in range(QT0, A0):
                bank = claim(n)
                j = 2 * (n - QT0)
                for jj in range(2):
                    for c in range(DC):
                        m = pe.transpose(bank[:, D * jj + P * c:D * jj + P * (c + 1)],
                                         Wq_sb[:, c, P * (j + jj):P * (j + jj + 1)], ident[:, :])
                m.then_inc(pre_mm, 1)
            evacuated(pe, A0 - 1)
            for n in range(A0, VT0, 2):
                j = (n - A0) // 2
                banks = [claim(n), claim(n + 1)]
                for c in range(DC):
                    for s in range(2):
                        rows = slice(DH * s, DH * (s + 1))
                        m = pe.matmul(banks[s][:, D * c:D * (c + 1)], WqT[rows, j, P * c:P * (c + 1)],
                                      KT[rows, j, :], start=True, stop=True)
                m.then_inc(pre_mm, 2)
            pe.wait_ge(ld_wv, 16)
            for n in range(VT0, VO0):
                project(n, Wv_sb, 2 * (n - VT0))
            pe.wait_ge(ld_wo, 16)
            evacuated(pe, VO0 - 1)
            for n in range(VO0, GROUPS):
                bank = claim(n)
                b, j = divmod(2 * (n - VO0), JC)
                for jj in range(2):
                    m = pe.matmul(bank[:, D * jj:D * (jj + 1)],
                                  VBD[:, j + jj, b].rearrange("p h k -> p (h k)"), Wo_sb[:, j + jj, :],
                                  start=True, stop=True)
                m.then_inc(pre_mm, 1)
            evacuated(pe, GROUPS - 1)

            def transpose_x(i, s):
                wait(pe, xn_ready, i + 1)
                wait(pe, xT_ready, i)
                for c in range(DC):
                    m = pe.transpose(xT_ps[:, P * c:P * (c + 1)], xn_b[s][:, P * c:P * (c + 1)], ident[:, :])
                m.then_inc(xT_mm, 1)

            transpose_x(0, 0)

            def step(g, u):
                i = 2 * g + u
                v = 1 - u
                static = isinstance(i, int)

                def scores(h):
                    b = batch_of(g, u)
                    if h == 0:
                        wait(pe, xT_ready, i + 1)
                    wait(pe, shifted, 2 * i - 2 + h + 1)
                    for c in range(DC):
                        a = A[:, c, :, BANK * h:BANK * (h + 1)]
                        m = pe.matmul(S_ps[h], xnT_b[u][:, c, :], at(a, b), start=(c == 0), stop=(c == DC - 1))
                    m.then_inc(s_mm, 1)

                if not static or i < TILES:
                    scores(0)
                if not static or 1 <= i <= TILES:
                    for h in range(2):
                        wait(pe, p_ready, 2 * i - 2 + h + 1)
                        wait(pe, pT_ready, 2 * i - 4 + h + 1)
                        for j in range(4):
                            c0 = BANK * h + P * j
                            m = pe.transpose(PT_ps[h][:, P * j:P * (j + 1)], E[:, v, c0:c0 + P], ident[:, :])
                        m.then_inc(pT_mm, 1)
                if not static or i < TILES:
                    scores(1)
                if not static or i + 1 < TILES:
                    transpose_x(i + 1, v)
                if not static or i >= 2:
                    wait(pe, xn2_ready, i - 1)
                    wait(pe, x2T_ready, i - 2)
                    for c in range(DC):
                        m = pe.transpose(x2T_ps[:, P * c:P * (c + 1)], xn2_b[u][:, P * c:P * (c + 1)], ident[:, :])
                    m.then_inc(x2T_mm, 1)
                if not static or 1 <= i <= TILES:
                    b = batch_of(g, u - 1)
                    wait(pe, x2_ready, i - 1)
                    for j in range(JC):
                        if j % 4 == 0:
                            wait(pe, pT_ready, 2 * i - 2 + j // 4 + 1)
                        m = pe.matmul(O_ps, PT[:, v, j, :], at(VO[:, :, j, :], b), start=(j == 0),
                                      stop=(j == JC - 1))
                    m.then_inc(o_mm, 1)
                if not static or i >= 2:
                    wait(pe, x2T_ready, i - 1)
                    k = i - 2
                    gate = (G_ps[:, EXPERTS * k:EXPERTS * (k + 1)] if static
                            else G_ps[:, bass.ds(k * EXPERTS, EXPERTS)])
                    for c in range(DC):
                        m = pe.matmul(gate, xn2T_b[u][:, c, :], gW[:, c, :], start=(c == 0), stop=(c == DC - 1))
                    m.then_inc(g_mm, 1)

            attention_steps(pe, step)

            for s in range(2):
                pe.wait_ge(st_x2T[s], 16 * TILES // 2)
            pe.wait_ge(c_pool, 11)
            pe.wait_ge(ld_shared, 16 * 3)

            def shared(q):
                z = PS[:, q % 4, :]
                if q >= 4:
                    pe.wait_ge(z_gelu, q - 3)
                pe.matmul(z, ones_row[:, :], sb_row[:, :, :].rearrange("p a n -> p (a n)"), start=True, stop=False,
                          skip_group_check=True)
                for t in range(2):
                    for c in range(DC):
                        m = pe.matmul(z[:, D * t:D * (t + 1)], XN2T[:, 2 * q + t, P * c:P * (c + 1)], sW[:, c, :],
                                      start=False, stop=(c == DC - 1), skip_group_check=True)
                m.then_inc(z_mm, 1)

            for q in range(3):
                shared(q)
            pe.wait_ge(M_ready, 1)
            for t in range(TILES):
                m = pe.matmul(cnt_ps, ones_b[:, :], M_bf[:, t, :], start=(t == 0), stop=(t == TILES - 1))
            m.then_inc(cnt_mm, 1)
            Mf = M_bf[:, :, :].rearrange("p t e -> p (t e)")
            n = TILES * EXPERTS
            pe.matmul(rank_ps, upper[:, :], Mf, start=True, stop=False, skip_group_check=True)
            for t in range(1, TILES):
                m = pe.matmul(rank_ps[:, EXPERTS * t:], ones_b[:, :], Mf[:, 0:n - EXPERTS * t], start=False,
                              stop=(t == TILES - 1), skip_group_check=True)
            m.then_inc(rank_mm, 1)
            for q in range(3, 7):
                shared(q)
            for k in range(PAIRS):
                if k % 8 == 0:
                    pe.wait_ge(oh_ready, k // 8 + 1)
                m = pe.matmul(tab_ps, OH_lo[:, k, :], RH[:, k, :, :].rearrange("p a m -> p (a m)"), start=(k == 0),
                              stop=(k == PAIRS - 1))
            m.then_inc(tab_mm, 1)
            shared(7)
            pe.wait_ge(z_gelu, TILES // 2)
            pe.wait_ge(route_ready, 1)
            pe.wait_ge(ld_exp, 16 * 2 * EXPERTS)

            def transpose_rows(g, u):
                i = 3 * g + u
                wait(pe, ga[u], 16 * (g + 1))
                wait(pe, xsT_ready, i)
                for c in range(DC):
                    m = pe.transpose(PS[:, 5, P * c:P * (c + 1)], xs[:, u, P * c:P * (c + 1)], ident[:, :])
                m.then_inc(xsT_mm, 1)

            transpose_rows(0, 0)

            def mix(g, u):
                i = 3 * g + u
                static = isinstance(i, int)
                if not static or i < MTILES:
                    e = pe.value_load(col(etile, i), min_val=0, max_val=EXPERTS - 1)
                    wait(pe, xsT_ready, i + 1)
                    for h in range(2):
                        wait(pe, h_ready, 2 * i - 2 + h + 1)
                        for c in range(DC):
                            m = pe.matmul(PS[:, h, :], xsT[:, c, :],
                                          at(W1_sb[:, :, c, BANK * h:BANK * (h + 1)], e), start=(c == 0),
                                          stop=(c == DC - 1))
                        m.then_inc(h_mm, 1)
                if not static or i + 1 < MTILES:
                    transpose_rows(g + (u + 1) // 3, (u + 1) % 3)
                if not static or i >= 1:
                    e = pe.value_load(col(etile, i - 1), min_val=0, max_val=EXPERTS - 1)
                    wait(pe, yb_ready, i - 1)
                    for j in range(HC):
                        if j % 4 == 0:
                            wait(pe, gel_ready, 2 * i - 2 + j // 4 + 1)
                        m = pe.matmul(PS[:, 4, 0:D], hidT[:, j, :], at(W2_sb[:, :, j, :], e), start=(j == 0),
                                      stop=(j == HC - 1))
                    m.then_inc(y_mm, 1)
                if not static or i < MTILES:
                    for h in range(2):
                        wait(pe, h_ready, 2 * i + h + 1)
                        wait(pe, gel_ready, 2 * i - 2 + h + 1)
                        for j in range(4):
                            c0 = BANK * h + P * j
                            m = pe.transpose(PS[:, 2 + h, P * j:P * (j + 1)], hid[:, c0:c0 + P], ident[:, :])
                        m.then_inc(hT_mm, 1)

            mixture_steps(pe, mix)


INPUTS = ["x", "ctx_1024", "g_xattn", "g_ffn", "L0_xattn_Wq", "L0_xattn_Wk", "L0_xattn_Wv", "L0_xattn_Wo",
          "L0_xattn_bo", "L0_ffn_W1", "L0_ffn_b1", "L0_ffn_W2", "L0_ffn_b2", "L0_ffn_gate_W", "L0_ffn_shared_W",
          "L0_ffn_shared_b", "L0_ffn_gamma", "L0_ffn_beta"]


def kernel(**inputs):
    import concourse.bacc as bacc
    from concourse.bass_utils import run_bass_kernel_spmd

    nc = bacc.Bacc("TRN2", target_bir_lowering=False, num_devices=1)
    arrays, args = {}, []
    for name in INPUTS:
        a = np.ascontiguousarray(inputs[name])
        arrays[name] = a
        args.append(nc.dram_tensor(name, a.shape, mybir.dt.from_np(a.dtype), kind="ExternalInput").ap())
    out = nc.dram_tensor("out", (B, S, D), f32, kind="ExternalOutput").ap()
    xn2_dram = nc.dram_tensor("xn2_rows", (TOKENS, D), f32, kind="Internal").ap()
    acc_dram = nc.dram_tensor("acc_rows", (TOKENS + P, D), f32, kind="Internal").ap()
    build(nc, *args, out, xn2_dram, acc_dram)
    r = run_bass_kernel_spmd(nc, [arrays], core_ids=[0])
    return r.results[0]["out"]
```

```python
from contextlib import ExitStack

import numpy as np
import concourse.bass as bass
from concourse import mybir

P = 128
B, S, D = 4, 512, 256
NCTX = 64
HEADS, DH = 16, 64
INNER = HEADS * DH
EXPERTS, HID = 8, 1024
CHOICES = 2
TOKENS = B * S
TILES = TOKENS // P
TPB = S // P
DC = D // P
HC = HID // P
JC = INNER // P
MTILES = (CHOICES * TOKENS + EXPERTS * (P - 1)) // P
PAIRS = CHOICES * TILES
BANK = 512
QUARTERS = 4
QW = DC * HID * 2 // QUARTERS
EARLY = 2
SPLIT_LEAD = 2
W_SCALE = 256.0
H_SCALE = 16.0
LN_EPS = 1e-5
SCALE = DH ** -0.5

f32 = mybir.dt.float32
bf16 = mybir.dt.bfloat16
f16 = mybir.dt.float16
i32 = mybir.dt.int32
ALU = mybir.AluOpType
ACT = mybir.ActivationFunctionType
AX = mybir.AxisListType.X


def build(nc, x, ctx_in, g_xattn, g_ffn, Wq, Wk, Wv, Wo, bo, W1, b1, W2, b2, gate_W, shared_W, shared_b,
          gamma, beta, out, xn2_dram, acc_dram):
    stack = ExitStack()
    with stack:
        def sb(name, shape, dt=f32):
            return stack.enter_context(nc.sbuf_tensor(name, shape, dt))

        def sem(name):
            return stack.enter_context(nc.semaphore(name))

        WE = sb("WE", [P, EXPERTS, QUARTERS * QW])
        W16 = WE[:, :, :].rearrange("p e n -> p (e n)").bitcast(f16).rearrange(
            "p (q a n) -> p q a n", q=QUARTERS * EXPERTS, a=2)
        W16e = W16.rearrange("p (e q) a n -> p e q a n", e=EXPERTS)
        half = DC * HID
        Wk_sb = WE[:, 2, 0:half].rearrange("p (c n) -> p c n", c=DC)
        Wv_sb = WE[:, 2, half:].rearrange("p (c n) -> p c n", c=DC)
        Wq_sb = WE[:, 3, 0:half].rearrange("p (c n) -> p c n", c=DC)
        Wo_sb = WE[:, 3, half:].rearrange("p (j n) -> p j n", j=JC)
        A = WE[:, B:2 * B, 0:half].rearrange("p b (c n) -> p c b n", c=DC)
        VO = WE[:, B:2 * B, half:].rearrange("p b (j n) -> p b j n", j=JC)
        stage = sb("stage", [P, 2, QW])

        X = sb("X", [P, TILES, D])
        XR = sb("XR", [P, TILES * D])
        VBD = XR[:, :].rearrange("p (j b h k) -> p j b h k", j=JC, b=B, h=2)
        XN2T = XR[:, :].rearrange("p (t n) -> p t n", t=TILES)
        b2_bc = XR[:, 0:EXPERTS * D].rearrange("p (e n) -> p e n", e=EXPERTS)
        AT = sb("AT", [P, 4 * HID])
        WqT = AT[:, 0:half].rearrange("p (j n) -> p j n", j=JC)
        KT = AT[:, half:].rearrange("p (j n) -> p j n", j=JC)
        E = AT[:, 0:2 * HID].rearrange("p (s n) -> p s n", s=2)
        PT = AT[:, 2 * HID:].rearrange("p (s j n) -> p s j n", s=2, j=JC)
        OH_lo = AT[:, 0:2048].bitcast(f16).rearrange("p (n m) -> p n m", m=P)
        RH = AT[:, 2048:2048 + PAIRS * 3 * MTILES // 2].bitcast(f16).rearrange("p (n a m) -> p n a m", a=3, m=MTILES)
        sm = AT[:, 3920:4080].rearrange("p (a t) -> p a t", t=TILES)
        assert PAIRS * P // 2 == 2048 and 2048 + PAIRS * 3 * MTILES // 2 <= 3920
        g16 = AT[:, 0:1024].bitcast(f16).rearrange("p (a j n) -> p a j n", a=2, j=HC)
        h32 = AT[:, 1024:2048]
        g32 = AT[:, 2048:3072].rearrange("p (j n) -> p j n", j=HC)
        ys = AT[:, 3072:3584].rearrange("p (s n) -> p s n", s=2)
        xs = AT[:, 3584:4096].rearrange("p (s n) -> p s n", s=2)
        F = AT[:, :].rearrange("p (t n) -> p t n", t=TILES)

        BUF = sb("BUF", [P, 2048])
        ctx_sb = BUF[:, 0:512].rearrange("p (t n) -> p t n", t=DC)
        cT = BUF[:, 512:1024].rearrange("p (c n) -> p c n", c=DC)
        xn2_b = [ctx_sb[:, s, :] for s in range(2)]
        xn2T_b = [cT[:, s, :].rearrange("p (c n) -> p c n", c=DC) for s in range(2)]
        xn_b = [BUF[:, 1024 + 256 * s:1280 + 256 * s] for s in range(2)]
        xnT_b = [BUF[:, 1536 + 256 * s:1792 + 256 * s].rearrange("p (c n) -> p c n", c=DC) for s in range(2)]
        eq_hi = BUF[:, 0:PAIRS * MTILES // 2].bitcast(f16).rearrange("p (n m) -> p n m", m=MTILES)
        cmp = BUF[0:1, 640:640 + MTILES * EXPERTS].rearrange("p (m e) -> p m e", e=EXPERTS)
        RT = [BUF[:, 1024 + 128 * n:1152 + 128 * n].rearrange("p (t e) -> p t e", e=EXPERTS) for n in range(5)]
        posi = BUF[:, 1664:1760].rearrange("p (a n) -> p a n", a=3).bitcast(i32)
        lohi = BUF[:, 1760:1824].rearrange("p (a n) -> p a n", a=2)
        cum = BUF[:, 1824:1888].rearrange("p (a n) -> p a n", a=4)
        iota_lo = BUF[:, 1888:1888 + P]
        cnti = BUF[:, 2016:2032].rearrange("p (a e) -> p a e", a=2).bitcast(i32)
        base8 = BUF[:, 2032:2040]

        R2 = sb("R2", [P, 1860])
        sW = R2[:, 0:512].rearrange("p (c n) -> p c n", c=DC)
        sb_row = R2[0:1, 512:768]
        tab = R2[:, 768:885].rearrange("p (a m) -> p a m", a=3)
        gidx = R2[:, 885:924].bitcast(i32)
        sidx = R2[:, 924:963].bitcast(i32)
        assert 3 * MTILES == 117
        xsT16 = R2[:, 964:1220].bitcast(f16).rearrange("p (a c n) -> p a c n", a=2, c=DC)
        res = R2[:, 1220:1732].rearrange("p (s n) -> p s n", s=2)
        b1_rows = R2[0:EXPERTS * HC, 1732:1732 + P]
        ident = sb("ident", [P, P])
        upper = sb("upper", [P, P], bf16)
        ones_b = sb("ones_b", [P, P], bf16)
        ones_row = sb("ones_row", [1, P])
        gW = sb("gW", [P, DC, EXPERTS])
        bo_bc = sb("bo_bc", [P, D])
        tgam = sb("tgam", [P, D])
        tbet = sb("tbet", [P, D])
        half_bc = sb("half_bc", [P, 1])
        tg = sb("tg", [P, 2])
        b1T = sb("b1T", [P, EXPERTS * HC])
        st = sb("st", [P, TILES, 6])
        mv = sb("mv", [P, TILES, 2])
        rstd = sb("rstd", [P, TILES])
        nmr = sb("nmr", [P, TILES])
        st2 = sb("st2", [P, 2, 6])
        mv2 = sb("mv2", [P, 2, 2])
        ve2 = sb("ve2", [P, 2])
        rs2 = sb("rs2", [P, 2, 2])
        mhalf = sb("mhalf", [P, TILES])
        mx = sb("mx", [P, 2, HEADS])
        rsum = sb("rsum", [P, 2, HEADS])
        rinv = sb("rinv", [P, 2, HEADS])
        M_bf = sb("M_bf", [P, TILES, EXPERTS], bf16)
        wtok = sb("wtok", [P, CHOICES, TILES])
        pos = sb("pos", [P, CHOICES, TILES])
        tokid = sb("tokid", [P, TILES])
        iota_m = sb("iota_m", [P, MTILES])
        rank8 = sb("rank8", [P, EXPERTS])
        pad_row = sb("pad_row", [P, 1])
        etf = sb("etf", [1, MTILES])
        etile = sb("etile", [1, MTILES], i32)
        w16 = sb("w16", [P, 2, CHOICES, TILES], f16)
        gslot = sb("gslot", [P, 2], i32)
        sslot = sb("sslot", [P, 2], i32)
        gcol = [gslot[:, s:s + 1] for s in range(2)]
        scol = [sslot[:, s:s + 1] for s in range(2)]

        PS = stack.enter_context(nc.psum_tensor("PS", [P, 8, BANK], f32))
        S_ps = [PS[:, 0, :], PS[:, 1, :]]
        PT_ps = [PS[:, 2, :], PS[:, 3, :]]
        O_ps = PS[:, 4, 0:D]
        xT_ps, x2T_ps = PS[:, 5, 0:D], PS[:, 6, D:2 * D]
        G_ps = PS[:, 6, 0:TILES * EXPERTS]
        rank_ps = PS[:, 7, 0:TILES * EXPERTS]
        cnt_ps = PS[:, 6, 256:256 + EXPERTS]
        tab_ps = PS[:, 7, 256:256 + 3 * MTILES]

        ld_ctx, ld_wk, ld_wq, ld_wv, ld_wo, ld_x, ld_small, ld_b2, ld_b1, ld_shared = [
            sem(n) for n in "ld_ctx ld_wk ld_wq ld_wv ld_wo ld_x ld_small ld_b2 ld_b1 ld_shared".split()]
        ldq = [sem(f"ldq{s}") for s in range(2)]
        hi_done, lo_done = sem("hi_done"), sem("lo_done")
        c_pool, c_ident, c_vbd, c_half = sem("c_pool"), sem("c_ident"), sem("c_vbd"), sem("c_half")
        pre_mm, pre_dve, pre_act = sem("pre_mm"), sem("pre_dve"), sem("pre_act")
        b1_mm, b1_ready = sem("b1_mm"), sem("b1_ready")
        tanh_ready, bo_ready, gb_ready = sem("tanh_ready"), sem("bo_ready"), sem("gb_ready")
        ln1_mv, ln1_ready = sem("ln1_mv"), sem("ln1_ready")
        s_mm, xT_mm, x2T_mm, pT_mm, o_mm, g_mm = [sem(n) for n in "s_mm xT_mm x2T_mm pT_mm o_mm g_mm".split()]
        xn_ready, xT_ready, exp_ready, pT_ready, xn2_ready, x2T_ready = [
            sem(n) for n in "xn_ready xT_ready exp_ready pT_ready xn2_ready x2T_ready".split()]
        mx_ready, shifted, sum_ready, rinv_ready, x2_ready, st2_ready, mv2_ready = [
            sem(n) for n in "mx_ready shifted sum_ready rinv_ready x2_ready st2_ready mv2_ready".split()]
        p_ready, bo_added, ve2_ready, pow2_ready, rstd2_ready = [
            sem(n) for n in "p_ready bo_added ve2_ready pow2_ready rstd2_ready".split()]
        st_xn2 = [sem(f"st_xn2_{s}") for s in range(2)]
        st_x2T = [sem(f"st_x2T_{s}") for s in range(2)]
        dchain, pchain = sem("dchain"), sem("pchain")
        z_mm, z_gelu, z_ready, x_beta = sem("z_mm"), sem("z_gelu"), sem("z_ready"), sem("x_beta")
        st_acc = [sem(f"st_acc{s}") for s in range(2)]
        pad_acc = sem("pad_acc")
        lg_ready, pexp_ready, M_ready, cnt_mm, rank_mm, oh_ready, tab_mm, route_ready = [
            sem(n) for n in "lg_ready pexp_ready M_ready cnt_mm rank_mm oh_ready tab_mm route_ready".split()]
        ga = [sem(f"ga{s}") for s in range(2)]
        sc = [sem(f"sc{s}") for s in range(2)]
        xsT_mm, h_mm, hT_mm, y_mm = [sem(n) for n in "xsT_mm h_mm hT_mm y_mm".split()]
        h_ready, y1_ready = sem("h_ready"), sem("y1_ready")
        xsTh_ready, gelu_done, gh_ready = sem("xsTh_ready"), sem("gelu_done"), sem("gh_ready")
        xsTl_ready, gl_ready, yb_ready, y_ready, gi_ready = [
            sem(n) for n in "xsTl_ready gl_ready yb_ready y_ready gi_ready".split()]
        ld_f = [sem(f"ld_f{k}") for k in range(B)]
        f_st, f_mv, f_norm, f_gam, f_rstd, f_ve, f_pow, f_out, st_out = [
            sem(n) for n in "f_st f_mv f_norm f_gam f_rstd f_ve f_pow f_out st_out".split()]

        dve_waits, pool_waits = sem("dve_waits"), sem("pool_waits")

        block = stack.enter_context(nc.Block())

        def wait(eng, s, value):
            if not isinstance(value, int) or value > 0:
                eng.wait_ge(s, value)

        def alone(eng, g, own):
            if not isinstance(g, int):
                eng.sem_inc(own, 1)

        def at(ap, i):
            if isinstance(i, int):
                return ap[:, i]
            one = ap[:, bass.ds(i, 1)]
            return one.rearrange("p o n -> p (o n)") if len(one.shape) == 3 else one

        def at4(ap, i):
            return ap[:, i] if isinstance(i, int) else ap[:, bass.ds(i, 1)].rearrange("p o a n -> p (o a) n")

        def batch_of(g, u):
            pair = g + u // 2
            b = pair // (TPB // 2)
            return b if isinstance(b, int) else b.with_bounds(min_val=0, max_val=B - 1)

        def col(ap, i):
            return ap[:, i:i + 1] if isinstance(i, int) else ap[:, bass.ds(i, 1)]

        x_t = x.rearrange("b (t p) d -> p (b t) d", p=P)
        out_t = out.rearrange("b (t p) d -> p (b t) d", p=P)
        xn2_rows = xn2_dram.rearrange("(t p) d -> p t d", p=P)
        acc_rows = acc_dram[0:TOKENS, :].rearrange("(t p) d -> p t d", p=P)

        def quarter_of(e, v):
            if v < DC:
                w = W1[:, P * v:P * (v + 1), :]
            else:
                w = W2[:, QW // D * P * (v - DC):QW // D * P * (v - DC + 1), :]
            one = w[e] if isinstance(e, int) else w[bass.ds(e, 1)].rearrange("o r n -> (o r) n")
            return one if v < DC else one.rearrange("(j p) n -> p j n", p=P)

        def stage_of(s, v):
            return stage[:, s, :] if v < DC else stage[:, s, :].rearrange("p (j n) -> p j n", n=D)

        def split_high(act, q, s):
            wait(act, ldq[s], 16 * (q // 2 + 1) if isinstance(q, int) else 16 * q[0])
            k = q if isinstance(q, int) else q[1]
            dst = W16[:, :, 0, :]
            act.activation(at(dst, k), stage[:, s, :], ACT.Copy, scale=W_SCALE).then_inc(hi_done, 1)

        def split_low(dve, q, s):
            k = q if isinstance(q, int) else q[1]
            wait(dve, hi_done, k + 1)
            dve.scalar_tensor_tensor(at(W16[:, :, 1, :], k), stage[:, s, :], W_SCALE, at(W16[:, :, 0, :], k),
                                     ALU.mult, ALU.subtract).then_inc(lo_done, 1)

        def step_quarters(i, g, u):
            if isinstance(i, int):
                first = QUARTERS * EARLY
                own = [first + 2 * i, first + 2 * i + 1] if i < 2 else []
                return own + ([first + QUARTERS + i - SPLIT_LEAD] if i >= SPLIT_LEAD else [])
            k = i + QUARTERS * (EARLY + 1) - SPLIT_LEAD
            return [(g + (QUARTERS * (EARLY + 1) - SPLIT_LEAD) // 2 + 1, k)]

        KT0, QT0, A0 = 1, 1 + JC // 2, 1 + JC
        VT0 = A0 + HEADS
        VO0 = VT0 + JC // 2
        GROUPS = VO0 + B * JC // 2
        SPLIT_FROM = GROUPS - 4 * QUARTERS * EARLY

        def evacuated(eng, n):
            wait(eng, pre_dve, n // 2 + 1)
            wait(eng, pre_act, (n + 1) // 2)

        A_PEEL_END = 14

        def attention_steps(eng, step):
            for i in range(4):
                step(i // 2, i % 2)
            with eng.Fori(2, A_PEEL_END // 2) as g:
                step(g, 0)
                step(g, 1)
            for i in range(A_PEEL_END, TILES + 2):
                step(i // 2, i % 2)

        M_PEEL_END = 36

        def mixture_steps(eng, step):
            for i in range(4):
                step(i // 2, i % 2)
            with eng.Fori(2, M_PEEL_END // 2) as g:
                step(g, 0)
                step(g, 1)
            for i in range(M_PEEL_END, MTILES + 1):
                step(i // 2, i % 2)

        @block.sync
        def _(sp):
            def load(q):
                e, v = divmod(q, QUARTERS)
                wait(sp, lo_done, q - 1)
                sp.dma_start(stage_of(q % 2, v), quarter_of(e, v)).then_inc(ldq[q % 2], 16)

            sp.dma_start(ctx_sb[:, :, :], ctx_in.rearrange("b k d -> (b k) d").rearrange("(t p) d -> p t d", p=P)
                         ).then_inc(ld_ctx, 16)
            sp.dma_start(Wk_sb, Wk.rearrange("(c p) n -> p c n", p=P)).then_inc(ld_wk, 16)
            sp.dma_start(Wq_sb, Wq.rearrange("(c p) n -> p c n", p=P)).then_inc(ld_wq, 16)
            for b in range(B):
                sp.dma_start(X[:, TPB * b:TPB * (b + 1), :], x_t[:, TPB * b:TPB * (b + 1), :]).then_inc(ld_x, 16)
            sp.dma_start(Wv_sb, Wv.rearrange("(c p) n -> p c n", p=P)).then_inc(ld_wv, 16)
            sp.dma_start(Wo_sb, Wo.rearrange("(j p) n -> p j n", p=P)).then_inc(ld_wo, 16)
            first = QUARTERS * (EARLY + 1)
            for q in range(first):
                load(q)

            with sp.Fori(0, B) as b:
                for v in range(QUARTERS):
                    wait(sp, lo_done, 4 * b + (first + v - 1))
                    sp.dma_start(stage_of(v % 2, v), quarter_of(b + (EARLY + 1), v)).then_inc(ldq[v % 2], 16)
                    i = b * TPB + v
                    wait(sp, xn2_ready, i + 1)
                    sp.dma_start(at(xn2_rows, i), xn2_b[v % 2]).then_inc(st_xn2[v % 2], 16)
                    wait(sp, x2T_ready, i + 1)
                    sp.dma_start(at(XN2T, i), xn2T_b[v % 2][:, :, :].rearrange("p c n -> p (c n)")
                                 ).then_inc(st_x2T[v % 2], 16)
            for q in range(QUARTERS * (EXPERTS - 1), QUARTERS * EXPERTS - 2):
                load(q)
            for t in range(2):
                sp.wait_ge(z_ready, t + 1)
                sp.dma_start(acc_rows[:, t, :], res[:, t % 2]).then_inc(st_acc[t % 2], 16)
            for q in range(QUARTERS * EXPERTS - 2, QUARTERS * EXPERTS):
                load(q)
            for t in range(2, TILES):
                sp.wait_ge(z_ready, t + 1)
                sp.dma_start(acc_rows[:, t, :], res[:, t % 2]).then_inc(st_acc[t % 2], 16)
            sp.wait_ge(z_mm, TILES)
            sp.dma_start(b2_bc, b2.rearrange("e n -> (e n)").partition_broadcast(P)
                         .rearrange("p (e n) -> p e n", e=EXPERTS)).then_inc(ld_b2, 16)
            for s in range(2):
                sp.wait_ge(sc[s], 16 * ((MTILES - s + 1) // 2))
            for k in range(B):
                sp.dma_start(F[:, TPB * k:TPB * (k + 1), :], acc_rows[:, TPB * k:TPB * (k + 1), :]
                             ).then_inc(ld_f[k], 16)
            for k in range(B):
                sp.wait_ge(f_out, k + 1)
                sp.dma_start(out_t[:, TPB * k:TPB * (k + 1), :], X[:, TPB * k:TPB * (k + 1), :]
                             ).then_inc(st_out, 16)
            sp.wait_ge(st_out, 16 * B)
            sp.wait_ge(pad_acc, 16)

        @block.gpsimd
        def _(pool):
            pool.memset(ident[:, :], 0.0).then_inc(c_pool, 1)
            pool.memset(upper[:, :], 1.0).then_inc(c_pool, 1)
            pool.memset(ones_b[:, :], 1.0).then_inc(c_pool, 1)
            pool.memset(ones_row[:, :], 1.0).then_inc(c_pool, 1)
            pool.memset(half_bc[:, :], 0.5).then_inc(c_pool, 1)
            pool.memset(mhalf[:, :], -0.5).then_inc(c_half, 1)
            pool.wait_ge(c_pool, 5)
            pool.affine_select(out=ident[:, :], in_=ident[:, :], compare_op=ALU.not_equal, fill=1.0, base=0,
                               pattern=[[-1, P]], channel_multiplier=1).then_inc(c_ident, 1)
            pool.affine_select(out=upper[:, :], in_=upper[:, :], compare_op=ALU.is_gt, fill=0.0, base=0,
                               pattern=[[1, P]], channel_multiplier=-1).then_inc(c_pool, 1)
            pool.memset(XR[:, :], 0.0).then_inc(c_vbd, 1)
            pool.iota(tokid[:, :], pattern=[[P, TILES]], base=1, channel_multiplier=1,
                      allow_small_or_imprecise_dtypes=True).then_inc(c_pool, 1)
            pool.iota(iota_m[:, :], pattern=[[1, MTILES]], base=0, channel_multiplier=0,
                      allow_small_or_imprecise_dtypes=True).then_inc(c_pool, 1)
            pool.iota(rank8[:, :], pattern=[[-1, EXPERTS]], base=EXPERTS, channel_multiplier=0,
                      allow_small_or_imprecise_dtypes=True).then_inc(c_pool, 1)
            pool.iota(pad_row[:, :], pattern=[[0, 1]], base=TOKENS + 1, channel_multiplier=1,
                      allow_small_or_imprecise_dtypes=True).then_inc(c_pool, 1)
            pool.wait_ge(tanh_ready, 1)
            pool.wait_ge(ld_small, 16 * 6)
            pool.tensor_scalar(bo_bc[:, :], bo_bc[:, :], tg[:, 0:1], None, ALU.mult).then_inc(bo_ready, 1)
            pool.tensor_scalar(tgam[:, :], tgam[:, :], tg[:, 1:2], None, ALU.mult).then_inc(gb_ready, 1)
            pool.tensor_scalar(tbet[:, :], tbet[:, :], tg[:, 1:2], None, ALU.mult).then_inc(gb_ready, 1)
            pool.wait_ge(ln1_mv, 1)
            pool.wait_ge(c_half, 1)
            pool.tensor_tensor(rstd[:, :], nmr[:, :], mhalf[:, :], ALU.pow).then_inc(pchain, 1)
            pool.wait_ge(pchain, 1)
            pool.tensor_tensor(nmr[:, :], mv[:, :, 0], rstd[:, :], ALU.mult).then_inc(pchain, 1)
            pool.wait_ge(pchain, 2)
            pool.tensor_scalar(nmr[:, :], nmr[:, :], -1.0, None, ALU.mult).then_inc(ln1_ready, 1)
            pool.wait_ge(bo_ready, 1)

            def step(g, u):
                i = 2 * g + u
                static = isinstance(i, int)
                if not static or i < TILES:
                    wait(pool, xn_ready, i + 1)
                    pool.tensor_tensor(at(X, i), at(X, i), bo_bc[:, :], ALU.add).then_inc(bo_added, 1)
                    for h in range(2):
                        wait(pool, rinv_ready, 2 * i + h + 1)
                        w = E[:, u, BANK * h:BANK * (h + 1)].rearrange("p (a k) -> p a k", k=NCTX)
                        r = rinv[:, u, 8 * h:8 * h + 8].unsqueeze(2).to_broadcast([P, 8, NCTX])
                        pool.tensor_tensor(w, w, r, ALU.mult).then_inc(p_ready, 1)
                if not static or 1 <= i <= TILES:
                    v = 1 - u
                    wait(pool, mv2_ready, i)
                    alone(pool, g, pool_waits)
                    pool.tensor_scalar(ve2[:, v:v + 1], mv2[:, v, 1:2], LN_EPS, None, ALU.add
                                       ).then_inc(ve2_ready, 1)
                    wait(pool, ve2_ready, i)
                    wait(pool, xn2_ready, i - 2)
                    pool.tensor_tensor(rs2[:, v, 0:1], ve2[:, v:v + 1], mhalf[:, 0:1], ALU.pow
                                       ).then_inc(pow2_ready, 1)
                    wait(pool, pow2_ready, i)
                    alone(pool, g, pool_waits)
                    pool.tensor_scalar(rs2[:, v, 1:2], mv2[:, v, 0:1], rs2[:, v, 0:1], -1.0, ALU.mult, ALU.mult
                                       ).then_inc(rstd2_ready, 1)

            attention_steps(pool, step)

            pool.wait_ge(o_mm, TILES)
            pool.iota(iota_lo[:, :], pattern=[[1, P]], base=0, channel_multiplier=0,
                      allow_small_or_imprecise_dtypes=True).then_inc(c_pool, 1)
            pool.memset(cum[:, :, :], 0.0).then_inc(c_pool, 1)
            pool.wait_ge(gb_ready, 2)
            pool.wait_ge(x2_ready, TILES)
            pool.wait_ge(mv2_ready, TILES)

            for t in range(TILES):
                pool.wait_ge(z_gelu, t + 1)
                pool.tensor_tensor(res[:, t % 2], res[:, t % 2], half_bc[:, :].to_broadcast([P, D]), ALU.mult
                                   ).then_inc(z_ready, 1)
                if t % TPB == TPB - 1:
                    k = t // TPB
                    part = X[:, TPB * k:TPB * (k + 1), :]
                    pool.wait_ge(xn2_ready, TILES)
                    pool.tensor_tensor(part, part, tbet[:, :].unsqueeze(1).to_broadcast([P, TPB, D]), ALU.add
                                       ).then_inc(x_beta, 1)
            pool.wait_ge(st_acc[0], 16 * (TILES // 2))
            pool.wait_ge(st_acc[1], 16 * (TILES // 2))
            pool.memset(res[:, 0, 0:D], 0.0).then_inc(pchain, 1)
            pool.wait_ge(pchain, 3)
            pool.dma_start(acc_dram[TOKENS:TOKENS + P, :], res[:, 0, 0:D]).then_inc(pad_acc, 16)
            for s in range(2):
                pool.wait_ge(st_xn2[s], 16 * TILES // 2)

            def gather(g, u):
                i = 2 * g + u
                wait(pool, gi_ready, i + 1)
                wait(pool, xsT_mm, i - 1)
                alone(pool, g, pool_waits)
                pool.indirect_dma_start(xs[:, u, :], None, xn2_dram,
                                        bass.IndirectOffsetOnAxis(ap=gcol[u], axis=0)).then_inc(ga[u], 16)

            gather(0, 0)
            gather(0, 1)
            pool.wait_ge(pad_acc, 16)

            def mix(g, u):
                i = 2 * g + u
                static = isinstance(i, int)
                if not static or i + 2 < MTILES:
                    gather(g + 1, u)
                if not static or i >= 1:
                    s = 1 - u
                    wait(pool, y_ready, i)
                    wait(pool, sc[u], 16 * g)
                    alone(pool, g, pool_waits)
                    pool.indirect_dma_start(acc_dram, bass.IndirectOffsetOnAxis(ap=scol[s], axis=0), ys[:, s, :],
                                            None, compute_op=ALU.add).then_inc(sc[s], 16)

            mixture_steps(pool, mix)

            for k in range(B):
                tiles = slice(TPB * k, TPB * (k + 1))
                pool.wait_ge(f_mv, k + 1)
                pool.tensor_scalar(nmr[:, tiles], mv[:, tiles, 1], LN_EPS, None, ALU.add).then_inc(f_ve, 1)
                pool.wait_ge(f_ve, k + 1)
                pool.tensor_tensor(rstd[:, tiles], nmr[:, tiles], mhalf[:, 0:TPB], ALU.pow).then_inc(f_pow, 1)
                pool.wait_ge(f_pow, 2 * k + 1)
                pool.tensor_tensor(nmr[:, tiles], mv[:, tiles, 0], rstd[:, tiles], ALU.mult).then_inc(f_pow, 1)
                pool.wait_ge(f_pow, 2 * k + 2)
                pool.tensor_scalar(nmr[:, tiles], nmr[:, tiles], -1.0, None, ALU.mult).then_inc(f_rstd, 1)
                if k >= 1:
                    last = slice(TPB * (k - 1), TPB * k)
                    pool.wait_ge(f_gam, k)
                    pool.tensor_tensor(X[:, last, :], X[:, last, :], F[:, last, :], ALU.add).then_inc(f_out, 1)
            last = slice(TPB * (B - 1), TPB * B)
            pool.wait_ge(f_gam, B)
            pool.tensor_tensor(X[:, last, :], X[:, last, :], F[:, last, :], ALU.add).then_inc(f_out, 1)

        @block.scalar
        def _(act):
            act.dma_start(tg[:, 0:1], g_xattn.partition_broadcast(P)).then_inc(ld_small, 16)
            act.dma_start(tg[:, 1:2], g_ffn.partition_broadcast(P)).then_inc(ld_small, 16)
            act.dma_start(gW[:, :, :], gate_W.rearrange("(c p) n -> p c n", p=P)).then_inc(ld_small, 16)
            act.dma_start(bo_bc[:, :], bo.partition_broadcast(P)).then_inc(ld_small, 16)
            act.dma_start(tgam[:, :], gamma.partition_broadcast(P)).then_inc(ld_small, 16)
            act.dma_start(tbet[:, :], beta.partition_broadcast(P)).then_inc(ld_small, 16)
            act.dma_start(b1_rows[:, :], b1.rearrange("e (j p) -> (e j) p", p=P)).then_inc(ld_b1, 16)
            act.dma_start(sW[:, :, :], shared_W.rearrange("(c p) n -> p c n", p=P)).then_inc(ld_shared, 16)
            act.dma_start(sb_row[:, :], shared_b.rearrange("(a n) -> a n", a=1)).then_inc(ld_shared, 16)

            for n in range(1, GROUPS, 2):
                act.wait_ge(pre_mm, n + 1)
                bank = PS[:, n % 8, :]
                if n < QT0:
                    j = 2 * (n - KT0)
                    m = act.activation(KT[:, j:j + 2, :].rearrange("p j n -> p (j n)"), bank, ACT.Copy, scale=SCALE)
                elif n < A0:
                    j = 2 * (n - QT0)
                    m = act.activation(WqT[:, j:j + 2, :].rearrange("p j n -> p (j n)"), bank, ACT.Copy)
                elif n < VT0:
                    h = n - A0
                    for c in range(DC):
                        m = act.activation(A[:, c, :, NCTX * h:NCTX * (h + 1)],
                                           bank[:, D * c:D * (c + 1)].rearrange("p (b k) -> p b k", b=B), ACT.Copy)
                elif n < VO0:
                    j = 2 * (n - VT0)
                    act.wait_ge(c_vbd, 1)
                    for s in range(2):
                        for jj in range(2):
                            m = act.activation(VBD[DH * s:DH * (s + 1), j + jj, :, s, :],
                                               bank[DH * s:DH * (s + 1), D * jj:D * (jj + 1)].rearrange(
                                                   "p (b k) -> p b k", b=B), ACT.Copy)
                else:
                    b, j = divmod(2 * (n - VO0), JC)
                    m = act.activation(VO[:, b, j:j + 2, :].rearrange("p j n -> p (j n)"), bank, ACT.Copy)
                m.then_inc(pre_act, 1)
                if n == QT0 + 2:
                    act.wait_ge(ld_small, 16 * 6)
                    act.activation(tg[:, :], tg[:, :], ACT.Tanh).then_inc(tanh_ready, 1)
                if n >= SPLIT_FROM and (n - SPLIT_FROM) % 4 in (0, 1) and (n - SPLIT_FROM) // 4 < QUARTERS * EARLY:
                    q = (n - SPLIT_FROM) // 4
                    split_high(act, q, q % 2)
            act.wait_ge(b1_mm, 1)
            act.activation(b1T[:, :], PS[:, 7, 0:EXPERTS * HC], ACT.Copy).then_inc(b1_ready, 1)

            act.wait_ge(ln1_ready, 1)

            def ln1(i, s):
                wait(act, xT_mm, i - 1)
                act.activation(xn_b[s][:, :], at(X, i), ACT.Identity, bias=col(nmr, i), scale=col(rstd, i)
                               ).then_inc(xn_ready, 1)

            def xT_evac(i, s):
                wait(act, xT_mm, i + 1)
                wait(act, s_mm, 2 * (i - 1))
                act.activation(xnT_b[s][:, :, :].rearrange("p c n -> p (c n)"), xT_ps, ACT.Copy
                               ).then_inc(xT_ready, 1)

            ln1(0, 0)
            xT_evac(0, 0)
            ln1(1, 1)

            def step(g, u):
                i = 2 * g + u
                v = 1 - u
                static = isinstance(i, int)
                scores = not static or i < TILES
                if not static or i >= 2:
                    wait(act, rstd2_ready, i - 1)
                    wait(act, st_xn2[u], 16 * (g - 1))
                    act.activation(xn2_b[u], at(X, i - 2), ACT.Identity, bias=rs2[:, u, 1:2],
                                   scale=rs2[:, u, 0:1]).then_inc(xn2_ready, 1)
                if not static or 1 <= i <= TILES:
                    for h in range(2):
                        wait(act, pT_mm, 2 * i - 2 + h + 1)
                        wait(act, o_mm, i - 2)
                        act.activation(PT[:, v, 4 * h:4 * h + 4, :].rearrange("p j n -> p (j n)"), PT_ps[h],
                                       ACT.Copy).then_inc(pT_ready, 1)
                if scores:
                    wait(act, shifted, 2 * i + 1)
                    act.activation(E[:, u, 0:BANK], E[:, u, 0:BANK], ACT.Exp).then_inc(exp_ready, 1)
                if not static or i + 1 < TILES:
                    xT_evac(i + 1, v)
                if not static or i >= 2:
                    wait(act, x2T_mm, i - 1)
                    wait(act, st_x2T[u], 16 * (g - 1))
                    wait(act, g_mm, i - 3 if static else 0)
                    act.activation(xn2T_b[u][:, :, :].rearrange("p c n -> p (c n)"), x2T_ps, ACT.Copy
                                   ).then_inc(x2T_ready, 1)
                if scores:
                    wait(act, shifted, 2 * i + 2)
                    act.activation(E[:, u, BANK:], E[:, u, BANK:], ACT.Exp).then_inc(exp_ready, 1)
                for q in step_quarters(i, g, u):
                    split_high(act, q, u if not static or i >= SPLIT_LEAD else q % 2)
                if not static or i + 2 < TILES:
                    ln1(i + 2, u)

            attention_steps(act, step)

            act.wait_ge(lg_ready, 1)
            act.activation(RT[0], RT[0], ACT.Exp).then_inc(pexp_ready, 1)
            for t in range(TILES):
                if t in (0, 1, 6, 7):
                    q = QUARTERS * (EXPERTS - 1) + (t if t < 2 else t - 4)
                    split_high(act, q, q % 2)
                act.wait_ge(z_mm, t + 1)
                if t >= 2:
                    act.wait_ge(st_acc[t % 2], 16 * (t // 2))
                act.activation(res[:, t % 2], PS[:, t % 4, 0:D], ACT.Gelu).then_inc(z_gelu, 1)
            act.wait_ge(route_ready, 1)
            act.wait_ge(b1_ready, 1)

            def rows_high(i):
                wait(act, xsT_mm, i + 1)
                wait(act, h_mm, 2 * i)
                act.activation(xsT16[:, 0].rearrange("p c n -> p (c n)"), PS[:, 5, 0:D], ACT.Copy
                               ).then_inc(xsTh_ready, 1)

            rows_high(0)

            def mix(g, u):
                i = 2 * g + u
                static = isinstance(i, int)

                def hidden(h):
                    wait(act, hT_mm, 2 * i + h + 1)
                    wait(act, gl_ready, 2 * i - 2 + h + 1)
                    for j in range(4 * h, 4 * h + 4):
                        m = act.activation(g32[:, j, :], PS[:, 2 + h, P * (j % 4):P * (j % 4 + 1)], ACT.Gelu,
                                           bias=b1T[:, bass.ds(e * HC + j, 1)], scale=1 / W_SCALE)
                    m.then_inc(gelu_done, 1)
                    wait(act, gelu_done, 2 * i + h + 1)
                    wait(act, y_mm, i)
                    act.activation(g16[:, 0, 4 * h:4 * h + 4, :].rearrange("p j n -> p (j n)"),
                                   g32[:, 4 * h:4 * h + 4, :].rearrange("p j n -> p (j n)"), ACT.Copy,
                                   scale=H_SCALE).then_inc(gh_ready, 1)

                if not static or i < MTILES:
                    e = act.value_load(col(etile, i), min_val=0, max_val=EXPERTS - 1)
                if not static or i + 1 < MTILES:
                    rows_high(i + 1)
                if not static or i < MTILES:
                    hidden(0)
                    hidden(1)

            mixture_steps(act, mix)

            for k in range(B):
                act.wait_ge(f_rstd, k + 1)
                for t in range(TPB * k, TPB * (k + 1)):
                    m = act.activation(F[:, t, :], F[:, t, :], ACT.Identity, bias=nmr[:, t:t + 1],
                                       scale=rstd[:, t:t + 1])
                m.then_inc(f_norm, 1)

        @block.vector
        def _(dve):
            chain = [0]

            def link(ins):
                chain[0] += 1
                ins.then_inc(dchain, 1)
                dve.wait_ge(dchain, chain[0])

            def evac(n):
                dve.wait_ge(pre_mm, n + 1)
                bank = PS[:, n % 8, :]
                if n == 0:
                    m = dve.tensor_copy(cT[:, :, :].rearrange("p c n -> p (c n)"), bank)
                elif n < QT0:
                    j = 2 * (n - KT0)
                    m = dve.tensor_scalar(KT[:, j:j + 2, :].rearrange("p j n -> p (j n)"), bank, SCALE, None,
                                          ALU.mult)
                elif n < A0:
                    j = 2 * (n - QT0)
                    m = dve.tensor_copy(WqT[:, j:j + 2, :].rearrange("p j n -> p (j n)"), bank)
                elif n < VT0:
                    h = n - A0
                    for c in range(DC):
                        m = dve.tensor_copy(A[:, c, :, NCTX * h:NCTX * (h + 1)],
                                            bank[:, D * c:D * (c + 1)].rearrange("p (b k) -> p b k", b=B))
                elif n < VO0:
                    j = 2 * (n - VT0)
                    dve.wait_ge(c_vbd, 1)
                    for s in range(2):
                        for jj in range(2):
                            m = dve.tensor_copy(VBD[DH * s:DH * (s + 1), j + jj, :, s, :],
                                                bank[DH * s:DH * (s + 1), D * jj:D * (jj + 1)].rearrange(
                                                    "p (b k) -> p b k", b=B))
                else:
                    b, j = divmod(2 * (n - VO0), JC)
                    m = dve.tensor_copy(VO[:, b, j:j + 2, :].rearrange("p j n -> p (j n)"), bank)
                m.then_inc(pre_dve, 1)

                if n >= SPLIT_FROM and (n - SPLIT_FROM) % 4 in (0, 1) and (n - SPLIT_FROM) // 4 < QUARTERS * EARLY:
                    q = (n - SPLIT_FROM) // 4
                    split_low(dve, q, q % 2)

            for n in range(0, A0, 2):
                evac(n)
            dve.wait_ge(ld_x, 16 * B)
            for t in range(TILES):
                m = dve.bn_stats(st[:, t, :], X[:, t, :])
            link(m)
            for t in range(TILES):
                m = dve.bn_aggr(mv[:, t, :], st[:, t, :])
            link(m)
            dve.tensor_scalar(nmr[:, :], mv[:, :, 1], LN_EPS, None, ALU.add).then_inc(ln1_mv, 1)
            for n in range(A0 + A0 % 2, GROUPS, 2):
                evac(n)
            dve.wait_ge(tanh_ready, 1)

            def step(g, u):
                i = 2 * g + u
                v = 1 - u
                static = isinstance(i, int)
                if not static or i < TILES:
                    for h in range(2):
                        s = S_ps[h].rearrange("p (a k) -> p a k", k=NCTX)
                        m8 = mx[:, u, 8 * h:8 * h + 8]
                        wait(dve, s_mm, 2 * i + h + 1)
                        dve.tensor_reduce(m8, s, AX, ALU.max).then_inc(mx_ready, 1)
                        wait(dve, mx_ready, 2 * i + h + 1)
                        wait(dve, pT_mm, 2 * i - 4 + h + 1)
                        dve.tensor_tensor(E[:, u, BANK * h:BANK * (h + 1)].rearrange("p (a k) -> p a k", k=NCTX), s,
                                          m8.unsqueeze(2).to_broadcast([P, 8, NCTX]), ALU.subtract
                                          ).then_inc(shifted, 1)
                    for h in range(2):
                        wait(dve, exp_ready, 2 * i + h + 1)
                        r8 = rsum[:, u, 8 * h:8 * h + 8]
                        dve.tensor_reduce(r8, E[:, u, BANK * h:BANK * (h + 1)].rearrange("p (a k) -> p a k", k=NCTX),
                                          AX, ALU.add).then_inc(sum_ready, 1)
                        wait(dve, sum_ready, 2 * i + h + 1)
                        wait(dve, p_ready, 2 * i - 4 + h + 1)
                        dve.reciprocal(rinv[:, u, 8 * h:8 * h + 8], r8).then_inc(rinv_ready, 1)
                if not static or 1 <= i <= TILES:
                    wait(dve, o_mm, i)
                    wait(dve, bo_added, i)
                    dve.scalar_tensor_tensor(at(X, i - 1), O_ps, tg[:, 0:1], at(X, i - 1), ALU.mult, ALU.add
                                             ).then_inc(x2_ready, 1)
                    wait(dve, x2_ready, i)
                    alone(dve, g, dve_waits)
                    dve.bn_stats(st2[:, v, :], at(X, i - 1)).then_inc(st2_ready, 1)
                    wait(dve, st2_ready, i)
                    wait(dve, rstd2_ready, i - 2)
                    alone(dve, g, dve_waits)
                    dve.bn_aggr(mv2[:, v, :], st2[:, v, :]).then_inc(mv2_ready, 1)
                for q in step_quarters(i, g, u):
                    split_low(dve, q, u if not static or i >= SPLIT_LEAD else q % 2)

            attention_steps(dve, step)

            TE = [P, TILES, EXPERTS]
            L = G_ps.rearrange("p (t e) -> p t e", e=EXPERTS)
            prob, oh1, oh2, tmp, tmp2 = RT[0], RT[1], RT[2], RT[3], RT[4]
            lmax, ssum, sinv, m1, m2, c1, c2, den = [sm[:, n, :] for n in range(8)]
            r8 = rank8[:, :].unsqueeze(1).to_broadcast(TE)

            def per_token(a):
                return a.unsqueeze(2).to_broadcast(TE)

            dve.wait_ge(g_mm, TILES)
            dve.wait_ge(c_pool, 12)
            link(dve.tensor_reduce(lmax, L, AX, ALU.max))
            dve.tensor_tensor(prob, L, per_token(lmax), ALU.subtract).then_inc(lg_ready, 1)
            dve.wait_ge(pexp_ready, 1)
            link(dve.tensor_reduce(ssum, prob, AX, ALU.add))
            link(dve.reciprocal(sinv, ssum))
            link(dve.tensor_tensor(prob, prob, per_token(sinv), ALU.mult))

            def largest(p, m, c, oh):
                link(dve.tensor_reduce(m, p, AX, ALU.max))
                link(dve.tensor_tensor(tmp, p, per_token(m), ALU.is_equal))
                link(dve.tensor_tensor(tmp, tmp, r8, ALU.mult))
                link(dve.tensor_reduce(c, tmp, AX, ALU.max))
                link(dve.tensor_tensor(oh, r8, per_token(c), ALU.is_equal))

            largest(prob, m1, c1, oh1)
            link(dve.scalar_tensor_tensor(tmp2, oh1, -2.0, prob, ALU.mult, ALU.add))
            largest(tmp2, m2, c2, oh2)
            dve.tensor_tensor(M_bf[:, :, :], oh1, oh2, ALU.add).then_inc(M_ready, 1)
            link(dve.tensor_tensor(den, m1, m2, ALU.add))
            link(dve.reciprocal(sinv, den))
            dve.tensor_tensor(wtok[:, 0, :], m1, sinv, ALU.mult)
            link(dve.tensor_tensor(wtok[:, 1, :], m2, sinv, ALU.mult))
            link(dve.tensor_copy(w16[:, 0], wtok[:, :, :]))
            link(dve.tensor_tensor(w16[:, 1], wtok[:, :, :], w16[:, 0], ALU.subtract))
            last = QUARTERS * (EXPERTS - 1)
            split_low(dve, last, 0)
            split_low(dve, last + 1, 1)
            dve.wait_ge(cnt_mm, 1)
            link(dve.tensor_scalar(cnti[:, 0, :], cnt_ps, float(P - 1), None, ALU.add))
            link(dve.tensor_scalar(cnti[:, 1, :], cnti[:, 0, :], 7, None, ALU.logical_shift_right))
            link(dve.tensor_copy(cum[:, 0, EXPERTS:], cnti[:, 1, :]))
            for n in range(3):
                link(dve.tensor_tensor(cum[:, n + 1, EXPERTS:], cum[:, n, EXPERTS:],
                                       cum[:, n, EXPERTS - 2 ** n:2 * EXPERTS - 2 ** n], ALU.add))
            first = cum[:, 3, EXPERTS - 1:2 * EXPERTS - 1]
            link(dve.tensor_scalar(base8[:, :], first, float(P), None, ALU.mult))
            dve.wait_ge(rank_mm, 1)
            link(dve.tensor_tensor(tmp, rank_ps.rearrange("p (t e) -> p t e", e=EXPERTS),
                                   base8[:, :].unsqueeze(1).to_broadcast(TE), ALU.add))
            for k, oh in ((0, oh1), (1, oh2)):
                link(dve.tensor_tensor(tmp2, tmp, oh, ALU.mult))
                link(dve.tensor_reduce(pos[:, k, :], tmp2, AX, ALU.add))
            link(dve.tensor_copy(posi[:, 0, :], pos[:, :, :].rearrange("p k t -> p (k t)")))
            dve.tensor_scalar(posi[:, 1, :], posi[:, 0, :], P - 1, None, ALU.bitwise_and)
            link(dve.tensor_scalar(posi[:, 2, :], posi[:, 0, :], 7, None, ALU.logical_shift_right))
            link(dve.tensor_copy(lohi[:, :, :], posi[:, 1:3, :]))
            for s in range(2):
                dve.wait_ge(st_xn2[s], 16 * TILES // 2)
                dve.wait_ge(st_x2T[s], 16 * TILES // 2)
            PM = [P, PAIRS, MTILES]
            link(dve.tensor_tensor(eq_hi, iota_m[:, :].unsqueeze(1).to_broadcast(PM),
                                   lohi[:, 1, :].unsqueeze(2).to_broadcast(PM), ALU.is_equal))
            for k in range(CHOICES):
                n = slice(TILES * k, TILES * (k + 1))
                TM = [P, TILES, MTILES]
                dve.tensor_tensor(RH[:, n, 0, :], eq_hi[:, n, :], tokid[:, :].unsqueeze(2).to_broadcast(TM),
                                  ALU.mult)
                for a in range(2):
                    dve.tensor_tensor(RH[:, n, 1 + a, :], eq_hi[:, n, :],
                                      w16[:, a, k, :].unsqueeze(2).to_broadcast(TM), ALU.mult)
            for n in range(0, PAIRS, 8):
                NM = [P, 8, P]
                dve.tensor_tensor(OH_lo[:, n:n + 8, :], iota_lo[:, :].unsqueeze(1).to_broadcast(NM),
                                  lohi[:, 0, n:n + 8].unsqueeze(2).to_broadcast(NM), ALU.is_equal
                                  ).then_inc(oh_ready, 1)
            ME = [1, MTILES, EXPERTS]
            link(dve.tensor_tensor(cmp[:, :, :], iota_m[0:1, :].unsqueeze(2).to_broadcast(ME),
                                   first[0:1, :].unsqueeze(1).to_broadcast(ME), ALU.is_ge))
            link(dve.tensor_reduce(etf[:, :], cmp[:, :, :], AX, ALU.add))
            link(dve.tensor_scalar(etile[:, :], etf[:, :], -1.0, None, ALU.add))
            split_low(dve, last + 2, 0)
            split_low(dve, last + 3, 1)
            dve.wait_ge(tab_mm, 1)
            link(dve.tensor_copy(tab[:, :, :].rearrange("p a m -> p (a m)"), tab_ps))
            link(dve.tensor_tensor(tab[:, 1, :], tab[:, 1, :], tab[:, 2, :], ALU.add))
            dve.tensor_scalar(gidx[:, :], tab[:, 0, :], -1.0, 0.0, ALU.add, ALU.max)
            link(dve.tensor_scalar(tab[:, 2, :], tab[:, 0, :], 0.0, None, ALU.is_equal))
            link(dve.scalar_tensor_tensor(tab[:, 2, :], tab[:, 2, :], pad_row[:, :], tab[:, 0, :], ALU.mult,
                                          ALU.add))
            dve.tensor_scalar(sidx[:, :], tab[:, 2, :], -1.0, None, ALU.add).then_inc(route_ready, 1)
            dve.wait_ge(route_ready, 1)

            def token_numbers(i, s, r):
                wait(dve, ga[s], 16 * r)
                dve.tensor_copy(gcol[s], col(gidx, i)).then_inc(gi_ready, 1)

            def rows_low(i):
                wait(dve, xsTh_ready, i + 1)
                dve.tensor_tensor(xsT16[:, 1].rearrange("p c n -> p (c n)"), PS[:, 5, 0:D],
                                  xsT16[:, 0].rearrange("p c n -> p (c n)"), ALU.subtract).then_inc(xsTl_ready, 1)

            token_numbers(0, 0, 0)
            token_numbers(1, 1, 0)
            rows_low(0)
            dve.wait_ge(ld_b2, 16)

            def mix(g, u):
                i = 2 * g + u
                static = isinstance(i, int)

                def hidden_low(h):
                    wait(dve, gh_ready, 2 * i + h + 1)
                    part = slice(4 * h, 4 * h + 4)
                    dve.scalar_tensor_tensor(g16[:, 1, part, :].rearrange("p j n -> p (j n)"),
                                             g32[:, part, :].rearrange("p j n -> p (j n)"), H_SCALE,
                                             g16[:, 0, part, :].rearrange("p j n -> p (j n)"), ALU.mult,
                                             ALU.subtract).then_inc(gl_ready, 1)

                if not static or i + 2 < MTILES:
                    token_numbers(i + 2, u, g + 1)
                if not static or i < MTILES:
                    for h in range(2):
                        wait(dve, h_mm, 2 * i + h + 1)
                        wait(dve, hT_mm, 2 * i - 2 + h + 1)
                        dve.tensor_copy(h32[:, BANK * h:BANK * (h + 1)], PS[:, h, :]).then_inc(h_ready, 1)
                if not static or i + 1 < MTILES:
                    rows_low(i + 1)
                if not static or i >= 1:
                    s = 1 - u
                    e = dve.value_load(col(etile, i - 1), min_val=0, max_val=EXPERTS - 1)
                    wait(dve, y_mm, i)
                    wait(dve, sc[s], 16 * (g - s))
                    dve.scalar_tensor_tensor(ys[:, s, :], PS[:, 4, 0:D], 1 / (W_SCALE * H_SCALE), at(b2_bc, e),
                                             ALU.mult, ALU.add).then_inc(y1_ready, 1)
                    dve.tensor_copy(scol[s], col(sidx, i - 1))
                    wait(dve, y1_ready, i)
                    dve.scalar_tensor_tensor(ys[:, s, :], PS[:, 4, D:2 * D], 1 / (W_SCALE * H_SCALE), ys[:, s, :],
                                             ALU.mult, ALU.add).then_inc(yb_ready, 1)
                    wait(dve, yb_ready, i)
                    dve.tensor_scalar(ys[:, s, :], ys[:, s, :], col(tab[:, 1, :], i - 1), None, ALU.mult
                                      ).then_inc(y_ready, 1)
                if not static or i < MTILES:
                    hidden_low(0)
                    hidden_low(1)

            mixture_steps(dve, mix)

            def gain(k):
                part = F[:, TPB * k:TPB * (k + 1), :]
                dve.wait_ge(f_norm, k + 1)
                dve.tensor_tensor(part, part, tgam[:, :].unsqueeze(1).to_broadcast([P, TPB, D]), ALU.mult
                                  ).then_inc(f_gam, 1)

            for k in range(B):
                dve.wait_ge(ld_f[k], 16)
                for t in range(TPB * k, TPB * (k + 1)):
                    m = dve.bn_stats(st[:, t, :], F[:, t, :])
                link(m)
                for t in range(TPB * k, TPB * (k + 1)):
                    m = dve.bn_aggr(mv[:, t, :], st[:, t, :])
                m.then_inc(f_mv, 1)
                if k >= 1:
                    gain(k - 1)
            gain(B - 1)

        @block.tensor
        def _(pe):
            pe.wait_ge(c_ident, 1)

            def claim(n):
                if n >= 8:
                    s, c = (pre_act, (n - 8) // 2 + 1) if n % 2 else (pre_dve, (n - 8) // 2 + 1)
                    pe.wait_ge(s, c)
                return PS[:, n % 8, :]

            pe.wait_ge(ld_ctx, 16)
            bank = claim(0)
            for c in range(DC):
                for t in range(DC):
                    m = pe.transpose(bank[:, D * c + P * t:D * c + P * (t + 1)], ctx_sb[:, t, P * c:P * (c + 1)],
                                     ident[:, :])
            m.then_inc(pre_mm, 1)

            def project(n, w, j):
                bank = claim(n)
                for jj in range(2):
                    for c in range(DC):
                        m = pe.matmul(bank[:, D * jj:D * (jj + 1)], w[:, c, P * (j + jj):P * (j + jj + 1)],
                                      cT[:, c, :], start=(c == 0), stop=(c == DC - 1))
                m.then_inc(pre_mm, 1)

            evacuated(pe, 0)
            pe.wait_ge(ld_wk, 16)
            for n in range(KT0, QT0):
                project(n, Wk_sb, 2 * (n - KT0))
            pe.wait_ge(ld_wq, 16)
            for n in range(QT0, A0):
                bank = claim(n)
                j = 2 * (n - QT0)
                for jj in range(2):
                    for c in range(DC):
                        m = pe.transpose(bank[:, D * jj + P * c:D * jj + P * (c + 1)],
                                         Wq_sb[:, c, P * (j + jj):P * (j + jj + 1)], ident[:, :])
                m.then_inc(pre_mm, 1)
            evacuated(pe, A0 - 1)
            for n in range(A0, VT0, 2):
                j = (n - A0) // 2
                banks = [claim(n), claim(n + 1)]
                for c in range(DC):
                    for s in range(2):
                        rows = slice(DH * s, DH * (s + 1))
                        m = pe.matmul(banks[s][:, D * c:D * (c + 1)], WqT[rows, j, P * c:P * (c + 1)],
                                      KT[rows, j, :], start=True, stop=True)
                m.then_inc(pre_mm, 2)
            pe.wait_ge(ld_wv, 16)
            for n in range(VT0, VO0):
                project(n, Wv_sb, 2 * (n - VT0))
            pe.wait_ge(ld_wo, 16)
            evacuated(pe, VO0 - 1)
            for n in range(VO0, GROUPS):
                bank = claim(n)
                b, j = divmod(2 * (n - VO0), JC)
                for jj in range(2):
                    m = pe.matmul(bank[:, D * jj:D * (jj + 1)],
                                  VBD[:, j + jj, b].rearrange("p h k -> p (h k)"), Wo_sb[:, j + jj, :],
                                  start=True, stop=True)
                m.then_inc(pre_mm, 1)
            evacuated(pe, GROUPS - 1)
            pe.wait_ge(ld_b1, 16)
            pe.transpose(PS[:, 7, 0:EXPERTS * HC], b1_rows[:, :], ident[0:EXPERTS * HC, 0:EXPERTS * HC]
                         ).then_inc(b1_mm, 1)
            pe.wait_ge(ld_small, 16 * 6)

            def transpose_x(i, s):
                wait(pe, xn_ready, i + 1)
                wait(pe, xT_ready, i)
                for c in range(DC):
                    m = pe.transpose(xT_ps[:, P * c:P * (c + 1)], xn_b[s][:, P * c:P * (c + 1)], ident[:, :])
                m.then_inc(xT_mm, 1)

            transpose_x(0, 0)

            def step(g, u):
                i = 2 * g + u
                v = 1 - u
                static = isinstance(i, int)

                def scores(h):
                    b = batch_of(g, u)
                    if h == 0:
                        wait(pe, xT_ready, i + 1)
                    wait(pe, shifted, 2 * i - 2 + h + 1)
                    for c in range(DC):
                        a = A[:, c, :, BANK * h:BANK * (h + 1)]
                        m = pe.matmul(S_ps[h], xnT_b[u][:, c, :], at(a, b), start=(c == 0), stop=(c == DC - 1))
                    m.then_inc(s_mm, 1)

                if not static or i < TILES:
                    scores(0)
                if not static or 1 <= i <= TILES:
                    for h in range(2):
                        wait(pe, p_ready, 2 * i - 2 + h + 1)
                        wait(pe, pT_ready, 2 * i - 4 + h + 1)
                        for j in range(4):
                            c0 = BANK * h + P * j
                            m = pe.transpose(PT_ps[h][:, P * j:P * (j + 1)], E[:, v, c0:c0 + P], ident[:, :])
                        m.then_inc(pT_mm, 1)
                if not static or i < TILES:
                    scores(1)
                if not static or i + 1 < TILES:
                    transpose_x(i + 1, v)
                if not static or i >= 2:
                    wait(pe, xn2_ready, i - 1)
                    wait(pe, x2T_ready, i - 2)
                    for c in range(DC):
                        m = pe.transpose(x2T_ps[:, P * c:P * (c + 1)], xn2_b[u][:, P * c:P * (c + 1)], ident[:, :])
                    m.then_inc(x2T_mm, 1)
                if not static or 1 <= i <= TILES:
                    b = batch_of(g, u - 1)
                    wait(pe, x2_ready, i - 1)
                    for j in range(JC):
                        if j % 4 == 0:
                            wait(pe, pT_ready, 2 * i - 2 + j // 4 + 1)
                        m = pe.matmul(O_ps, PT[:, v, j, :], at(VO[:, :, j, :], b), start=(j == 0),
                                      stop=(j == JC - 1))
                    m.then_inc(o_mm, 1)
                if not static or i >= 2:
                    wait(pe, x2T_ready, i - 1)
                    k = i - 2
                    gate = (G_ps[:, EXPERTS * k:EXPERTS * (k + 1)] if static
                            else G_ps[:, bass.ds(k * EXPERTS, EXPERTS)])
                    for c in range(DC):
                        m = pe.matmul(gate, xn2T_b[u][:, c, :], gW[:, c, :], start=(c == 0), stop=(c == DC - 1))
                    m.then_inc(g_mm, 1)

            attention_steps(pe, step)

            for s in range(2):
                pe.wait_ge(st_x2T[s], 16 * TILES // 2)
            pe.wait_ge(c_pool, 12)
            pe.wait_ge(ld_shared, 16 * 2)

            def shared(t):
                z = PS[:, t % 4, 0:D]
                if t >= 4:
                    pe.wait_ge(z_gelu, t - 3)
                pe.matmul(z, ones_row[:, :], sb_row[:, :], start=True, stop=False)
                for c in range(DC):
                    m = pe.matmul(z, XN2T[:, t, P * c:P * (c + 1)], sW[:, c, :], start=False, stop=(c == DC - 1))
                m.then_inc(z_mm, 1)

            for t in range(5):
                shared(t)
            pe.wait_ge(M_ready, 1)
            for t in range(TILES):
                m = pe.matmul(cnt_ps, ones_b[:, :], M_bf[:, t, :], start=(t == 0), stop=(t == TILES - 1))
            m.then_inc(cnt_mm, 1)
            Mf = M_bf[:, :, :].rearrange("p t e -> p (t e)")
            n = TILES * EXPERTS
            pe.matmul(rank_ps, upper[:, :], Mf, start=True, stop=False, skip_group_check=True)
            for t in range(1, TILES):
                m = pe.matmul(rank_ps[:, EXPERTS * t:], ones_b[:, :], Mf[:, 0:n - EXPERTS * t], start=False,
                              stop=(t == TILES - 1), skip_group_check=True)
            m.then_inc(rank_mm, 1)
            for t in range(5, 13):
                shared(t)
            for k in range(PAIRS):
                if k % 8 == 0:
                    pe.wait_ge(oh_ready, k // 8 + 1)
                m = pe.matmul(tab_ps, OH_lo[:, k, :], RH[:, k, :, :].rearrange("p a m -> p (a m)"), start=(k == 0),
                              stop=(k == PAIRS - 1))
            m.then_inc(tab_mm, 1)
            for t in range(13, TILES):
                shared(t)
            pe.wait_ge(z_gelu, TILES)
            pe.wait_ge(route_ready, 1)
            pe.wait_ge(lo_done, QUARTERS * EXPERTS)

            def transpose_rows(g, u):
                i = 2 * g + u
                wait(pe, ga[u], 16 * (g + 1))
                wait(pe, xsTl_ready, i)
                for c in range(DC):
                    m = pe.transpose(PS[:, 5, P * c:P * (c + 1)], xs[:, u, P * c:P * (c + 1)], ident[:, :])
                m.then_inc(xsT_mm, 1)

            transpose_rows(0, 0)
            HIGH, LOW = 0, 1

            def mix(g, u):
                i = 2 * g + u
                static = isinstance(i, int)
                if not static or i < MTILES:
                    e = pe.value_load(col(etile, i), min_val=0, max_val=EXPERTS - 1)
                    wait(pe, xsTh_ready, i + 1)
                    wait(pe, xsTl_ready, i + 1)
                    for h in range(2):
                        wait(pe, h_ready, 2 * i - 2 + h + 1)
                        for n, (c, w) in enumerate([(c, w) for c in range(DC) for w in (HIGH, LOW)]):
                            wp = at(W16e[:, :, c, w, BANK * h:BANK * (h + 1)], e)
                            for a in ((HIGH, LOW) if w == HIGH else (HIGH,)):
                                m = pe.matmul(PS[:, h, :], xsT16[:, a, c, :], wp, start=(n == 0 and a == HIGH),
                                              stop=(n == 3))
                        m.then_inc(h_mm, 1)
                if not static or i + 1 < MTILES:
                    transpose_rows(g + (u + 1) // 2, 1 - u)
                if not static or i >= 1:
                    e = pe.value_load(col(etile, i - 1), min_val=0, max_val=EXPERTS - 1)
                    wait(pe, yb_ready, i - 1)
                    for j in range(HC):
                        if j % 4 == 0:
                            wait(pe, gh_ready, 2 * i - 2 + j // 4 + 1)
                        w = at4(W16e[:, :, DC + j // 4, :, D * (j % 4):D * (j % 4 + 1)], e)
                        pe.matmul(PS[:, 4, :].rearrange("p (a n) -> p a n", a=2), g16[:, HIGH, j, :], w,
                                  start=(j == 0), stop=False, skip_group_check=True)
                        if j % 4 == 0:
                            wait(pe, gl_ready, 2 * i - 2 + j // 4 + 1)
                        m = pe.matmul(PS[:, 4, 0:D], g16[:, LOW, j, :], w[:, 0, :], start=False,
                                      stop=(j == HC - 1), skip_group_check=True)
                    m.then_inc(y_mm, 1)
                if not static or i < MTILES:
                    for h in range(2):
                        wait(pe, h_ready, 2 * i + h + 1)
                        wait(pe, gelu_done, 2 * i - 2 + h + 1)
                        for j in range(4):
                            c0 = BANK * h + P * j
                            m = pe.transpose(PS[:, 2 + h, P * j:P * (j + 1)], h32[:, c0:c0 + P], ident[:, :])
                        m.then_inc(hT_mm, 1)

            mixture_steps(pe, mix)


INPUTS = ["x", "ctx_1024", "g_xattn", "g_ffn", "L0_xattn_Wq", "L0_xattn_Wk", "L0_xattn_Wv", "L0_xattn_Wo",
          "L0_xattn_bo", "L0_ffn_W1", "L0_ffn_b1", "L0_ffn_W2", "L0_ffn_b2", "L0_ffn_gate_W", "L0_ffn_shared_W",
          "L0_ffn_shared_b", "L0_ffn_gamma", "L0_ffn_beta"]


def kernel(**inputs):
    import concourse.bacc as bacc
    from concourse.bass_utils import run_bass_kernel_spmd

    nc = bacc.Bacc("TRN2", target_bir_lowering=False, num_devices=1)
    arrays, args = {}, []
    for name in INPUTS:
        a = np.ascontiguousarray(inputs[name])
        arrays[name] = a
        args.append(nc.dram_tensor(name, a.shape, mybir.dt.from_np(a.dtype), kind="ExternalInput").ap())
    out = nc.dram_tensor("out", (B, S, D), f32, kind="ExternalOutput").ap()
    xn2_dram = nc.dram_tensor("xn2_rows", (TOKENS, D), f32, kind="Internal").ap()
    acc_dram = nc.dram_tensor("acc_rows", (TOKENS + P, D), f32, kind="Internal").ap()
    build(nc, *args, out, xn2_dram, acc_dram)
    r = run_bass_kernel_spmd(nc, [arrays], core_ids=[0])
    return r.results[0]["out"]
```

```python
from contextlib import ExitStack

import numpy as np
import concourse.bass as bass
from concourse import mybir

P = 128
B, S, D = 4, 512, 256
NCTX = 64
HEADS, DH = 16, 64
INNER = HEADS * DH
EXPERTS, HID = 8, 1024
CHOICES = 2
TOKENS = B * S
TILES = TOKENS // P
TPB = S // P
DC = D // P
HC = HID // P
JC = INNER // P
LAST_BY_DVE = [0, 0, 0, 2]
MTILES = (CHOICES * TOKENS + EXPERTS * (P - 1)) // P
PAIRS = CHOICES * TILES
BANK = 512
QUARTERS = 4
QW = DC * HID * 2 // QUARTERS
EARLY = 2
SPLIT_LEAD = 2
W_SCALE = 256.0
H_SCALE = 16.0
A_SCALE = 64.0
ACC_SCALE = 2.0
LN_EPS = 1e-5
SCALE = DH ** -0.5

f32 = mybir.dt.float32
bf16 = mybir.dt.bfloat16
f16 = mybir.dt.float16
i32 = mybir.dt.int32
ALU = mybir.AluOpType
ACT = mybir.ActivationFunctionType
AX = mybir.AxisListType.X


def build(nc, x, ctx_in, g_xattn, g_ffn, Wq, Wk, Wv, Wo, bo, W1, b1, W2, b2, gate_W, shared_W, shared_b,
          gamma, beta, out, xn2_dram, acc_dram):
    stack = ExitStack()
    with stack:
        def sb(name, shape, dt=f32):
            return stack.enter_context(nc.sbuf_tensor(name, shape, dt))

        def sem(name):
            return stack.enter_context(nc.semaphore(name))

        WE = sb("WE", [P, EXPERTS, QUARTERS * QW])
        W16 = WE[:, :, :].rearrange("p e n -> p (e n)").bitcast(f16).rearrange(
            "p (q a n) -> p q a n", q=QUARTERS * EXPERTS, a=2)
        W16e = W16.rearrange("p (e q) a n -> p e q a n", e=EXPERTS)
        half = DC * HID
        Wk_sb = WE[:, 2, 0:half].rearrange("p (c n) -> p c n", c=DC)
        Wv_sb = WE[:, 2, half:].rearrange("p (c n) -> p c n", c=DC)
        Wq_sb = WE[:, 3, 0:half].rearrange("p (c n) -> p c n", c=DC)
        Wo_sb = WE[:, 3, half:].rearrange("p (j n) -> p j n", j=JC)
        A16 = W16e[:, B:2 * B, 0:DC]
        VO = WE[:, B:2 * B, half:].rearrange("p b (j n) -> p b j n", j=JC)
        stage = sb("stage", [P, 2, QW])

        X = sb("X", [P, TILES, D])
        XR = sb("XR", [P, TILES * D])
        VBD = XR[:, :].rearrange("p (j b h k) -> p j b h k", j=JC, b=B, h=2)
        XN2T = XR[:, :].rearrange("p (t n) -> p t n", t=TILES)
        b2_bc = XR[:, 0:EXPERTS * D].rearrange("p (e n) -> p e n", e=EXPERTS)
        AT = sb("AT", [P, 4 * HID])
        WqT = AT[:, 0:half].rearrange("p (j n) -> p j n", j=JC)
        KT = AT[:, half:].rearrange("p (j n) -> p j n", j=JC)
        E = AT[:, 0:2 * HID].rearrange("p (s n) -> p s n", s=2)
        PT = AT[:, 2 * HID:].rearrange("p (s j n) -> p s j n", s=2, j=JC)
        OH_lo = AT[:, 0:2048].bitcast(f16).rearrange("p (n m) -> p n m", m=P)
        RH = AT[:, 2048:2048 + PAIRS * 3 * MTILES // 2].bitcast(f16).rearrange("p (n a m) -> p n a m", a=3, m=MTILES)
        sm = AT[:, 3920:4080].rearrange("p (a t) -> p a t", t=TILES)
        assert PAIRS * P // 2 == 2048 and 2048 + PAIRS * 3 * MTILES // 2 <= 3920
        g16 = AT[:, 0:1024].bitcast(f16).rearrange("p (a j n) -> p a j n", a=2, j=HC)
        h32 = AT[:, 1024:2048]
        g32 = AT[:, 2048:3072].rearrange("p (j n) -> p j n", j=HC)
        ys = AT[:, 3072:3584].rearrange("p (s n) -> p s n", s=2)
        xs = AT[:, 3584:4096].rearrange("p (s n) -> p s n", s=2)
        F = AT[:, :].rearrange("p (t n) -> p t n", t=TILES)

        BUF = sb("BUF", [P, 2048])
        ctx_sb = BUF[:, 0:512].rearrange("p (t n) -> p t n", t=DC)
        cT = BUF[:, 512:1024].rearrange("p (c n) -> p c n", c=DC)
        xn2_b = [ctx_sb[:, s, :] for s in range(2)]
        xn2T_b = [cT[:, s, :].rearrange("p (c n) -> p c n", c=DC) for s in range(2)]
        xn_b = [BUF[:, 1024 + 256 * s:1280 + 256 * s] for s in range(2)]
        xnT16 = [BUF[:, 1536 + 256 * s:1792 + 256 * s].bitcast(f16).rearrange("p (w c n) -> p w c n", w=2, c=DC)
                 for s in range(2)]
        eq_hi = BUF[:, 0:PAIRS * MTILES // 2].bitcast(f16).rearrange("p (n m) -> p n m", m=MTILES)
        cmp = BUF[0:1, 640:640 + MTILES * EXPERTS].rearrange("p (m e) -> p m e", e=EXPERTS)
        RT = [BUF[:, 1024 + 128 * n:1152 + 128 * n].rearrange("p (t e) -> p t e", e=EXPERTS) for n in range(5)]
        posi = BUF[:, 1664:1760].rearrange("p (a n) -> p a n", a=3).bitcast(i32)
        lohi = BUF[:, 1760:1824].rearrange("p (a n) -> p a n", a=2)
        cum = BUF[:, 1824:1888].rearrange("p (a n) -> p a n", a=4)
        iota_lo = BUF[:, 1888:1888 + P]
        cnti = BUF[:, 2016:2032].rearrange("p (a e) -> p a e", a=2).bitcast(i32)
        base8 = BUF[:, 2032:2040]

        R2 = sb("R2", [P, 1860])
        sW = R2[:, 0:512].rearrange("p (c n) -> p c n", c=DC)
        sb_row = R2[0:1, 512:768]
        tab = R2[:, 768:885].rearrange("p (a m) -> p a m", a=3)
        gidx = R2[:, 885:924].bitcast(i32)
        sidx = R2[:, 924:963].bitcast(i32)
        assert 3 * MTILES == 117
        xsT16 = R2[:, 964:1220].bitcast(f16).rearrange("p (a c n) -> p a c n", a=2, c=DC)
        zero_rows = R2[:, 1220:1220 + D]
        b1_rows = R2[0:EXPERTS * HC, 1732:1732 + P]
        ident = sb("ident", [P, P])
        upper = sb("upper", [P, P], bf16)
        ones_b = sb("ones_b", [P, P], bf16)
        ones_row = sb("ones_row", [1, P])
        gW = sb("gW", [P, DC, EXPERTS])
        bo_bc = sb("bo_bc", [P, D])
        tgam = sb("tgam", [P, D])
        tbet = sb("tbet", [P, D])
        tg = sb("tg", [P, 2])
        b1T = sb("b1T", [P, EXPERTS * HC])
        st = sb("st", [P, TILES, 6])
        mv = sb("mv", [P, TILES, 2])
        rstd = sb("rstd", [P, TILES])
        nmr = sb("nmr", [P, TILES])
        st2 = sb("st2", [P, 2, 6])
        mv2 = sb("mv2", [P, 2, 2])
        ve2 = sb("ve2", [P, 2])
        rs2 = sb("rs2", [P, 2, 2])
        mhalf = sb("mhalf", [P, TILES])
        mx = sb("mx", [P, 2, HEADS])
        rsum = sb("rsum", [P, 2, HEADS])
        rinv = sb("rinv", [P, 2, HEADS])
        Msum = sb("Msum", [P, EXPERTS], bf16)
        M_bf = sb("M_bf", [P, TILES, EXPERTS], bf16)
        share = sb("share", [P, TILES])
        wtok = sb("wtok", [P, CHOICES, TILES])
        pos = sb("pos", [P, CHOICES, TILES])
        tokid = sb("tokid", [P, TILES])
        iota_m = sb("iota_m", [P, MTILES])
        rank8 = sb("rank8", [P, EXPERTS])
        pad_row = sb("pad_row", [P, 1])
        etf = sb("etf", [1, MTILES])
        etile = sb("etile", [1, MTILES], i32)
        w16 = sb("w16", [P, 2, CHOICES, TILES], f16)
        gslot = sb("gslot", [P, 2], i32)
        sslot = sb("sslot", [P, 2], i32)
        gcol = [gslot[:, s:s + 1] for s in range(2)]
        scol = [sslot[:, s:s + 1] for s in range(2)]

        PS = stack.enter_context(nc.psum_tensor("PS", [P, 8, BANK], f32))
        S_ps = [PS[:, 0, :], PS[:, 1, :]]
        PT_ps = [PS[:, 2, :], PS[:, 3, :]]
        O_ps = PS[:, 4, 0:D]
        xT_ps, x2T_ps = PS[:, 5, 0:D], PS[:, 6, D:2 * D]
        G_ps = PS[:, 6, 0:TILES * EXPERTS]
        rank_ps = PS[:, 7, 0:TILES * EXPERTS]
        cnt_ps = PS[:, 6, 256:256 + EXPERTS]
        tab_ps = PS[:, 7, 256:256 + 3 * MTILES]

        ld_x = [sem(f"ld_x{b}") for b in range(B)]
        ld_wk = [sem(f"ld_wk{k}") for k in range(2)]
        ld_ctx, ld_wq, ld_wv, ld_wo, ld_small, ld_b2, ld_b1, ld_shared = [
            sem(n) for n in "ld_ctx ld_wq ld_wv ld_wo ld_small ld_b2 ld_b1 ld_shared".split()]
        ldq = [sem(f"ldq{s}") for s in range(2)]
        ld_last = [sem(f"ld_last{v}") for v in range(QUARTERS)]
        hi_done, scaled, pool_lo = sem("hi_done"), sem("scaled"), sem("pool_lo")
        c_pool, c_ident, c_vbd, c_half = sem("c_pool"), sem("c_ident"), sem("c_vbd"), sem("c_half")
        pre_mm, pre_dve, pre_act = sem("pre_mm"), sem("pre_dve"), sem("pre_act")
        b1_mm, b1_ready = sem("b1_mm"), sem("b1_ready")
        tanh_ready, bo_ready, gb_ready = sem("tanh_ready"), sem("bo_ready"), sem("gb_ready")
        ln1_st, ln1_mv, ln1_ready = sem("ln1_st"), sem("ln1_mv"), sem("ln1_ready")
        s_mm, xT_mm, x2T_mm, pT_mm, o_mm, g_mm = [sem(n) for n in "s_mm xT_mm x2T_mm pT_mm o_mm g_mm".split()]
        xn_ready, xT_ready, exp_ready, pT_ready, xn2_ready, x2T_ready = [
            sem(n) for n in "xn_ready xT_ready exp_ready pT_ready xn2_ready x2T_ready".split()]
        mx_ready, shifted, sum_ready, rinv_ready, x2_ready, st2_ready, mv2_ready = [
            sem(n) for n in "mx_ready shifted sum_ready rinv_ready x2_ready st2_ready mv2_ready".split()]
        p_ready, bo_added, ve2_ready, pow2_ready, rstd2_ready = [
            sem(n) for n in "p_ready bo_added ve2_ready pow2_ready rstd2_ready".split()]
        st_xn2 = [sem(f"st_xn2_{s}") for s in range(2)]
        st_x2T = [sem(f"st_x2T_{s}") for s in range(2)]
        dchain, pchain = sem("dchain"), sem("pchain")
        z_mm, z_gelu, x_beta = sem("z_mm"), sem("z_gelu"), sem("x_beta")
        st_acc = [sem(f"st_acc{k}") for k in range(B)]
        pad_acc = sem("pad_acc")
        lg_ready, pexp_ready, M_ready, Msum_ready, cnt_mm, rank_mm, oh_ready, tab_mm, route_ready = [
            sem(n) for n in "lg_ready pexp_ready M_ready Msum_ready cnt_mm rank_mm oh_ready tab_mm route_ready".split()]
        ga = [sem(f"ga{s}") for s in range(2)]
        sc = [sem(f"sc{s}") for s in range(2)]
        xsT_mm, h_mm, hT_mm, y_mm = [sem(n) for n in "xsT_mm h_mm hT_mm y_mm".split()]
        h_ready, y1_ready = sem("h_ready"), sem("y1_ready")
        xsTh_ready, gelu_done, gh_ready = sem("xsTh_ready"), sem("gelu_done"), sem("gh_ready")
        xsTl_ready, gl_ready, yb_ready, y_ready, gi_ready = [
            sem(n) for n in "xsTl_ready gl_ready yb_ready y_ready gi_ready".split()]
        eq_ready, pool_oh, etile_ready, xTl_ready = [
            sem(n) for n in "eq_ready pool_oh etile_ready xTl_ready".split()]
        ld_f = [sem(f"ld_f{k}") for k in range(B)]
        f_last, f_cen, f_norm, f_gam, f_rstd, f_ve, f_pow, f_out, st_out = [
            sem(n) for n in "f_last f_cen f_norm f_gam f_rstd f_ve f_pow f_out st_out".split()]

        dve_waits, pool_waits = sem("dve_waits"), sem("pool_waits")

        block = stack.enter_context(nc.Block())

        def wait(eng, s, value):
            if not isinstance(value, int) or value > 0:
                eng.wait_ge(s, value)

        def alone(eng, g, own):
            if not isinstance(g, int):
                eng.sem_inc(own, 1)

        def at(ap, i):
            if isinstance(i, int):
                return ap[:, i]
            one = ap[:, bass.ds(i, 1)]
            return one.rearrange("p o n -> p (o n)") if len(one.shape) == 3 else one

        def at4(ap, i):
            return ap[:, i] if isinstance(i, int) else ap[:, bass.ds(i, 1)].rearrange("p o a n -> p (o a) n")

        def batch_of(g, u):
            pair = g + u // 2
            b = pair // (TPB // 2)
            return b if isinstance(b, int) else b.with_bounds(min_val=0, max_val=B - 1)

        def col(ap, i):
            return ap[:, i:i + 1] if isinstance(i, int) else ap[:, bass.ds(i, 1)]

        x_t = x.rearrange("b (t p) d -> p (b t) d", p=P)
        out_t = out.rearrange("b (t p) d -> p (b t) d", p=P)
        xn2_rows = xn2_dram.rearrange("(t p) d -> p t d", p=P)
        acc_rows = acc_dram[0:TOKENS, :].rearrange("(t p) d -> p t d", p=P)

        def quarter_of(e, v):
            if v < DC:
                w = W1[:, P * v:P * (v + 1), :]
            else:
                w = W2[:, QW // D * P * (v - DC):QW // D * P * (v - DC + 1), :]
            one = w[e] if isinstance(e, int) else w[bass.ds(e, 1)].rearrange("o r n -> (o r) n")
            return one if v < DC else one.rearrange("(j p) n -> p j n", p=P)

        def stage_of(s, v):
            return stage[:, s, :] if v < DC else stage[:, s, :].rearrange("p (j n) -> p j n", n=D)

        def split_high(act, q, s, loaded=None):
            static = isinstance(q, int)
            if loaded is None:
                wait(act, ldq[s], 16 * (q // 2 + 1) if static else 16 * q[0])
            else:
                act.wait_ge(loaded, 16)
            k = q if static else q[1]
            act.activation(at(W16[:, :, 0, :], k), stage[:, s, :], ACT.Copy, scale=W_SCALE).then_inc(hi_done, 1)
            act.activation(stage[:, s, :], stage[:, s, :], ACT.Copy, scale=W_SCALE).then_inc(scaled, 1)

        def pool_low(pool, q, s):
            k = q if isinstance(q, int) else q[1]
            wait(pool, scaled, k + 1)
            wait(pool, hi_done, k + 1)
            pool.tensor_tensor(at(W16[:, :, 1, :], k), stage[:, s, :], at(W16[:, :, 0, :], k), ALU.subtract
                               ).then_inc(pool_lo, 1)

        def low_written(eng, q):
            wait(eng, pool_lo, q + 1)

        def step_quarters(i, g, u):
            if isinstance(i, int):
                first = QUARTERS * EARLY
                own = [first + 2 * i, first + 2 * i + 1] if i < 2 else []
                return own + ([first + QUARTERS + i - SPLIT_LEAD] if i >= SPLIT_LEAD else [])
            k = i + QUARTERS * (EARLY + 1) - SPLIT_LEAD
            return [(g + (QUARTERS * (EARLY + 1) - SPLIT_LEAD) // 2 + 1, k)]

        KT0, QT0, A0 = 1, 1 + JC // 2, 1 + JC
        VT0 = A0 + HEADS
        VO0 = VT0 + JC // 2
        GROUPS = VO0 + B * JC // 2

        def split_group(n):
            return A0 <= n < VT0

        def A_part(h, w):
            return A16[:, :, :, w, NCTX * h:NCTX * (h + 1)].rearrange("p b c k -> p c b k")

        def act_count(n):
            return sum(1 for m in range(n + 1) if m % 2 or split_group(m))

        def dve_count(n):
            return sum(1 for m in range(n + 1) if not m % 2 or split_group(m))

        LN1_PARTS = [slice(0, 2 * TPB), slice(2 * TPB, TILES)]
        LN1_AFTER = [0, 6]
        X_GROUP = GROUPS - 3
        SPLIT_FROM = GROUPS - 32

        def evacuated(eng, n):
            wait(eng, pre_dve, dve_count(n))
            wait(eng, pre_act, act_count(n))

        A_PEEL_END = 12

        def attention_steps(eng, step):
            for i in range(4):
                step(i // 2, i % 2)
            with eng.Fori(1, A_PEEL_END // 4) as pair:
                for n in range(2):
                    step(2 * pair + n, 0)
                    step(2 * pair + n, 1)
            for i in range(A_PEEL_END, TILES + 2):
                step(i // 2, i % 2)

        M_PEEL_END = 36

        def mixture_steps(eng, step):
            for i in range(4):
                step(i // 2, i % 2)
            with eng.Fori(1, M_PEEL_END // 4) as pair:
                for n in range(2):
                    step(2 * pair + n, 0)
                    step(2 * pair + n, 1)
            for i in range(M_PEEL_END, MTILES + 1):
                step(i // 2, i % 2)

        @block.sync
        def _(sp):
            def load(q):
                e, v = divmod(q, QUARTERS)
                low_written(sp, q - 2)
                sp.dma_start(stage_of(q % 2, v), quarter_of(e, v)).then_inc(ldq[q % 2], 16)

            sp.dma_start(ctx_sb[:, :, :], ctx_in.rearrange("b k d -> (b k) d").rearrange("(t p) d -> p t d", p=P)
                         ).then_inc(ld_ctx, 16)
            for k in range(2):
                part = slice(INNER // 2 * k, INNER // 2 * (k + 1))
                sp.dma_start(Wk_sb[:, :, part], Wk[:, part].rearrange("(c p) n -> p c n", p=P)
                             ).then_inc(ld_wk[k], 16)
            sp.dma_start(Wq_sb, Wq.rearrange("(c p) n -> p c n", p=P)).then_inc(ld_wq, 16)
            for b in range(B):
                sp.dma_start(X[:, TPB * b:TPB * (b + 1), :], x_t[:, TPB * b:TPB * (b + 1), :]).then_inc(ld_x[b], 16)
            load(0)
            load(1)
            sp.dma_start(Wv_sb, Wv.rearrange("(c p) n -> p c n", p=P)).then_inc(ld_wv, 16)
            sp.dma_start(Wo_sb, Wo.rearrange("(j p) n -> p j n", p=P)).then_inc(ld_wo, 16)
            first = QUARTERS * (EARLY + 1)
            for q in range(2, first):
                load(q)

            with sp.Fori(0, B) as b:
                for v in range(QUARTERS):
                    wait(sp, pool_lo, 4 * b + (first + v - 1))
                    sp.dma_start(stage_of(v % 2, v), quarter_of(b + (EARLY + 1), v)).then_inc(ldq[v % 2], 16)
                    i = b * TPB + v
                    wait(sp, xn2_ready, i + 1)
                    sp.dma_start(at(xn2_rows, i), xn2_b[v % 2]).then_inc(st_xn2[v % 2], 16)
                    wait(sp, x2T_ready, i + 1)
                    sp.dma_start(at(XN2T, i), xn2T_b[v % 2][:, :, :].rearrange("p c n -> p (c n)")
                                 ).then_inc(st_x2T[v % 2], 16)
            for k in range(B):
                if k < 2:
                    q = QUARTERS * EXPERTS - 2 + k
                    low_written(sp, q - 2)
                    sp.dma_start(stage_of(q % 2, q % QUARTERS), quarter_of(EXPERTS - 1, q % QUARTERS)
                                 ).then_inc(ld_last[q % QUARTERS], 16)
                tiles = slice(TPB * k, TPB * (k + 1))
                sp.wait_ge(z_gelu, TPB * (k + 1))
                sp.dma_start(acc_rows[:, tiles, :], XN2T[:, tiles, :]).then_inc(st_acc[k], 16)
            for k in range(2):
                sp.wait_ge(st_acc[k], 16)
            sp.dma_start(b2_bc, b2.rearrange("e n -> (e n)").partition_broadcast(P)
                         .rearrange("p (e n) -> p e n", e=EXPERTS)).then_inc(ld_b2, 16)
            for s in range(2):
                sp.wait_ge(sc[s], 16 * ((MTILES - s + 1) // 2))
            for k in range(B):
                sp.dma_start(F[:, TPB * k:TPB * (k + 1), :], acc_rows[:, TPB * k:TPB * (k + 1), :]
                             ).then_inc(ld_f[k], 16)
            for k in range(B):
                sp.wait_ge(f_out, k + 1)
                wait(sp, f_last, sum(LAST_BY_DVE[:k + 1]))
                sp.dma_start(out_t[:, TPB * k:TPB * (k + 1), :], X[:, TPB * k:TPB * (k + 1), :]
                             ).then_inc(st_out, 16)
            sp.wait_ge(st_out, 16 * B)
            sp.wait_ge(pad_acc, 16)

        @block.gpsimd
        def _(pool):
            pool.memset(ident[:, :], 0.0).then_inc(c_pool, 1)
            pool.memset(upper[:, :], 1.0).then_inc(c_pool, 1)
            pool.memset(ones_b[:, :], 1.0).then_inc(c_pool, 1)
            pool.memset(ones_row[:, :], 1.0).then_inc(c_pool, 1)
            pool.memset(zero_rows, 0.0).then_inc(c_pool, 1)
            pool.memset(mhalf[:, :], -0.5).then_inc(c_half, 1)
            pool.wait_ge(c_pool, 5)
            pool.affine_select(out=ident[:, :], in_=ident[:, :], compare_op=ALU.not_equal, fill=1.0, base=0,
                               pattern=[[-1, P]], channel_multiplier=1).then_inc(c_ident, 1)
            pool.affine_select(out=upper[:, :], in_=upper[:, :], compare_op=ALU.is_gt, fill=0.0, base=0,
                               pattern=[[1, P]], channel_multiplier=-1).then_inc(c_pool, 1)
            pool.memset(XR[:, :], 0.0).then_inc(c_vbd, 1)
            pool.dma_start(acc_dram[TOKENS:TOKENS + P, :], zero_rows).then_inc(pad_acc, 16)
            pool.iota(tokid[:, :], pattern=[[P, TILES]], base=1, channel_multiplier=1,
                      allow_small_or_imprecise_dtypes=True).then_inc(c_pool, 1)
            pool.iota(iota_m[:, :], pattern=[[1, MTILES]], base=0, channel_multiplier=0,
                      allow_small_or_imprecise_dtypes=True).then_inc(c_pool, 1)
            pool.iota(rank8[:, :], pattern=[[-1, EXPERTS]], base=EXPERTS, channel_multiplier=0,
                      allow_small_or_imprecise_dtypes=True).then_inc(c_pool, 1)
            pool.iota(pad_row[:, :], pattern=[[0, 1]], base=TOKENS + 1, channel_multiplier=1,
                      allow_small_or_imprecise_dtypes=True).then_inc(c_pool, 1)
            pool.wait_ge(tanh_ready, 1)
            pool.wait_ge(ld_small, 16 * 6)
            pool.tensor_scalar(bo_bc[:, :], bo_bc[:, :], tg[:, 0:1], None, ALU.mult).then_inc(bo_ready, 1)
            pool.tensor_scalar(tgam[:, :], tgam[:, :], tg[:, 1:2], None, ALU.mult).then_inc(gb_ready, 1)
            pool.tensor_scalar(tbet[:, :], tbet[:, :], tg[:, 1:2], None, ALU.mult).then_inc(gb_ready, 1)
            pool.wait_ge(c_half, 1)
            q = 0
            for part, tiles in enumerate(LN1_PARTS):
                while q < LN1_AFTER[part]:
                    pool_low(pool, q, q % 2)
                    q += 1
                pool.wait_ge(ln1_mv, part + 1)
                pool.tensor_tensor(rstd[:, tiles], nmr[:, tiles], mhalf[:, tiles], ALU.pow).then_inc(pchain, 1)
                pool.wait_ge(pchain, 2 * part + 1)
                pool.tensor_tensor(nmr[:, tiles], mv[:, tiles, 0], rstd[:, tiles], ALU.mult).then_inc(pchain, 1)
                pool.wait_ge(pchain, 2 * part + 2)
                pool.tensor_scalar(nmr[:, tiles], nmr[:, tiles], -1.0, None, ALU.mult).then_inc(ln1_ready, 1)
            for q in range(LN1_AFTER[1], QUARTERS * EARLY):
                pool_low(pool, q, q % 2)
            pool.wait_ge(bo_ready, 1)

            def step(g, u):
                i = 2 * g + u
                static = isinstance(i, int)
                if not static or i < TILES:
                    wait(pool, xn_ready, i + 1)
                    pool.tensor_tensor(at(X, i), at(X, i), bo_bc[:, :], ALU.add).then_inc(bo_added, 1)
                    for h in range(2):
                        wait(pool, rinv_ready, 2 * i + h + 1)
                        w = E[:, u, BANK * h:BANK * (h + 1)].rearrange("p (a k) -> p a k", k=NCTX)
                        r = rinv[:, u, 8 * h:8 * h + 8].unsqueeze(2).to_broadcast([P, 8, NCTX])
                        pool.tensor_tensor(w, w, r, ALU.mult).then_inc(p_ready, 1)
                if static and i == TILES:
                    pool_low(pool, step_quarters(i, g, u)[0], u)
                if not static or 1 <= i <= TILES:
                    v = 1 - u
                    wait(pool, mv2_ready, i)
                    alone(pool, g, pool_waits)
                    pool.tensor_scalar(ve2[:, v:v + 1], mv2[:, v, 1:2], LN_EPS, None, ALU.add
                                       ).then_inc(ve2_ready, 1)
                    wait(pool, ve2_ready, i)
                    wait(pool, xn2_ready, i - 2)
                    pool.tensor_tensor(rs2[:, v, 0:1], ve2[:, v:v + 1], mhalf[:, 0:1], ALU.pow
                                       ).then_inc(pow2_ready, 1)
                    wait(pool, pow2_ready, i)
                    alone(pool, g, pool_waits)
                    pool.tensor_scalar(rs2[:, v, 1:2], mv2[:, v, 0:1], rs2[:, v, 0:1], -1.0, ALU.mult, ALU.mult
                                       ).then_inc(rstd2_ready, 1)
                if not static or i != TILES:
                    for q in step_quarters(i, g, u):
                        pool_low(pool, q, u if not static or i >= SPLIT_LEAD else q % 2)

            attention_steps(pool, step)

            pool.wait_ge(s_mm, 2 * TILES)
            pool.iota(iota_lo[:, :], pattern=[[1, P]], base=0, channel_multiplier=0,
                      allow_small_or_imprecise_dtypes=True).then_inc(c_pool, 1)
            pool.memset(cum[:, :, :], 0.0).then_inc(c_pool, 1)

            def last_low(v):
                pool_low(pool, QUARTERS * (EXPERTS - 1) + v, v % 2)

            for v in range(2):
                last_low(v)
            pool.wait_ge(eq_ready, 1)
            pool.wait_ge(o_mm, TILES)
            n = slice(TILES, PAIRS)
            for a, factor in enumerate((tokid[:, :], w16[:, 0, 1, :], w16[:, 1, 1, :])):
                pool.tensor_tensor(RH[:, n, a, :], eq_hi[:, n, :],
                                   factor.unsqueeze(2).to_broadcast([P, TILES, MTILES]), ALU.mult
                                   ).then_inc(pool_oh, 1)
            for v in range(2, QUARTERS):
                last_low(v)
            for s in range(2):
                pool.wait_ge(st_xn2[s], 16 * TILES // 2)

            def gather(g, u):
                i = 2 * g + u
                wait(pool, gi_ready, i + 1)
                wait(pool, xsT_mm, i - 1)
                alone(pool, g, pool_waits)
                pool.indirect_dma_start(xs[:, u, :], None, xn2_dram,
                                        bass.IndirectOffsetOnAxis(ap=gcol[u], axis=0)).then_inc(ga[u], 16)

            gather(0, 0)
            gather(0, 1)
            pool.wait_ge(pad_acc, 16)
            for k in range(B):
                pool.wait_ge(st_acc[k], 16)
            pool.wait_ge(gb_ready, 2)
            pool.wait_ge(x2_ready, TILES)
            pool.wait_ge(xn2_ready, TILES)
            pool.wait_ge(mv2_ready, TILES)

            def mix(g, u):
                i = 2 * g + u
                static = isinstance(i, int)
                if not static or i + 2 < MTILES:
                    gather(g + 1, u)
                if not static or i >= 1:
                    s = 1 - u
                    wait(pool, y_ready, i)
                    wait(pool, sc[u], 16 * g)
                    alone(pool, g, pool_waits)
                    pool.indirect_dma_start(acc_dram, bass.IndirectOffsetOnAxis(ap=scol[s], axis=0), ys[:, s, :],
                                            None, compute_op=ALU.add).then_inc(sc[s], 16)
                if static and i < B:
                    part = X[:, TPB * i:TPB * (i + 1), :]
                    pool.tensor_tensor(part, part, tbet[:, :].unsqueeze(1).to_broadcast([P, TPB, D]), ALU.add
                                       ).then_inc(x_beta, 1)

            mixture_steps(pool, mix)

            def add_residual(k):
                part = slice(TPB * k, TPB * (k + 1) - LAST_BY_DVE[k])
                pool.wait_ge(f_gam, k + 1)
                pool.tensor_tensor(X[:, part, :], X[:, part, :], F[:, part, :], ALU.add).then_inc(f_out, 1)

            for k in range(B):
                tiles = slice(TPB * k, TPB * (k + 1))
                pool.wait_ge(f_ve, k + 1)
                pool.tensor_tensor(rstd[:, tiles], nmr[:, tiles], mhalf[:, 0:TPB], ALU.pow).then_inc(f_pow, 1)
                if k >= 1:
                    add_residual(k - 1)
            add_residual(B - 1)

        @block.scalar
        def _(act):
            act.dma_start(tg[:, 0:1], g_xattn.partition_broadcast(P)).then_inc(ld_small, 16)
            act.dma_start(tg[:, 1:2], g_ffn.partition_broadcast(P)).then_inc(ld_small, 16)
            act.dma_start(gW[:, :, :], gate_W.rearrange("(c p) n -> p c n", p=P)).then_inc(ld_small, 16)
            act.dma_start(bo_bc[:, :], bo.partition_broadcast(P)).then_inc(ld_small, 16)
            act.dma_start(tgam[:, :], gamma.partition_broadcast(P)).then_inc(ld_small, 16)
            act.dma_start(tbet[:, :], beta.partition_broadcast(P)).then_inc(ld_small, 16)
            act.dma_start(b1_rows[:, :], b1.rearrange("e (j p) -> (e j) p", p=P)).then_inc(ld_b1, 16)
            act.dma_start(sW[:, :, :], shared_W.rearrange("(c p) n -> p c n", p=P)).then_inc(ld_shared, 16)
            act.dma_start(sb_row[:, :], shared_b.rearrange("(a n) -> a n", a=1)).then_inc(ld_shared, 16)

            def ln1(i, s):
                wait(act, xT_mm, i - 1)
                act.activation(xn_b[s][:, :], at(X, i), ACT.Identity, bias=col(nmr, i), scale=col(rstd, i)
                               ).then_inc(xn_ready, 1)

            def xT_evac(i, s):
                wait(act, xT_mm, i + 1)
                wait(act, s_mm, 2 * (i - 1))
                act.activation(xnT16[s][:, 0].rearrange("p c n -> p (c n)"), xT_ps, ACT.Copy
                               ).then_inc(xT_ready, 1)

            def evac(n):
                act.wait_ge(pre_mm, n + 1)
                bank = PS[:, n % 8, :]
                if n < QT0:
                    j = 2 * (n - KT0)
                    m = act.activation(KT[:, j:j + 2, :].rearrange("p j n -> p (j n)"), bank, ACT.Copy, scale=SCALE)
                elif n < A0:
                    j = 2 * (n - QT0)
                    m = act.activation(WqT[:, j:j + 2, :].rearrange("p j n -> p (j n)"), bank, ACT.Copy)
                elif n < VT0:
                    m = act.activation(A_part(n - A0, 0), bank.rearrange("p (c b k) -> p c b k", c=DC, b=B), ACT.Copy,
                                       scale=A_SCALE)
                elif n < VO0:
                    j = 2 * (n - VT0)
                    act.wait_ge(c_vbd, 1)
                    for s in range(2):
                        m = act.activation(VBD[DH * s:DH * (s + 1), j:j + 2, :, s, :], bank[DH * s:DH * (s + 1), :]
                                           .rearrange("p (j b k) -> p j b k", j=2, b=B), ACT.Copy)
                else:
                    b, j = divmod(2 * (n - VO0), JC)
                    m = act.activation(VO[:, b, j:j + 2, :].rearrange("p j n -> p (j n)"), bank, ACT.Copy)
                m.then_inc(pre_act, 1)

            for n in range(1, GROUPS):
                if n % 2 or split_group(n):
                    evac(n)
                if n == QT0 + 2:
                    act.wait_ge(ld_small, 16 * 6)
                    act.activation(tg[:, :], tg[:, :], ACT.Tanh).then_inc(tanh_ready, 1)
                if n >= SPLIT_FROM and (n - SPLIT_FROM) % 4 == 0 and (n - SPLIT_FROM) // 4 < QUARTERS * EARLY:
                    q = (n - SPLIT_FROM) // 4
                    split_high(act, q, q % 2)
                if n == X_GROUP - 3:
                    act.wait_ge(ln1_ready, 1)
                    ln1(0, 0)
                    ln1(1, 1)
            xT_evac(0, 0)

            def load_last(v):
                q = QUARTERS * (EXPERTS - 1) + v
                low_written(act, q - 2)
                act.dma_start(stage_of(v, v), quarter_of(EXPERTS - 1, v)).then_inc(ld_last[v], 16)

            def step(g, u):
                i = 2 * g + u
                v = 1 - u
                static = isinstance(i, int)
                scores = not static or i < TILES
                if static and i == TILES + 1:
                    for q in step_quarters(i, g, u):
                        split_high(act, q, q % 2)
                    load_last(0)
                if not static or 1 <= i <= TILES:
                    for h in range(2):
                        wait(act, pT_mm, 2 * i - 2 + h + 1)
                        wait(act, o_mm, i - 2)
                        act.activation(PT[:, v, 4 * h:4 * h + 4, :].rearrange("p j n -> p (j n)"), PT_ps[h],
                                       ACT.Copy).then_inc(pT_ready, 1)
                if not static or i >= 2:
                    wait(act, rstd2_ready, i - 1)
                    wait(act, st_xn2[u], 16 * (g - 1))
                    act.activation(xn2_b[u], at(X, i - 2), ACT.Identity, bias=rs2[:, u, 1:2],
                                   scale=rs2[:, u, 0:1]).then_inc(xn2_ready, 1)
                if scores:
                    wait(act, shifted, 2 * i + 1)
                    act.activation(E[:, u, 0:BANK], E[:, u, 0:BANK], ACT.Exp, scale=1 / A_SCALE
                                   ).then_inc(exp_ready, 1)
                if not static or i + 1 < TILES:
                    xT_evac(i + 1, v)
                if not static or i >= 2:
                    wait(act, x2T_mm, i - 1)
                    wait(act, st_x2T[u], 16 * (g - 1))
                    if static:
                        wait(act, g_mm, i - 3)
                    act.activation(xn2T_b[u][:, :, :].rearrange("p c n -> p (c n)"), x2T_ps, ACT.Copy
                                   ).then_inc(x2T_ready, 1)
                if scores:
                    wait(act, shifted, 2 * i + 2)
                    act.activation(E[:, u, BANK:], E[:, u, BANK:], ACT.Exp, scale=1 / A_SCALE
                                   ).then_inc(exp_ready, 1)
                if not static or i <= TILES:
                    for q in step_quarters(i, g, u):
                        split_high(act, q, u if not static or i >= SPLIT_LEAD else q % 2)
                if static and i + 2 == TPB:
                    act.wait_ge(ln1_ready, 2)
                if not static or i + 2 < TILES:
                    ln1(i + 2, u)

            attention_steps(act, step)

            load_last(1)

            def last_high(v):
                split_high(act, QUARTERS * (EXPERTS - 1) + v, v % 2, ld_last[v])

            last_high(0)
            act.wait_ge(lg_ready, 1)
            act.activation(share[:, :], share[:, :], ACT.Exp).then_inc(pexp_ready, 1)

            def rows_high(i):
                wait(act, xsT_mm, i + 1)
                wait(act, h_mm, 2 * i)
                act.activation(xsT16[:, 0].rearrange("p c n -> p (c n)"), PS[:, 5, 0:D], ACT.Copy
                               ).then_inc(xsTh_ready, 1)

            for t in range(TILES):
                if t == 14:
                    rows_high(0)
                if t % 2 == 0:
                    act.wait_ge(z_mm, t + 2)
                act.activation(XN2T[:, t, :], PS[:, t // 2 % 4, D * (t % 2):D * (t % 2 + 1)], ACT.Gelu
                               ).then_inc(z_gelu, 1)
                if t in (1, 5, 9):
                    last_high(1 + t // 4)
                if t == 11:
                    act.wait_ge(b1_mm, 1)
                    act.activation(b1T[:, :], PS[:, 5, 0:EXPERTS * HC], ACT.Copy).then_inc(b1_ready, 1)
            act.wait_ge(b1_ready, 1)
            act.wait_ge(etile_ready, 1)

            def mix(g, u):
                i = 2 * g + u
                static = isinstance(i, int)

                def hidden(h):
                    wait(act, hT_mm, 2 * i + h + 1)
                    wait(act, gl_ready, 2 * i - 2 + h + 1)
                    for j in range(4 * h, 4 * h + 4):
                        m = act.activation(g32[:, j, :], PS[:, 2 + h, P * (j % 4):P * (j % 4 + 1)], ACT.Gelu,
                                           bias=b1T[:, bass.ds(e * HC + j, 1)], scale=1 / W_SCALE)
                    m.then_inc(gelu_done, 1)
                    wait(act, gelu_done, 2 * i + h + 1)
                    wait(act, y_mm, i)
                    act.activation(g16[:, 0, 4 * h:4 * h + 4, :].rearrange("p j n -> p (j n)"),
                                   g32[:, 4 * h:4 * h + 4, :].rearrange("p j n -> p (j n)"), ACT.Copy,
                                   scale=H_SCALE).then_inc(gh_ready, 1)

                if not static or i < MTILES:
                    e = act.value_load(col(etile, i), min_val=0, max_val=EXPERTS - 1)
                if not static or i + 1 < MTILES:
                    rows_high(i + 1)
                if not static or i < MTILES:
                    hidden(0)
                    hidden(1)

            mixture_steps(act, mix)

            for k in range(B):
                act.wait_ge(f_rstd, k + 1)
                for t in range(TPB * k, TPB * (k + 1) - LAST_BY_DVE[k]):
                    m = act.activation(F[:, t, :], F[:, t, :], ACT.Identity, bias=nmr[:, t:t + 1],
                                       scale=rstd[:, t:t + 1])
                m.then_inc(f_norm, 1)

        @block.vector
        def _(dve):
            chain = [0]

            def link(ins, other=None):
                if other is not None:
                    ins.then_inc(other, 1)
                    dve.wait_ge(other, 1)
                    return
                chain[0] += 1
                ins.then_inc(dchain, 1)
                dve.wait_ge(dchain, chain[0])

            def evac(n):
                dve.wait_ge(pre_mm, n + 1)
                if split_group(n):
                    dve.wait_ge(pre_act, act_count(n))
                bank = PS[:, n % 8, :]
                if n == 0:
                    m = dve.tensor_copy(cT[:, :, :].rearrange("p c n -> p (c n)"), bank)
                elif n < QT0:
                    j = 2 * (n - KT0)
                    m = dve.tensor_scalar(KT[:, j:j + 2, :].rearrange("p j n -> p (j n)"), bank, SCALE, None,
                                          ALU.mult)
                elif n < A0:
                    j = 2 * (n - QT0)
                    m = dve.tensor_copy(WqT[:, j:j + 2, :].rearrange("p j n -> p (j n)"), bank)
                elif n < VT0:
                    for c in range(DC):
                        m = dve.scalar_tensor_tensor(A_part(n - A0, 1)[:, c], bank[:, D * c:D * (c + 1)].rearrange(
                            "p (b k) -> p b k", b=B), A_SCALE, A_part(n - A0, 0)[:, c], ALU.mult, ALU.subtract)
                elif n < VO0:
                    j = 2 * (n - VT0)
                    dve.wait_ge(c_vbd, 1)
                    for s in range(2):
                        m = dve.tensor_copy(VBD[DH * s:DH * (s + 1), j:j + 2, :, s, :], bank[DH * s:DH * (s + 1), :]
                                            .rearrange("p (j b k) -> p j b k", j=2, b=B))
                else:
                    b, j = divmod(2 * (n - VO0), JC)
                    m = dve.tensor_copy(VO[:, b, j:j + 2, :].rearrange("p j n -> p (j n)"), bank)
                m.then_inc(pre_dve, 1)

            def group(n):
                if not n % 2 or split_group(n):
                    evac(n)

            def row_stats(t0, t1):
                for t in range(t0, t1):
                    dve.bn_stats(st[:, t, :], X[:, t, :]).then_inc(ln1_st, 1)

            def row_means(part):
                tiles = LN1_PARTS[part]
                dve.wait_ge(ln1_st, tiles.stop)
                for t in range(tiles.start, tiles.stop):
                    m = dve.bn_aggr(mv[:, t, :], st[:, t, :])
                link(m)
                dve.tensor_scalar(nmr[:, tiles], mv[:, tiles, 1], LN_EPS, None, ALU.add).then_inc(ln1_mv, 1)

            for n in range(A0):
                group(n)
                if n in (4, 6):
                    k = n // 2 - 2
                    dve.wait_ge(ld_x[k], 16)
                    row_stats(TPB * k, TPB * (k + 1))
            row_means(0)
            for k in range(2, B):
                dve.wait_ge(ld_x[k], 16)

            for n in range(A0, GROUPS):
                group(n)
                k = 2 * TPB + n - VO0
                if 2 * TPB <= k < TILES:
                    row_stats(k, k + 1)
                if k == TILES:
                    row_means(1)
            dve.wait_ge(tanh_ready, 1)

            def xT_low(i, s):
                wait(dve, xT_ready, i + 1)
                dve.tensor_tensor(xnT16[s][:, 1].rearrange("p c n -> p (c n)"), xT_ps,
                                  xnT16[s][:, 0].rearrange("p c n -> p (c n)"), ALU.subtract).then_inc(xTl_ready, 1)

            xT_low(0, 0)

            def step(g, u):
                i = 2 * g + u
                v = 1 - u
                static = isinstance(i, int)

                def shift(h):
                    s = S_ps[h].rearrange("p (a k) -> p a k", k=NCTX)
                    m8 = mx[:, u, 8 * h:8 * h + 8]
                    wait(dve, s_mm, 2 * i + h + 1)
                    dve.tensor_reduce(m8, s, AX, ALU.max).then_inc(mx_ready, 1)
                    wait(dve, mx_ready, 2 * i + h + 1)
                    wait(dve, pT_mm, 2 * i - 4 + h + 1)
                    dve.tensor_tensor(E[:, u, BANK * h:BANK * (h + 1)].rearrange("p (a k) -> p a k", k=NCTX), s,
                                      m8.unsqueeze(2).to_broadcast([P, 8, NCTX]), ALU.subtract
                                      ).then_inc(shifted, 1)

                if not static or i < TILES:
                    shift(0)
                if not static or i < TILES:
                    shift(1)
                if not static or i + 1 < TILES:
                    xT_low(i + 1, v)
                if not static or i < TILES:
                    for h in range(2):
                        wait(dve, exp_ready, 2 * i + h + 1)
                        r8 = rsum[:, u, 8 * h:8 * h + 8]
                        dve.tensor_reduce(r8, E[:, u, BANK * h:BANK * (h + 1)].rearrange("p (a k) -> p a k", k=NCTX),
                                          AX, ALU.add).then_inc(sum_ready, 1)
                        wait(dve, sum_ready, 2 * i + h + 1)
                        wait(dve, p_ready, 2 * i - 4 + h + 1)
                        dve.reciprocal(rinv[:, u, 8 * h:8 * h + 8], r8).then_inc(rinv_ready, 1)
                if not static or 1 <= i <= TILES:
                    wait(dve, o_mm, i)
                    wait(dve, bo_added, i)
                    dve.scalar_tensor_tensor(at(X, i - 1), O_ps, tg[:, 0:1], at(X, i - 1), ALU.mult, ALU.add
                                             ).then_inc(x2_ready, 1)
                    wait(dve, x2_ready, i)
                    alone(dve, g, dve_waits)
                    dve.bn_stats(st2[:, v, :], at(X, i - 1)).then_inc(st2_ready, 1)
                    wait(dve, st2_ready, i)
                    wait(dve, rstd2_ready, i - 2)
                    alone(dve, g, dve_waits)
                    dve.bn_aggr(mv2[:, v, :], st2[:, v, :]).then_inc(mv2_ready, 1)

            attention_steps(dve, step)

            TE = [P, TILES, EXPERTS]
            L = G_ps.rearrange("p (t e) -> p t e", e=EXPERTS)
            oh1, oh2, tmp, tmp2 = RT[1], RT[2], RT[3], RT[4]
            m1, m2, c1, c2, den, sinv = [sm[:, n, :] for n in range(6)]
            r8 = rank8[:, :].unsqueeze(1).to_broadcast(TE)

            def per_token(a):
                return a.unsqueeze(2).to_broadcast(TE)

            def largest(p, m, c, oh):
                link(dve.tensor_reduce(m, p, AX, ALU.max))
                link(dve.tensor_tensor(tmp, p, per_token(m), ALU.is_equal))
                link(dve.tensor_tensor(tmp, tmp, r8, ALU.mult))
                link(dve.tensor_reduce(c, tmp, AX, ALU.max))
                link(dve.tensor_tensor(oh, r8, per_token(c), ALU.is_equal))

            dve.wait_ge(g_mm, TILES)
            dve.wait_ge(c_pool, 12)
            largest(L, m1, c1, oh1)
            link(dve.scalar_tensor_tensor(tmp2, oh1, -1e30, L, ALU.mult, ALU.add))
            largest(tmp2, m2, c2, oh2)
            link(dve.tensor_tensor(M_bf[:, :, :], oh1, oh2, ALU.add), M_ready)
            with nc.allow_low_precision(reason="whole numbers up to TILES are exact"):
                dve.tensor_reduce(Msum[:, :], M_bf[:, :, :].rearrange("p t e -> p e t"), AX, ALU.add
                                  ).then_inc(Msum_ready, 1)
            dve.tensor_tensor(share[:, :], m2, m1, ALU.subtract).then_inc(lg_ready, 1)
            dve.wait_ge(cnt_mm, 1)
            link(dve.tensor_scalar(cnti[:, 0, :], cnt_ps, float(P - 1), None, ALU.add))
            link(dve.tensor_scalar(cnti[:, 1, :], cnti[:, 0, :], 7, None, ALU.logical_shift_right))
            link(dve.tensor_copy(cum[:, 0, EXPERTS:], cnti[:, 1, :]))
            for n in range(3):
                link(dve.tensor_tensor(cum[:, n + 1, EXPERTS:], cum[:, n, EXPERTS:],
                                       cum[:, n, EXPERTS - 2 ** n:2 * EXPERTS - 2 ** n], ALU.add))
            first = cum[:, 3, EXPERTS - 1:2 * EXPERTS - 1]
            link(dve.tensor_scalar(base8[:, :], first, float(P), None, ALU.mult))
            dve.wait_ge(pexp_ready, 1)
            link(dve.tensor_scalar(den, share[:, :], 1.0, None, ALU.add))
            link(dve.reciprocal(sinv, den))
            dve.tensor_scalar(wtok[:, 0, :], sinv, ACC_SCALE, None, ALU.mult)
            link(dve.scalar_tensor_tensor(wtok[:, 1, :], share[:, :], ACC_SCALE, sinv, ALU.mult, ALU.mult))
            link(dve.tensor_copy(w16[:, 0], wtok[:, :, :]))
            link(dve.tensor_tensor(w16[:, 1], wtok[:, :, :], w16[:, 0], ALU.subtract))
            dve.wait_ge(rank_mm, 1)
            link(dve.tensor_tensor(tmp, rank_ps.rearrange("p (t e) -> p t e", e=EXPERTS),
                                   base8[:, :].unsqueeze(1).to_broadcast(TE), ALU.add))
            for k, oh in ((0, oh1), (1, oh2)):
                link(dve.tensor_tensor(tmp2, tmp, oh, ALU.mult))
                link(dve.tensor_reduce(pos[:, k, :], tmp2, AX, ALU.add))
            link(dve.tensor_copy(posi[:, 0, :], pos[:, :, :].rearrange("p k t -> p (k t)")))
            dve.tensor_scalar(posi[:, 1, :], posi[:, 0, :], P - 1, None, ALU.bitwise_and)
            link(dve.tensor_scalar(posi[:, 2, :], posi[:, 0, :], 7, None, ALU.logical_shift_right))
            link(dve.tensor_copy(lohi[:, :, :], posi[:, 1:3, :]))
            for s in range(2):
                dve.wait_ge(st_xn2[s], 16 * TILES // 2)
                dve.wait_ge(st_x2T[s], 16 * TILES // 2)
            TM = [P, TILES, MTILES]
            for k in (1, 0):
                n = slice(TILES * k, TILES * (k + 1))
                m = dve.tensor_tensor(eq_hi[:, n, :], iota_m[:, :].unsqueeze(1).to_broadcast(TM),
                                      lohi[:, 1, n].unsqueeze(2).to_broadcast(TM), ALU.is_equal
                                      ).then_inc(eq_ready, 1)
            dve.wait_ge(eq_ready, 2)
            for a, factor in enumerate((tokid[:, :], w16[:, 0, 0, :], w16[:, 1, 0, :])):
                dve.tensor_tensor(RH[:, 0:TILES, a, :], eq_hi[:, 0:TILES, :], factor.unsqueeze(2).to_broadcast(TM),
                                  ALU.mult)
            for n in range(0, PAIRS, 8):
                NM = [P, 8, P]
                dve.tensor_tensor(OH_lo[:, n:n + 8, :], iota_lo[:, :].unsqueeze(1).to_broadcast(NM),
                                  lohi[:, 0, n:n + 8].unsqueeze(2).to_broadcast(NM), ALU.is_equal
                                  ).then_inc(oh_ready, 1)
            dve.wait_ge(tab_mm, 1)
            link(dve.tensor_copy(tab[:, :, :].rearrange("p a m -> p (a m)"), tab_ps))
            link(dve.tensor_tensor(tab[:, 1, :], tab[:, 1, :], tab[:, 2, :], ALU.add))
            dve.tensor_scalar(gidx[:, :], tab[:, 0, :], -1.0, 0.0, ALU.add, ALU.max)
            link(dve.tensor_scalar(tab[:, 2, :], tab[:, 0, :], 0.0, None, ALU.is_equal))
            link(dve.scalar_tensor_tensor(tab[:, 2, :], tab[:, 2, :], pad_row[:, :], tab[:, 0, :], ALU.mult,
                                          ALU.add))
            dve.tensor_scalar(sidx[:, :], tab[:, 2, :], -1.0, None, ALU.add).then_inc(route_ready, 1)
            dve.wait_ge(route_ready, 1)

            def token_numbers(i, s, r):
                wait(dve, ga[s], 16 * r)
                dve.tensor_copy(gcol[s], col(gidx, i)).then_inc(gi_ready, 1)

            def rows_low(i):
                wait(dve, xsTh_ready, i + 1)
                dve.tensor_tensor(xsT16[:, 1].rearrange("p c n -> p (c n)"), PS[:, 5, 0:D],
                                  xsT16[:, 0].rearrange("p c n -> p (c n)"), ALU.subtract).then_inc(xsTl_ready, 1)

            token_numbers(0, 0, 0)
            token_numbers(1, 1, 0)
            ME = [1, MTILES, EXPERTS]
            link(dve.tensor_tensor(cmp[:, :, :], iota_m[0:1, :].unsqueeze(2).to_broadcast(ME),
                                   first[0:1, :].unsqueeze(1).to_broadcast(ME), ALU.is_ge))
            link(dve.tensor_reduce(etf[:, :], cmp[:, :, :], AX, ALU.add))
            dve.tensor_scalar(etile[:, :], etf[:, :], -1.0, None, ALU.add).then_inc(etile_ready, 1)
            dve.wait_ge(etile_ready, 1)
            rows_low(0)

            def mix(g, u):
                i = 2 * g + u
                static = isinstance(i, int)

                def hidden_low(h):
                    wait(dve, gh_ready, 2 * i + h + 1)
                    part = slice(4 * h, 4 * h + 4)
                    dve.scalar_tensor_tensor(g16[:, 1, part, :].rearrange("p j n -> p (j n)"),
                                             g32[:, part, :].rearrange("p j n -> p (j n)"), H_SCALE,
                                             g16[:, 0, part, :].rearrange("p j n -> p (j n)"), ALU.mult,
                                             ALU.subtract).then_inc(gl_ready, 1)

                if not static or i + 2 < MTILES:
                    token_numbers(i + 2, u, g + 1)
                if not static or i < MTILES:
                    for h in range(2):
                        wait(dve, h_mm, 2 * i + h + 1)
                        wait(dve, hT_mm, 2 * i - 2 + h + 1)
                        dve.tensor_copy(h32[:, BANK * h:BANK * (h + 1)], PS[:, h, :]).then_inc(h_ready, 1)
                if not static or i + 1 < MTILES:
                    rows_low(i + 1)
                if not static or i >= 1:
                    s = 1 - u
                    e = dve.value_load(col(etile, i - 1), min_val=0, max_val=EXPERTS - 1)
                    if static and i == 1:
                        dve.wait_ge(ld_b2, 16)
                    wait(dve, y_mm, i)
                    wait(dve, sc[s], 16 * (g - s))
                    dve.scalar_tensor_tensor(ys[:, s, :], PS[:, 4, 0:D], 1 / (W_SCALE * H_SCALE), at(b2_bc, e),
                                             ALU.mult, ALU.add).then_inc(y1_ready, 1)
                    dve.tensor_copy(scol[s], col(sidx, i - 1))
                    wait(dve, y1_ready, i)
                    dve.scalar_tensor_tensor(ys[:, s, :], PS[:, 4, D:2 * D], 1 / (W_SCALE * H_SCALE), ys[:, s, :],
                                             ALU.mult, ALU.add).then_inc(yb_ready, 1)
                    wait(dve, yb_ready, i)
                    dve.tensor_scalar(ys[:, s, :], ys[:, s, :], col(tab[:, 1, :], i - 1), None, ALU.mult
                                      ).then_inc(y_ready, 1)
                if not static or i < MTILES:
                    hidden_low(0)
                    hidden_low(1)

            mixture_steps(dve, mix)

            def own(k):
                return range(TPB * (k + 1) - LAST_BY_DVE[k], TPB * (k + 1))

            def statistics(k):
                tiles = slice(TPB * k, TPB * (k + 1))
                dve.wait_ge(ld_f[k], 16)
                for t in range(TPB * k, TPB * (k + 1)):
                    m = dve.bn_stats(st[:, t, :], F[:, t, :])
                link(m)
                for t in range(TPB * k, TPB * (k + 1)):
                    m = dve.bn_aggr(mv[:, t, :], st[:, t, :])
                link(m)
                dve.tensor_scalar(nmr[:, tiles], mv[:, tiles, 1], LN_EPS * ACC_SCALE ** 2, None, ALU.add
                                  ).then_inc(f_ve, 1)
                for t in own(k):
                    dve.scalar_tensor_tensor(F[:, t, :], F[:, t, :], mv[:, t, 0:1], tgam[:, :], ALU.subtract,
                                             ALU.mult).then_inc(f_cen, 1)

            def scales(k):
                tiles = slice(TPB * k, TPB * (k + 1))
                dve.wait_ge(f_pow, k + 1)
                dve.scalar_tensor_tensor(nmr[:, tiles], mv[:, tiles, 0], -1.0, rstd[:, tiles], ALU.mult, ALU.mult
                                         ).then_inc(f_rstd, 1)

            def finish(k):
                for t in own(k):
                    dve.wait_ge(f_cen, sum(LAST_BY_DVE[:k + 1]))
                    dve.wait_ge(x_beta, B)
                    dve.scalar_tensor_tensor(X[:, t, :], F[:, t, :], rstd[:, t:t + 1], X[:, t, :], ALU.mult,
                                             ALU.add).then_inc(f_last, 1)

            def gain(k):
                part = F[:, TPB * k:TPB * (k + 1) - LAST_BY_DVE[k], :]
                n = TPB - LAST_BY_DVE[k]
                dve.wait_ge(f_norm, k + 1)
                dve.tensor_tensor(part, part, tgam[:, :].unsqueeze(1).to_broadcast([P, n, D]), ALU.mult
                                  ).then_inc(f_gam, 1)

            statistics(0)
            for k in range(B):
                scales(k)
                if k + 1 < B:
                    statistics(k + 1)
                finish(k)
                gain(k)

        @block.tensor
        def _(pe):
            HIGH, LOW = 0, 1
            pe.wait_ge(c_ident, 1)

            def claim(n):
                if n >= 8 and (n % 2 == 0 or split_group(n - 8)):
                    pe.wait_ge(pre_dve, dve_count(n - 8))
                elif n >= 8:
                    pe.wait_ge(pre_act, act_count(n - 8))
                return PS[:, n % 8, :]

            pe.wait_ge(ld_ctx, 16)
            bank = claim(0)
            for c in range(DC):
                for t in range(DC):
                    m = pe.transpose(bank[:, D * c + P * t:D * c + P * (t + 1)], ctx_sb[:, t, P * c:P * (c + 1)],
                                     ident[:, :])
            m.then_inc(pre_mm, 1)

            def project(n, w, j):
                bank = claim(n)
                for jj in range(2):
                    for c in range(DC):
                        m = pe.matmul(bank[:, D * jj:D * (jj + 1)], w[:, c, P * (j + jj):P * (j + jj + 1)],
                                      cT[:, c, :], start=(c == 0), stop=(c == DC - 1))
                m.then_inc(pre_mm, 1)

            evacuated(pe, 0)
            for n in range(KT0, QT0):
                pe.wait_ge(ld_wk[2 * (n - KT0) // (JC // 2)], 16)
                project(n, Wk_sb, 2 * (n - KT0))
            pe.wait_ge(ld_wq, 16)
            for n in range(QT0, A0):
                bank = claim(n)
                j = 2 * (n - QT0)
                for jj in range(2):
                    for c in range(DC):
                        m = pe.transpose(bank[:, D * jj + P * c:D * jj + P * (c + 1)],
                                         Wq_sb[:, c, P * (j + jj):P * (j + jj + 1)], ident[:, :])
                m.then_inc(pre_mm, 1)
            for n in range(A0, VT0, 2):
                j = (n - A0) // 2
                if j % 2 == 0:
                    evacuated(pe, QT0 + j // 2)
                banks = [claim(n), claim(n + 1)]
                for c in range(DC):
                    for s in range(2):
                        rows = slice(DH * s, DH * (s + 1))
                        m = pe.matmul(banks[s][:, D * c:D * (c + 1)], WqT[rows, j, P * c:P * (c + 1)],
                                      KT[rows, j, :], start=True, stop=True)
                m.then_inc(pre_mm, 2)
            pe.wait_ge(ld_wv, 16)
            for n in range(VT0, VO0):
                project(n, Wv_sb, 2 * (n - VT0))
            pe.wait_ge(ld_wo, 16)

            def transpose_x(i, s):
                wait(pe, xn_ready, i + 1)
                wait(pe, xTl_ready, i)
                for c in range(DC):
                    m = pe.transpose(xT_ps[:, P * c:P * (c + 1)], xn_b[s][:, P * c:P * (c + 1)], ident[:, :])
                m.then_inc(xT_mm, 1)

            for n in range(VO0, GROUPS):
                if n == X_GROUP:
                    pe.wait_ge(pre_act, act_count(GROUPS - 8))
                    transpose_x(0, 0)
                bank = claim(n)
                b, j = divmod(2 * (n - VO0), JC)
                if b == 0:
                    evacuated(pe, VT0 + j // 2)
                for jj in range(2):
                    m = pe.matmul(bank[:, D * jj:D * (jj + 1)],
                                  VBD[:, j + jj, b].rearrange("p h k -> p (h k)"), Wo_sb[:, j + jj, :],
                                  start=True, stop=True)
                m.then_inc(pre_mm, 1)

            def shared(t):
                z = PS[:, t // 2 % 4, D * (t % 2):D * (t % 2 + 1)]
                if t in (0, 2):
                    pe.wait_ge(shifted, 2 * TILES)
                elif t in (4, 6):
                    pe.wait_ge(pT_ready, 2 * TILES)
                elif t % 2 == 0:
                    pe.wait_ge(z_gelu, t - 6)
                pe.matmul(z, ones_row[:, :], sb_row[:, :], start=True, stop=False)
                for c in range(DC):
                    m = pe.matmul(z, XN2T[:, t, P * c:P * (c + 1)], sW[:, c, :], start=False, stop=(c == DC - 1))
                m.then_inc(z_mm, 1)

            evacuated(pe, 8 * (GROUPS // 8) + 1)
            pe.wait_ge(ld_small, 16 * 6)

            def step(g, u):
                i = 2 * g + u
                v = 1 - u
                static = isinstance(i, int)

                def scores(h):
                    b = batch_of(g, u)
                    if h == 0:
                        wait(pe, xT_ready, i + 1)
                    wait(pe, shifted, 2 * i - 2 + h + 1)
                    for c in range(DC):
                        for w in (HIGH, LOW):
                            a = at(A16[:, :, c, w, BANK * h:BANK * (h + 1)], b)
                            pe.matmul(S_ps[h], xnT16[u][:, HIGH, c, :], a, start=(c == 0 and w == HIGH), stop=False)
                    wait(pe, xTl_ready, i + 1)
                    for c in range(DC):
                        a = at(A16[:, :, c, HIGH, BANK * h:BANK * (h + 1)], b)
                        m = pe.matmul(S_ps[h], xnT16[u][:, LOW, c, :], a, start=False, stop=(c == DC - 1))
                    m.then_inc(s_mm, 1)

                if not static or i < TILES:
                    scores(0)
                if static and i == 1:
                    evacuated(pe, GROUPS - 1)
                if static and i == TILES + 1:
                    for t in range(1, 5):
                        shared(t)
                if not static or 1 <= i <= TILES:
                    for h in range(2):
                        wait(pe, p_ready, 2 * i - 2 + h + 1)
                        wait(pe, pT_ready, 2 * i - 4 + h + 1)
                        for j in range(4):
                            c0 = BANK * h + P * j
                            m = pe.transpose(PT_ps[h][:, P * j:P * (j + 1)], E[:, v, c0:c0 + P], ident[:, :])
                        m.then_inc(pT_mm, 1)
                if not static or i < TILES:
                    scores(1)
                if not static or i + 1 < TILES:
                    transpose_x(i + 1, v)
                if static and i == TILES:
                    pe.wait_ge(c_pool, 6)
                    pe.wait_ge(ld_shared, 16 * 2)
                    for s in range(2):
                        pe.wait_ge(st_x2T[s], 16 * (TILES // 2 - 2))
                    shared(0)
                if not static or i >= 2:
                    wait(pe, xn2_ready, i - 1)
                    wait(pe, x2T_ready, i - 2)
                    for c in range(DC):
                        m = pe.transpose(x2T_ps[:, P * c:P * (c + 1)], xn2_b[u][:, P * c:P * (c + 1)], ident[:, :])
                    m.then_inc(x2T_mm, 1)
                if not static or 1 <= i <= TILES:
                    b = batch_of(g, u - 1)
                    wait(pe, x2_ready, i - 1)
                    for j in range(JC):
                        if j % 4 == 0:
                            wait(pe, pT_ready, 2 * i - 2 + j // 4 + 1)
                        m = pe.matmul(O_ps, PT[:, v, j, :], at(VO[:, :, j, :], b), start=(j == 0),
                                      stop=(j == JC - 1))
                    m.then_inc(o_mm, 1)
                if not static or i >= 2:
                    wait(pe, x2T_ready, i - 1)
                    k = i - 2
                    gate = (G_ps[:, EXPERTS * k:EXPERTS * (k + 1)] if static
                            else G_ps[:, bass.ds(k * EXPERTS, EXPERTS)])
                    for c in range(DC):
                        m = pe.matmul(gate, xn2T_b[u][:, c, :], gW[:, c, :], start=(c == 0), stop=(c == DC - 1))
                    m.then_inc(g_mm, 1)

            attention_steps(pe, step)

            for t in range(5, 7):
                shared(t)
            pe.wait_ge(M_ready, 1)
            Mf = M_bf[:, :, :].rearrange("p t e -> p (t e)")
            n = TILES * EXPERTS
            pe.matmul(rank_ps, upper[:, :], Mf, start=True, stop=False, skip_group_check=True)
            for t in range(1, TILES):
                if t == TILES // 4:
                    pe.wait_ge(Msum_ready, 1)
                    pe.matmul(cnt_ps, ones_b[:, :], Msum[:, :], start=True, stop=True).then_inc(cnt_mm, 1)
                m = pe.matmul(rank_ps[:, EXPERTS * t:], ones_b[:, :], Mf[:, 0:n - EXPERTS * t], start=False,
                              stop=(t == TILES - 1), skip_group_check=True)
            m.then_inc(rank_mm, 1)
            for s in range(2):
                pe.wait_ge(st_x2T[s], 16 * TILES // 2)
            for t in range(7, 13):
                shared(t)
            pe.wait_ge(ld_b1, 16)
            pe.transpose(PS[:, 5, 0:EXPERTS * HC], b1_rows[:, :], ident[0:EXPERTS * HC, 0:EXPERTS * HC]
                         ).then_inc(b1_mm, 1)
            for k in range(PAIRS):
                if k % 8 == 0:
                    pe.wait_ge(oh_ready, k // 8 + 1)
                if k == TILES:
                    pe.wait_ge(pool_oh, 3)
                m = pe.matmul(tab_ps, OH_lo[:, k, :], RH[:, k, :, :].rearrange("p a m -> p (a m)"), start=(k == 0),
                              stop=(k == PAIRS - 1))
            m.then_inc(tab_mm, 1)
            for t in range(13, 15):
                shared(t)
            pe.wait_ge(b1_ready, 1)
            pe.wait_ge(etile_ready, 1)
            pe.wait_ge(pool_lo, QUARTERS * EXPERTS)

            def transpose_rows(g, u):
                i = 2 * g + u
                wait(pe, ga[u], 16 * (g + 1))
                wait(pe, xsTl_ready, i)
                for c in range(DC):
                    m = pe.transpose(PS[:, 5, P * c:P * (c + 1)], xs[:, u, P * c:P * (c + 1)], ident[:, :])
                m.then_inc(xsT_mm, 1)

            transpose_rows(0, 0)
            for t in range(15, TILES):
                shared(t)
            pe.wait_ge(z_gelu, 3 * TPB)

            def mix(g, u):
                i = 2 * g + u
                static = isinstance(i, int)
                if not static or i < MTILES:
                    e = pe.value_load(col(etile, i), min_val=0, max_val=EXPERTS - 1)
                if static and i == 1:
                    pe.wait_ge(z_gelu, TILES)
                if not static or i >= 1:
                    for h in range(2):
                        wait(pe, h_ready, 2 * i - 2 + h + 1)
                        wait(pe, gelu_done, 2 * i - 4 + h + 1)
                        for j in range(4):
                            c0 = BANK * h + P * j
                            m = pe.transpose(PS[:, 2 + h, P * j:P * (j + 1)], h32[:, c0:c0 + P], ident[:, :])
                        m.then_inc(hT_mm, 1)
                if not static or i < MTILES:
                    wait(pe, xsTh_ready, i + 1)
                    wait(pe, xsTl_ready, i + 1)
                    for h in range(2):
                        wait(pe, h_ready, 2 * i - 2 + h + 1)
                        for n, (c, w) in enumerate([(c, w) for c in range(DC) for w in (HIGH, LOW)]):
                            wp = at(W16e[:, :, c, w, BANK * h:BANK * (h + 1)], e)
                            for a in ((HIGH, LOW) if w == HIGH else (HIGH,)):
                                m = pe.matmul(PS[:, h, :], xsT16[:, a, c, :], wp, start=(n == 0 and a == HIGH),
                                              stop=(n == 3))
                        m.then_inc(h_mm, 1)
                if not static or i + 1 < MTILES:
                    transpose_rows(g + (u + 1) // 2, 1 - u)
                if not static or i >= 1:
                    e = pe.value_load(col(etile, i - 1), min_val=0, max_val=EXPERTS - 1)
                    wait(pe, yb_ready, i - 1)
                    for j in range(HC):
                        if j % 4 == 0:
                            wait(pe, gh_ready, 2 * i - 2 + j // 4 + 1)
                        w = at4(W16e[:, :, DC + j // 4, :, D * (j % 4):D * (j % 4 + 1)], e)
                        pe.matmul(PS[:, 4, :].rearrange("p (a n) -> p a n", a=2), g16[:, HIGH, j, :], w,
                                  start=(j == 0), stop=False, skip_group_check=True)
                        if j % 4 == 0:
                            wait(pe, gl_ready, 2 * i - 2 + j // 4 + 1)
                        m = pe.matmul(PS[:, 4, 0:D], g16[:, LOW, j, :], w[:, 0, :], start=False,
                                      stop=(j == HC - 1), skip_group_check=True)
                    m.then_inc(y_mm, 1)

            mixture_steps(pe, mix)


INPUTS = ["x", "ctx_1024", "g_xattn", "g_ffn", "L0_xattn_Wq", "L0_xattn_Wk", "L0_xattn_Wv", "L0_xattn_Wo",
          "L0_xattn_bo", "L0_ffn_W1", "L0_ffn_b1", "L0_ffn_W2", "L0_ffn_b2", "L0_ffn_gate_W", "L0_ffn_shared_W",
          "L0_ffn_shared_b", "L0_ffn_gamma", "L0_ffn_beta"]


def kernel(**inputs):
    import concourse.bacc as bacc
    from concourse.bass_utils import run_bass_kernel_spmd

    nc = bacc.Bacc("TRN2", target_bir_lowering=False, num_devices=1)
    arrays, args = {}, []
    for name in INPUTS:
        a = np.ascontiguousarray(inputs[name])
        arrays[name] = a
        args.append(nc.dram_tensor(name, a.shape, mybir.dt.from_np(a.dtype), kind="ExternalInput").ap())
    out = nc.dram_tensor("out", (B, S, D), f32, kind="ExternalOutput").ap()
    xn2_dram = nc.dram_tensor("xn2_rows", (TOKENS, D), f32, kind="Internal").ap()
    acc_dram = nc.dram_tensor("acc_rows", (TOKENS + P, D), f32, kind="Internal").ap()
    build(nc, *args, out, xn2_dram, acc_dram)
    r = run_bass_kernel_spmd(nc, [arrays], core_ids=[0])
    return r.results[0]["out"]
```
